# Optimizing a Trainium2 kernel written in Bass

```python
import numpy as np
import jax
import jax.numpy as jnp

def _softmax(x, axis=-1):
    return jax.nn.softmax(x, axis=axis)

def _gelu(x):
    return jax.nn.gelu(x, approximate=True)

def _silu(x):
    return jax.nn.silu(x)

def _sigmoid(x):
    return jax.nn.sigmoid(x)

def _layernorm(x, axis=-1, eps=1e-05):
    m = jnp.mean(x, axis=axis, keepdims=True)
    v = jnp.var(x, axis=axis, keepdims=True)
    return (x - m) / jnp.sqrt(v + eps)

def _scatter_add(tgt, idx, src, axis=0):
    return tgt.at[idx].add(src)

def _segment_sum(src, seg, n):
    return jax.ops.segment_sum(src, seg, n)
kernel_name = 'mk_flamingo_gated_d1_seqx_r8_08b214'

def setup_inputs(seed: int=0):
    np.random.seed(seed)
    _w = jnp.asarray

    def _rec_inputs():
        import jax
        import jax.numpy as jnp
        _rk = jax.random.key(seed)
        x = -0.0002928 + 1 * jax.random.normal(jax.random.fold_in(_rk, 1), (1, 1024, 128), jnp.float32)
        _lenS = 1024 - jax.random.randint(jax.random.fold_in(_rk, 7), (1,), 0, max(1, 1024 // 4) + 1, jnp.int32)
        _lenS2 = 6404 - jax.random.randint(jax.random.fold_in(_rk, 8), (1,), 0, max(1, 6404 // 4) + 1, jnp.int32)
        _ctx_1024P = jax.random.normal(jax.random.fold_in(_rk, 11), (1, 16, 128), jnp.float32)
        _ctx_1024c = jax.random.dirichlet(jax.random.fold_in(_rk, 511), 0.3 * jnp.ones((16,), jnp.float32), (1, 6404))
        _ctx_1024t = jnp.einsum('bsk,bkd->bsd', _ctx_1024c, _ctx_1024P)
        _ctx_1024t = _ctx_1024t * jax.lax.rsqrt(jnp.mean(jnp.square(_ctx_1024t)) + 1e-12) * 0.953939
        ctx_1024 = -1.39393e-06 + 0.999914 * (_ctx_1024t + 0.3 * jax.random.normal(jax.random.fold_in(_rk, 611), (1, 6404, 128), jnp.float32))
        _validS = jnp.arange(1024)[None, :] < _lenS[:, None]
        _validS2 = jnp.arange(6404)[None, :] < _lenS2[:, None]
        _causal = jnp.tril(jnp.ones((1024, 1024), dtype=bool))
        mask_Bx1xS2_ik0 = jnp.where(jnp.broadcast_to(_validS2[:, None, :], (1, 1, 6404)), 0, 1).astype(jnp.int32)
        _g = jax.random.normal(jax.random.fold_in(_rk, 9001), (2, 1), jnp.float32)
        _g = jnp.sign(_g) * jnp.maximum(jnp.abs(_g), 1.0) + (_g == 0) * 1.0
        g_xattn = _g[0]
        g_ffn = _g[1]
        return (x, ctx_1024, mask_Bx1xS2_ik0, g_xattn, g_ffn)
    x, ctx_1024, mask_Bx1xS2_ik0, g_xattn, g_ffn = _rec_inputs()

    def _L0_xattn_setup():
        import jax, jax.numpy as jnp
        import numpy as np
        B, S, D, H = (2, 256, 128, 16)
        DK = D // H

        def _proj(x, W, b):
            y = jnp.einsum('bsd,ed->bse', x, W) + b
            return y.reshape(x.shape[0], -1, H, DK).transpose(0, 2, 1, 3)
        key = jax.random.key(seed)
        ks = jax.random.split(key, 12)
        inp = {'query': jax.random.normal(ks[0], (B, S, D), jnp.float32), 'key': jax.random.normal(ks[1], (B, S, D), jnp.float32), 'value': jax.random.normal(ks[2], (B, S, D), jnp.float32), 'mask': jax.random.randint(ks[3], (B, 1, S), 0, 2, jnp.int32)}
        sc = 1.0 / np.sqrt(D)
        inp['Wq'] = jax.random.normal(ks[4], (D, D), jnp.float32) * sc
        inp['bq'] = jnp.zeros((D,), jnp.float32)
        inp['Wk'] = jax.random.normal(ks[5], (D, D), jnp.float32) * sc
        inp['bk'] = jnp.zeros((D,), jnp.float32)
        inp['Wv'] = jax.random.normal(ks[6], (D, D), jnp.float32) * sc
        inp['bv'] = jnp.zeros((D,), jnp.float32)
        inp['Wo'] = jax.random.normal(ks[7], (D, D), jnp.float32) * sc
        inp['bo'] = jnp.zeros((D,), jnp.float32)
        return inp
    _L0_xattn_all = _L0_xattn_setup()
    _L0_xattn_in = {k: v for k, v in _L0_xattn_all.items() if k in ('Wq', 'bq', 'Wk', 'bk', 'Wv', 'bv', 'Wo', 'bo')}
    del _L0_xattn_all

    def _L0_ffn_setup():
        import math
        import jax
        import jax.numpy as jnp
        import numpy as np
        B, T, D = (1, 256, 128)
        H, KV, DH = (16, 4, 64)
        E, TOPK, DFF = (32, 4, 128)
        WINDOW = 128
        EPS = 1e-05
        ROPE_BASE = 150000.0
        ROPE_SCALE = 32.0

        def _rmsnorm(x, w):
            rms = jax.lax.rsqrt(jnp.mean(x * x, axis=-1, keepdims=True) + EPS)
            return w * (x * rms)

        def _apply_rope(x, sin, cos):
            x1, x2 = (x[..., ::2], x[..., 1::2])
            out = jnp.stack([x1 * cos - x2 * sin, x1 * sin + x2 * cos], axis=-1)
            return out.reshape(x.shape)
        key = jax.random.key(seed)
        ks = jax.random.split(key, 12)
        s = 0.02
        return {'x': jax.random.normal(ks[0], (B, T, D), jnp.float32), 'attn_norm_w': 1.0 + 0.02 * jax.random.normal(ks[1], (D,), jnp.float32), 'ffn_norm_w': 1.0 + 0.02 * jax.random.normal(ks[2], (D,), jnp.float32), 'qkv_w': s * jax.random.normal(ks[3], (D, H * DH + 2 * KV * DH), jnp.float32), 'qkv_b': s * jax.random.normal(ks[4], (H * DH + 2 * KV * DH,), jnp.float32), 'proj_w': s * jax.random.normal(ks[5], (H * DH, D), jnp.float32), 'proj_b': s * jax.random.normal(ks[6], (D,), jnp.float32), 'attn_sink': 0.5 * jax.random.normal(ks[7], (H,), jnp.float32), 'gate_w': s * jax.random.normal(ks[8], (D, E), jnp.float32), 'gate_b': s * jax.random.normal(ks[9], (E,), jnp.float32), 'W_up': s * jax.random.normal(ks[10], (E, D, 2 * DFF), jnp.float32), 'W_down': s * jax.random.normal(ks[11], (E, DFF, D), jnp.float32)}
    _L0_ffn_all = _L0_ffn_setup()
    _L0_ffn_in = {k: v for k, v in _L0_ffn_all.items() if k in ('attn_norm_w', 'ffn_norm_w', 'qkv_w', 'qkv_b', 'proj_w', 'proj_b', 'attn_sink', 'gate_w', 'gate_b', 'W_up', 'W_down')}
    del _L0_ffn_all
    return {'x': x, 'ctx_1024': ctx_1024, 'mask_Bx1xS2_ik0': mask_Bx1xS2_ik0, 'g_xattn': g_xattn, 'g_ffn': g_ffn, 'L0_xattn_Wq': _L0_xattn_in['Wq'], 'L0_xattn_bq': _L0_xattn_in['bq'], 'L0_xattn_Wk': _L0_xattn_in['Wk'], 'L0_xattn_bk': _L0_xattn_in['bk'], 'L0_xattn_Wv': _L0_xattn_in['Wv'], 'L0_xattn_bv': _L0_xattn_in['bv'], 'L0_xattn_Wo': _L0_xattn_in['Wo'], 'L0_xattn_bo': _L0_xattn_in['bo'], 'L0_ffn_attn_norm_w': _L0_ffn_in['attn_norm_w'], 'L0_ffn_ffn_norm_w': _L0_ffn_in['ffn_norm_w'], 'L0_ffn_qkv_w': _L0_ffn_in['qkv_w'], 'L0_ffn_qkv_b': _L0_ffn_in['qkv_b'], 'L0_ffn_proj_w': _L0_ffn_in['proj_w'], 'L0_ffn_proj_b': _L0_ffn_in['proj_b'], 'L0_ffn_attn_sink': _L0_ffn_in['attn_sink'], 'L0_ffn_gate_w': _L0_ffn_in['gate_w'], 'L0_ffn_gate_b': _L0_ffn_in['gate_b'], 'L0_ffn_W_up': _L0_ffn_in['W_up'], 'L0_ffn_W_down': _L0_ffn_in['W_down']}

def reference(x, ctx_1024, mask_Bx1xS2_ik0, g_xattn, g_ffn, L0_xattn_Wq, L0_xattn_bq, L0_xattn_Wk, L0_xattn_bk, L0_xattn_Wv, L0_xattn_bv, L0_xattn_Wo, L0_xattn_bo, L0_ffn_attn_norm_w, L0_ffn_ffn_norm_w, L0_ffn_qkv_w, L0_ffn_qkv_b, L0_ffn_proj_w, L0_ffn_proj_b, L0_ffn_attn_sink, L0_ffn_gate_w, L0_ffn_gate_b, L0_ffn_W_up, L0_ffn_W_down):
    import jax
    import jax.numpy as jnp

    def _L0_xattn_ref(query, key, value, mask, Wq, bq, Wk, bk, Wv, bv, Wo, bo):
        import jax, jax.numpy as jnp
        import numpy as np
        B, S, D, H = (2, 256, 128, 16)
        DK = D // H

        def _proj(x, W, b):
            y = jnp.einsum('bsd,ed->bse', x, W) + b
            return y.reshape(x.shape[0], -1, H, DK).transpose(0, 2, 1, 3)
        q = _proj(query, Wq, bq)
        k = _proj(key, Wk, bk)
        v = _proj(value, Wv, bv)
        scores = jnp.einsum('bhqd,bhkd->bhqk', q, k) / np.sqrt(DK)
        m = mask[:, None, :, :]
        scores = jnp.where(m == 0, jnp.float32(-1000000000.0), scores)
        p = jax.nn.softmax(scores, axis=-1)
        x = jnp.einsum('bhqk,bhkd->bhqd', p, v)
        x = x.transpose(0, 2, 1, 3).reshape(query.shape[0], -1, D)
        return jnp.einsum('bsd,ed->bse', x, Wo) + bo

    def _L0_ffn_ref(x, attn_norm_w, ffn_norm_w, qkv_w, qkv_b, proj_w, proj_b, attn_sink, gate_w, gate_b, W_up, W_down):
        import math
        import jax
        import jax.numpy as jnp
        import numpy as np
        B, T, D = (1, 256, 128)
        H, KV, DH = (16, 4, 64)
        E, TOPK, DFF = (32, 4, 128)
        WINDOW = 128
        EPS = 1e-05
        ROPE_BASE = 150000.0
        ROPE_SCALE = 32.0

        def _rmsnorm(x, w):
            rms = jax.lax.rsqrt(jnp.mean(x * x, axis=-1, keepdims=True) + EPS)
            return w * (x * rms)

        def _apply_rope(x, sin, cos):
            x1, x2 = (x[..., ::2], x[..., 1::2])
            out = jnp.stack([x1 * cos - x2 * sin, x1 * sin + x2 * cos], axis=-1)
            return out.reshape(x.shape)
        Bx, Tx, Dx = x.shape
        h = _rmsnorm(x, attn_norm_w)
        qkv = h @ qkv_w + qkv_b
        q = qkv[..., :H * DH].reshape(Bx, Tx, H, DH).transpose(0, 2, 1, 3)
        k = qkv[..., H * DH:H * DH + KV * DH].reshape(Bx, Tx, KV, DH).transpose(0, 2, 1, 3)
        v = qkv[..., H * DH + KV * DH:].reshape(Bx, Tx, KV, DH).transpose(0, 2, 1, 3)
        pos = jnp.arange(Tx, dtype=jnp.float32) / ROPE_SCALE
        inv_freq = 1.0 / ROPE_BASE ** (jnp.arange(0, DH, 2, dtype=jnp.float32) / DH)
        freqs = pos[:, None] * inv_freq[None, :]
        sin, cos = (jnp.sin(freqs), jnp.cos(freqs))
        q = _apply_rope(q, sin, cos)
        k = _apply_rope(k, sin, cos)
        rep = H // KV
        k = jnp.repeat(k, rep, axis=1)
        v = jnp.repeat(v, rep, axis=1)
        logits = jnp.einsum('bhqd,bhkd->bhqk', q, k) / math.sqrt(DH)
        i = jnp.arange(Tx)[:, None]
        j = jnp.arange(Tx)[None, :]
        mask = (j > i) | (i - j > WINDOW)
        logits = jnp.where(mask, -jnp.inf, logits)
        lse = jax.nn.logsumexp(logits, axis=-1, keepdims=True)
        denom_log = jnp.logaddexp(lse, attn_sink.reshape(1, H, 1, 1))
        attn = jnp.exp(logits - denom_log)
        y = jnp.einsum('bhqk,bhkd->bhqd', attn, v)
        y = y.transpose(0, 2, 1, 3).reshape(Bx, Tx, H * DH)
        x = x + (y @ proj_w + proj_b)
        h2 = _rmsnorm(x, ffn_norm_w).reshape(Bx * Tx, Dx)
        glogits = h2 @ gate_w + gate_b
        topv, topi = jax.lax.top_k(glogits, TOPK)
        gw = jax.nn.softmax(topv, axis=-1)
        N = Bx * Tx
        combine = jnp.zeros((N, E), x.dtype).at[jnp.arange(N)[:, None], topi].add(gw)

        def body(acc, we):
            wu, wd, ce = we
            ug = h2 @ wu
            u, g = (ug[:, :DFF], ug[:, DFF:])
            return (acc + ce[:, None] * (jax.nn.silu(g) * u @ wd), None)
        y2, _ = jax.lax.scan(body, jnp.zeros_like(h2), (W_up, W_down, combine.T))
        return x + y2.reshape(Bx, Tx, Dx)
    x = x + jnp.tanh(g_xattn[0]) * _L0_xattn_ref(_layernorm(x, axis=-1), ctx_1024, ctx_1024, mask_Bx1xS2_ik0, L0_xattn_Wq, L0_xattn_bq, L0_xattn_Wk, L0_xattn_bk, L0_xattn_Wv, L0_xattn_bv, L0_xattn_Wo, L0_xattn_bo)
    x = x + jnp.tanh(g_ffn[0]) * _L0_ffn_ref(_layernorm(x, axis=-1), L0_ffn_attn_norm_w, L0_ffn_ffn_norm_w, L0_ffn_qkv_w, L0_ffn_qkv_b, L0_ffn_proj_w, L0_ffn_proj_b, L0_ffn_attn_sink, L0_ffn_gate_w, L0_ffn_gate_b, L0_ffn_W_up, L0_ffn_W_down)
    return x

_drawn_inputs = setup_inputs


def setup_inputs(seed=0):
    import zlib

    import numpy as np

    out = dict(_drawn_inputs(seed))
    spreads = {'L0_xattn_bq': (0.0, 0.333),
     'L0_xattn_bk': (0.0, 0.8),
     'L0_xattn_bv': (0.0, 0.1),
     'L0_xattn_bo': (0.0, 0.1)}
    factors = {'L0_ffn_attn_norm_w': 8.0,
     'L0_ffn_ffn_norm_w': 8.0,
     'L0_ffn_attn_sink': 8.0,
     'L0_ffn_gate_w': 3.934,
     'L0_ffn_gate_b': 8.0,
     'L0_ffn_W_up': 3.683,
     'L0_ffn_W_down': 3.654}
    for name, (base, spread) in spreads.items():
        noise = np.random.default_rng([zlib.crc32(name.encode()), seed]).standard_normal(out[name].shape)
        drawn = base * np.exp(spread * noise) if base else spread * noise
        out[name] = jnp.asarray(drawn.astype(out[name].dtype))
    for name, factor in factors.items():
        out[name] = (out[name] * factor).astype(out[name].dtype)
    return out
```

```python
from contextlib import ExitStack

import numpy as np

import concourse.bass as bass
from concourse import mybir

F32 = mybir.dt.float32
BF16 = mybir.dt.bfloat16
I32 = mybir.dt.int32
U32 = mybir.dt.uint32
ALU = mybir.AluOpType
ACT = mybir.ActivationFunctionType
X = mybir.AxisListType.X

P = 128
S = 1024
D = 128
NT = S // P
SK = 6404
KC = 126
NC = -(-SK // KC)
NCE = NC + NC % 2
H = 16
DK = D // H
ROWS = 64
NP = H * ROWS // P
Q_PARTS = [0, 0, 1, 1, 0, 2]
K_PARTS = [0, 1, 0, 1, 2, 0]
EXT = ROWS - DK * len(Q_PARTS)
ROW_MASK = DK * len(Q_PARTS)
ROW_MAX = ROW_MASK + 3
QB = 256
NB = S // QB
QT = QB // P
NG = H // 4
HF = 16
KV = 4
DH = 64
NE = 32
FF = 128
TOPK = 4
WIN = 128
EPS = 1e-5
MASKED = 1e9
NEG = -1e30

C_ID, C_SUM, C_BAND, C_IOTA, C_TRI, C_ONES, C_START, C_EXTS, C_EXTT = 0, 128, 256, 512, 576, 640, 768, 769, 770
C_EIOTA, C_END = 771, 803


def head_of(g, j):
    return 2 * g + j % 2, j // 2


class Chain:

    def __init__(self, engine, sem):
        self.engine, self.sem, self.count = engine, sem, 0

    def __call__(self, instruction):
        self.count += 1
        instruction.then_inc(self.sem, 1)
        self.engine.wait_ge(self.sem, self.count)


def build(nc, a, out):
    with ExitStack() as root:
        sb_of, sem_of = {}, {}

        def sb(name, shape, dt=F32, ctx=root):
            return ctx.enter_context(nc.sbuf_tensor(name, shape, dt))

        def sem(name):
            return root.enter_context(nc.semaphore(name))

        ps = root.enter_context(nc.psum_tensor("ps", [P, 8, 512], F32))
        const = sb("const", [P, C_END])
        ident = const[:, C_ID:C_ID + P]
        x0 = sb("x0", [P, NT, D])
        x1 = sb("x1", [P, NT, D])
        wrk = sb("wrk", [P, NT, D])
        st = sb("st", [P, 8, NT])
        gates = sb("gates", [P, 2])
        tanhs = sb("tanhs", [P, 2])
        k_dram = nc.dram_tensor("k_scratch", [NCE + 1, P, NP, KC], BF16).ap()
        v_dram = nc.dram_tensor("v_scratch", [NCE + 1, KC, H * (DK + 1)], F32).ap()
        q_dram = nc.dram_tensor("q_scratch", [P, NP, S], BF16).ap()

        def normalise(chain_dve, act_wait, act_signal, dve_signal, src, dst, centre):
            dve = nc.vector
            total, mean, var, root_, rstd = (st[:, n, :] for n in range(5))
            cur = src
            if centre:
                chain_dve(dve.tensor_reduce(total, src[:, :, :], X, ALU.add))
                chain_dve(dve.tensor_scalar(mean, total, 1.0 / D, None, ALU.mult))
                chain_dve(dve.tensor_tensor(dst[:, :, :], src[:, :, :],
                                            mean.unsqueeze(2).broadcast_to([P, NT, D]), ALU.subtract))
                cur = dst
            chain_dve(dve.tensor_tensor(wrk[:, :, :], cur[:, :, :], cur[:, :, :], ALU.mult))
            chain_dve(dve.tensor_reduce(total, wrk[:, :, :], X, ALU.add))
            dve.tensor_scalar(var, total, 1.0 / D, EPS, ALU.mult, ALU.add).then_inc(dve_signal, 1)
            nc.vector.wait_ge(*act_wait)
            chain_dve(dve.reciprocal(rstd, root_))
            chain_dve(dve.tensor_tensor(dst[:, :, :], cur[:, :, :],
                                        rstd.unsqueeze(2).broadcast_to([P, NT, D]), ALU.mult))

        with ExitStack() as cross:
            q_all = sb("q_all", [P, NP, S], BF16, cross)
            chunk_list = sb("chunk_list", [1, NCE + 1], I32, cross)
            oacc = sb("oacc", [P, NB, NG, QB], F32, cross)
            wo = sb("wo", [P, D], F32, cross)
            bo = sb("bo", [P, D], F32, cross)

            with ExitStack() as ph:
                xn = sb("xn", [P, NT, D], F32, ph)
                xT = sb("xT", [P, S], F32, ph)
                qf = sb("qf", [P, S], F32, ph)
                qr = sb("qr", [P, S], F32, ph)
                qp = sb("qp", [P, 3, S], BF16, ph)
                qext = sb("qext", [EXT, S], BF16, ph)
                wq = sb("wq", [P, D], F32, ph)
                bq = sb("bq", [P, 1], F32, ph)
                mask_c = sb("mask_c", [NC, KC], I32, ph)
                mask_f = sb("mask_f", [NC, KC], F32, ph)
                fl = sb("fl", [NC, 4], F32, ph)
                onehot = sb("onehot", [NC, NC], F32, ph)
                consts_in, x_in, wq_in, mask_in, late_in = (sem(n) for n in
                                                             ("consts_in", "x_in", "wq_in", "mask_in", "late_in"))
                dve_own1, var_ready1, root_ready1, xn_ready, flag_ready, pos_ready = (
                    sem(n) for n in ("dve_own1", "var_ready1", "root_ready1", "xn_ready", "flag_ready", "pos_ready"))
                xt_in_psum, xt_ready, q_in_psum, q_parts_ready, q_written, q_loaded, listed = (
                    sem(n) for n in ("xt_in_psum", "xt_ready", "q_in_psum", "q_parts_ready", "q_written",
                                     "q_loaded", "listed"))
                block = ph.enter_context(nc.Block())

                @block.sync
                def _(sp):
                    sp.dma_start(x0[:, :, :], a["x"].rearrange("b (t p) d -> p (b t) d", p=P)).then_inc(x_in, 16)
                    sp.dma_start(mask_c[:, :], a["mask"].rearrange("(c k) -> c k", k=KC)).then_inc(mask_in, 16)
                    sp.dma_start(const[:, :], a["consts"]).then_inc(consts_in, 16)
                    sp.dma_start(wq[:, :], a["WqT"]).then_inc(wq_in, 16)
                    sp.dma_start(bq[:, :], a["bq"]).then_inc(wq_in, 16)
                    sp.dma_start(gates[:, 0:1], a["g_xattn"].partition_broadcast(P)).then_inc(late_in, 16)
                    sp.dma_start(gates[:, 1:2], a["g_ffn"].partition_broadcast(P)).then_inc(late_in, 16)
                    sp.dma_start(wo[:, :], a["WoT"]).then_inc(late_in, 16)
                    sp.dma_start(bo[:, :], a["bo"].partition_broadcast(P)).then_inc(late_in, 16)
                    sp.wait_ge(q_parts_ready, 1)
                    for half in range(2):
                        for n, part in enumerate(Q_PARTS):
                            r = ROWS * half + DK * n
                            sp.dma_start(q_dram[r:r + DK].rearrange("d p s -> (d p) s"),
                                         qp[64 * half:64 * half + 64, part, :]).then_inc(q_written, 16)
                        for p in range(NP):
                            r = ROWS * half + ROW_MASK
                            sp.dma_start(q_dram[r:r + EXT, p, :], qext[:, :]).then_inc(q_written, 16)
                    sp.wait_ge(q_written, 2 * (len(Q_PARTS) + NP) * 16)
                    sp.dma_start(q_all[:, :, :], q_dram).then_inc(q_loaded, 16)
                    sp.wait_ge(q_loaded, 16)
                    sp.wait_ge(late_in, 64)

                @block.vector
                def _(dve):
                    own = Chain(dve, dve_own1)
                    dve.wait_ge(x_in, 16)
                    normalise(own, (root_ready1, 1), None, var_ready1, x0, xn, True)
                    nc.vector.engine_nop().then_inc(xn_ready, 1)
                    dve.wait_ge(mask_in, 16)
                    dve.wait_ge(consts_in, 16)
                    own(nc.vector.tensor_scalar(mask_f[:, :], mask_c[:, :], 0.0, None, ALU.not_equal))
                    own(nc.vector.tensor_reduce(fl[:, 0:1], mask_f[:, :], X, ALU.max))
                    nc.vector.engine_nop().then_inc(flag_ready, 1)
                    dve.wait_ge(pos_ready, 1)
                    own(nc.vector.tensor_scalar(fl[:, 1:2], ps[0:NC, 0, 0:1], 0.0, None, ALU.is_equal))
                    own(nc.vector.tensor_tensor(fl[:, 2:3], fl[:, 0:1], fl[:, 1:2], ALU.max))
                    nc.vector.engine_nop().then_inc(flag_ready, 1)
                    dve.wait_ge(pos_ready, 2)
                    own(nc.vector.tensor_copy(fl[:, 3:4], ps[0:NC, 1, 0:1]))
                    own(nc.vector.tensor_scalar(onehot[:, :], const[0:NC, C_IOTA:C_IOTA + NC],
                                                fl[:, 3:4], fl[:, 2:3], ALU.is_equal, ALU.mult))
                    nc.vector.engine_nop().then_inc(flag_ready, 1)
                    dve.wait_ge(pos_ready, 3)
                    own(nc.vector.memset(chunk_list[:, :], 0))
                    own(nc.vector.tensor_copy(chunk_list[0:1, 0:NC], ps[0:1, 2, 0:NC]))
                    own(nc.vector.tensor_copy(chunk_list[0:1, NCE:NCE + 1], ps[0:1, 3, 0:1]))
                    for n in range(2):
                        dve.wait_ge(xt_in_psum, n + 1)
                        last = nc.vector.tensor_copy(xT[:, 512 * n:512 * n + 512], ps[:, 4 + n, :])
                        last.then_inc(xt_ready, 1)
                    for n in range(2):
                        dve.wait_ge(q_in_psum, n + 1)
                        own(nc.vector.tensor_scalar(qf[:, 512 * n:512 * n + 512], ps[:, 6 + n, :], bq[:, 0:1],
                                                    float(DK) ** -0.5, ALU.add, ALU.mult))
                    own(nc.vector.tensor_copy(qp[:, 0, :], qf[:, :]))
                    own(nc.vector.tensor_tensor(qr[:, :], qf[:, :], qp[:, 0, :], ALU.subtract))
                    own(nc.vector.tensor_copy(qp[:, 1, :], qr[:, :]))
                    own(nc.vector.tensor_tensor(qp[:, 2, :], qr[:, :], qp[:, 1, :], ALU.subtract))
                    own(nc.vector.memset(qext[:, :], 0.0))
                    own(nc.vector.memset(qext[0:3, :], 1.0))
                    nc.vector.engine_nop().then_inc(q_parts_ready, 1)

                @block.scalar
                def _(act):
                    act.wait_ge(var_ready1, 1)
                    nc.scalar.activation(st[:, 3, :], st[:, 2, :], ACT.Sqrt).then_inc(root_ready1, 1)
                    act.wait_ge(late_in, 64)
                    nc.scalar.activation(tanhs[:, :], gates[:, :], ACT.Tanh).then_inc(listed, 1)
                    act.wait_ge(listed, 1)

                @block.tensor
                def _(pe):
                    one = const[0:NC, C_ONES:C_ONES + NC]
                    pe.wait_ge(flag_ready, 1)
                    nc.tensor.matmul(ps[0:NC, 0, 0:1], one, fl[:, 0:1], start=True, stop=True).then_inc(pos_ready, 1)
                    pe.wait_ge(flag_ready, 2)
                    nc.tensor.matmul(ps[0:NC, 1, 0:1], const[0:NC, C_TRI:C_TRI + NC], fl[:, 2:3],
                                     start=True, stop=True).then_inc(pos_ready, 1)
                    pe.wait_ge(flag_ready, 3)
                    nc.tensor.matmul(ps[0:1, 2, 0:NC], const[0:NC, C_START:C_START + 1], onehot[:, :],
                                     start=True, stop=True)
                    nc.tensor.matmul(ps[0:1, 3, 0:1], fl[:, 2:3], const[0:NC, C_ONES:C_ONES + 1],
                                     start=True, stop=True).then_inc(pos_ready, 1)
                    pe.wait_ge(xn_ready, 1)
                    for t in range(NT):
                        last = nc.tensor.transpose(ps[:, 4 + t // 4, P * (t % 4):P * (t % 4) + P], xn[:, t, :], ident)
                        if t % 4 == 3:
                            last.then_inc(xt_in_psum, 1)
                    pe.wait_ge(wq_in, 32)
                    for n in range(2):
                        pe.wait_ge(xt_ready, n + 1)
                        nc.tensor.matmul(ps[:, 6 + n, :], wq[:, :], xT[:, 512 * n:512 * n + 512],
                                         start=True, stop=True).then_inc(q_in_psum, 1)

            with ExitStack() as ph:
                wk = sb("wk", [P, D], F32, ph)
                bk = sb("bk", [P, 1], F32, ph)
                wv = sb("wv", [P, D], F32, ph)
                bv = sb("bv", [P, D], F32, ph)
                ctx_in = sb("ctx_in", [P, 2, KC], F32, ph)
                mask_b = sb("mask_b", [P, 2, KC], I32, ph)
                valid = sb("valid", [KC, 2, 1], F32, ph)
                unmasked = sb("unmasked", [P, 2, KC], F32, ph)
                kf = sb("kf", [P, 2, KC], F32, ph)
                kr = sb("kr", [P, 2, KC], F32, ph)
                kp = sb("kp", [P, 2, 3, KC], BF16, ph)
                kext = sb("kext", [EXT, 2, KC], BF16, ph)
                vv = sb("vv", [KC, 2, H, DK + 1], F32, ph)
                w_in, sp_passed2, act_passed = sem("wkv_in"), sem("sp_passed2"), sem("act_passed")
                chunk_in = [sem(f"chunk_in{n}") for n in range(2)]
                mask_ready = [sem(f"mask_ready{n}") for n in range(2)]
                kv_in_psum = [sem(f"kv_in_psum{n}") for n in range(2)]
                k_biased = [sem(f"k_biased{n}") for n in range(2)]
                k_high = [sem(f"k_high{n}") for n in range(2)]
                k_rest = [sem(f"k_rest{n}") for n in range(2)]
                k_mid = [sem(f"k_mid{n}") for n in range(2)]
                parts_ready = [sem(f"parts_ready{n}") for n in range(2)]
                kv_written = [sem(f"kv_written{n}") for n in range(2)]
                block = ph.enter_context(nc.Block())
                WRITES = 2 * len(K_PARTS) + 2 + 1

                def chunks(eng, body):
                    n = eng.value_load(chunk_list[0:1, NCE:NCE + 1], min_val=1, max_val=NC)
                    with eng.Fori(0, NCE, 2) as i:
                        for s in range(2):
                            with eng.If(i + s < n):
                                body(i, s)
                    return n

                @block.sync
                def _(sp):
                    sp.dma_start(wk[:, :], a["WkT"]).then_inc(w_in, 16)
                    sp.dma_start(bk[:, :], a["bk"]).then_inc(w_in, 16)
                    sp.dma_start(wv[:, :], a["WvT"]).then_inc(w_in, 16)
                    sp.dma_start(bv[:, :], a["bv"].partition_broadcast(P)).then_inc(w_in, 16)

                    def body(i, s):
                        sp.wait_ge(parts_ready[s], i + 2)
                        sp.sem_inc(sp_passed2, 1)
                        off = sp.value_load(chunk_list[0:1, bass.ds(i + s, 1)], min_val=0, max_val=(NC - 1) * KC)
                        sp.dma_start(ctx_in[:, s, :], a["ctxT"][:, bass.ds(off, KC)]).then_inc(chunk_in[s], 16)
                        sp.dma_start(mask_b[:, s, :], a["mask"][bass.ds(off, KC)].partition_broadcast(P)
                                     ).then_inc(chunk_in[s], 16)
                        sp.dma_start(valid[:, s, :], a["valid"][bass.ds(off, KC), :]).then_inc(chunk_in[s], 16)

                    chunks(sp, body)

                @block.scalar
                def _(act):
                    def body(i, s):
                        act.wait_ge(parts_ready[s], i + 4)
                        for half in range(2):
                            for n, part in enumerate(K_PARTS):
                                r = ROWS * half + DK * n
                                act.dma_start(k_dram[bass.ds(i + s, 1), r:r + DK].rearrange("c d p k -> (c d p) k"),
                                               kp[64 * half:64 * half + 64, s, part, :]).then_inc(kv_written[s], 16)
                            r = ROWS * half + ROW_MASK
                            act.dma_start(k_dram[bass.ds(i + s, 1), r:r + EXT].rearrange("c d p k -> (c d) p k"),
                                           kext[:, s, :].unsqueeze(1).broadcast_to([EXT, NP, KC])
                                           ).then_inc(kv_written[s], 16)
                        act.dma_start(v_dram[bass.ds(i + s, 1)].rearrange("c k n -> (c k) n"),
                                       vv[:, s, :, :].rearrange("k h d -> k (h d)")).then_inc(kv_written[s], 16)

                    for s in range(2):
                        act.sem_inc(kv_written[s], 16)
                    n = chunks(act, body)
                    act.wait_ge(kv_written[0], (n + 1) // 2 * (WRITES * 16) + 16)
                    act.sem_inc(act_passed, 1)
                    act.wait_ge(kv_written[1], n // 2 * (WRITES * 16) + 16)
                    act.sem_inc(act_passed, 1)

                @block.tensor
                def _(pe):
                    pe.wait_ge(w_in, 64)

                    def body(i, s):
                        pe.wait_ge(chunk_in[s], i * 24 + 48)
                        pe.wait_ge(parts_ready[s], i + 2)
                        nc.tensor.matmul(ps[:, 2 * s, 0:KC], wk[:, :], ctx_in[:, s, :], start=True, stop=True)
                        nc.tensor.matmul(ps[0:KC, 2 * s + 1, 0:D], ctx_in[:, s, :], wv[:, :],
                                         start=True, stop=True).then_inc(kv_in_psum[s], 1)

                    chunks(pe, body)

                @block.vector
                def _(dve):
                    dve.wait_ge(w_in, 64)
                    for s in range(2):
                        dve.sem_inc(parts_ready[s], 2)

                    def body(i, s):
                        turn = i // 2
                        dve.wait_ge(chunk_in[s], i * 24 + 48)
                        nc.vector.tensor_scalar(unmasked[:, s, :], mask_b[:, s, :], 0.0, None, ALU.not_equal
                                                ).then_inc(mask_ready[s], 1)
                        dve.wait_ge(kv_in_psum[s], turn + 1)
                        dve.wait_ge(mask_ready[s], turn + 1)
                        nc.vector.scalar_tensor_tensor(kf[:, s, :], ps[:, 2 * s, 0:KC], bk[:, 0:1],
                                                       unmasked[:, s, :], ALU.add, ALU.mult).then_inc(k_biased[s], 1)
                        dve.wait_ge(kv_written[s], turn * (WRITES * 16) + 16)
                        nc.vector.tensor_scalar(kext[:, s, :], unmasked[0:EXT, s, :], const[0:EXT, C_EXTS:C_EXTS + 1],
                                                const[0:EXT, C_EXTT:C_EXTT + 1], ALU.mult, ALU.add)
                        dve.wait_ge(k_biased[s], turn + 1)
                        nc.vector.tensor_copy(kp[:, s, 0, :], kf[:, s, :]).then_inc(k_high[s], 1)
                        nc.vector.scalar_tensor_tensor(vv[:, s, :, 0:DK],
                                                       bv[0:KC, :].rearrange("k (h d) -> k h d", d=DK),
                                                       valid[:, s, :],
                                                       ps[0:KC, 2 * s + 1, 0:D].rearrange("k (h d) -> k h d", d=DK),
                                                       ALU.mult, ALU.add)
                        dve.wait_ge(k_high[s], turn + 1)
                        nc.vector.tensor_tensor(kr[:, s, :], kf[:, s, :], kp[:, s, 0, :], ALU.subtract
                                                ).then_inc(k_rest[s], 1)
                        nc.vector.tensor_copy(vv[:, s, :, DK:DK + 1],
                                              valid[:, s, :].unsqueeze(1).broadcast_to([KC, H, 1])
                                              ).then_inc(parts_ready[s], 1)
                        dve.wait_ge(k_rest[s], turn + 1)
                        nc.vector.tensor_copy(kp[:, s, 1, :], kr[:, s, :]).then_inc(k_mid[s], 1)
                        dve.wait_ge(k_mid[s], turn + 1)
                        nc.vector.tensor_tensor(kp[:, s, 2, :], kr[:, s, :], kp[:, s, 1, :], ALU.subtract
                                                ).then_inc(parts_ready[s], 1)

                    chunks(dve, body)

            with ExitStack() as ph:
                k_slot = sb("k_slot", [P, 2, NP, KC], BF16, ph)
                v_slot = sb("v_slot", [KC, 2, H, DK + 1], F32, ph)
                probs = sb("probs", [KC, 2, 4, QB], F32, ph)
                zeros = sb("zeros", [P, 512], BF16, ph)
                mx = sb("mx", [P, 2, H, QT], F32, ph)
                run_max = sb("run_max", [P, QT, H], F32, ph)
                neg_f = sb("neg_f", [H, QB], F32, ph)
                neg_r = sb("neg_r", [H, QB], F32, ph)
                neg_p = sb("neg_p", [H, 3, QB], BF16, ph)
                dve_own3, zeros_ready = sem("dve_own3"), sem("zeros_ready")
                max_t, max_rows_ready, max_rows_in = sem("max_t"), sem("max_rows_ready"), sem("max_rows_in")
                oacc_saved, init_ready = sem("oacc_saved"), sem("init_ready")
                sp_passed = sem("sp_passed")
                stage_sems = []
                for s in range(NB + 1):
                    names = ["kv_in0", "kv_in1", "kv_free0", "kv_free1", "s1_ready", "s1_free", "mx_ready",
                             "s2_ready", "s2_free", "p_free", "pv_end"]
                    stage_sems.append({n: nc.alloc_semaphore(name=f"{n}_st{s}") for n in names})
                S1, S2, AC = 0, 2, 6
                block = ph.enter_context(nc.Block())

                @block.sync
                def _(sp):
                    n = sp.value_load(chunk_list[0:1, NCE:NCE + 1], min_val=1, max_val=NC)
                    for stage in range(NB + 1):
                        z = stage_sems[stage]
                        if stage:
                            zp = stage_sems[stage - 1]
                            sp.wait_ge(zp["kv_free0"], (n + 1) // 2 + 1)
                            sp.sem_inc(sp_passed, 1)
                            sp.wait_ge(zp["kv_free1"], n // 2 + 1)
                            sp.sem_inc(sp_passed, 1)
                        for s in range(2):
                            sp.sem_inc(z[f"kv_free{s}"], 1)
                        with sp.Fori(0, NCE, 2) as i:
                            for s in range(2):
                                with sp.If(i + s < n):
                                    sp.wait_ge(z[f"kv_free{s}"], i // 2 + 1)
                                    sp.sem_inc(sp_passed, 1)
                                    sp.dma_start(k_slot[:, s, :, :],
                                                 k_dram[bass.ds(i + s, 1)].rearrange("c r p k -> (c r) p k")
                                                 ).then_inc(z[f"kv_in{s}"], 16)
                                    sp.dma_start(v_slot[:, s, :, :].rearrange("k h d -> k (h d)"),
                                                 v_dram[bass.ds(i + s, 1)].rearrange("c k n -> (c k) n")
                                                 ).then_inc(z[f"kv_in{s}"], 16)
                        if stage < NB:
                            sp.wait_ge(max_rows_ready, stage + 1)
                            for half in range(2):
                                for j in range(3):
                                    r = ROWS * half + ROW_MAX + j
                                    sp.dma_start(q_all[r:r + 1, :, QB * stage:QB * stage + QB],
                                                 neg_p[NP * half:NP * half + NP, j, :]).then_inc(max_rows_in, 16)
                    sp.wait_ge(max_rows_in, NB * 96)

                @block.tensor
                def _(pe):
                    n = pe.value_load(chunk_list[0:1, NCE:NCE + 1], min_val=1, max_val=NC)
                    pe.wait_ge(zeros_ready, 1)
                    for stage in range(NB + 1):
                        z = stage_sems[stage]
                        one, two = stage < NB, stage > 0
                        q1, q2 = QB * stage, QB * (stage - 1)
                        if two:
                            if stage > 1:
                                pe.wait_ge(oacc_saved, stage - 1)
                            for b in range(2):
                                nc.tensor.matmul(ps[:, AC + b, :], zeros[:, 0:P], zeros[:, :], start=True, stop=True)
                            pe.wait_ge(max_rows_in, 96 * stage)

                        def scores_one(i, s, g):
                            for half in range(2):
                                pe.wait_ge(z["s1_free"], 8 * (i + s) + 2 * g + half + 1)
                            for u in range(2):
                                for qt in range(QT):
                                    for half in range(2):
                                        r = slice(ROWS * half, ROWS * half + ROWS)
                                        q, pair = q1 + P * qt, 2 * g + u
                                        last = nc.tensor.matmul(
                                            ps[:, S1 + half, KC * (2 * u + qt):KC * (2 * u + qt) + KC],
                                            q_all[r, pair, q:q + P], k_slot[r, s, pair, :], start=True, stop=True)
                                        if u == 1 and qt == QT - 1:
                                            last.then_inc(z["s1_ready"], 1)

                        def scores_two(i, s, g):
                            pe.wait_ge(z["s2_free"], 4 * (i + s) + g + 1)
                            for j in (0, 2, 1, 3):
                                pair, half = head_of(g, j)
                                r = slice(ROWS * half, ROWS * half + ROWS)
                                last = nc.tensor.matmul(
                                    ps[0:KC, S2 + 2 * (g % 2) + j // 2, QB * (j % 2):QB * (j % 2) + QB],
                                    k_slot[r, s, pair, :], q_all[r, pair, q2:q2 + QB], start=True, stop=True)
                            last.then_inc(z["s2_ready"], 1)

                        def values(i, s, g):
                            pe.wait_ge(z["s2_free"], 4 * (i + s) + g + 3)
                            for j in range(4):
                                pair, half = head_of(g, j)
                                head, c = NP * half + pair, 32 * (2 * (pair % 2) + half)
                                last = nc.tensor.matmul(
                                    ps[c:c + DK + 1, AC + g // 2, QB * (g % 2):QB * (g % 2) + QB],
                                    v_slot[:, s, head, :], probs[:, g % 2, j, :], start=False, stop=True,
                                    skip_group_check=True, tile_position=(0, c))
                            last.then_inc(z["p_free"], 1)

                        with pe.Fori(0, NCE, 2) as i:
                            for s in range(2):
                                with pe.If(i + s < n):
                                    pe.wait_ge(z[f"kv_in{s}"], 16 * i + 32)
                                    for g in range(NG):
                                        if two:
                                            scores_two(i, s, g)
                                        if one and g < 3:
                                            scores_one(i, s, g)
                                        if two and g > 0:
                                            values(i, s, g - 1)
                                    if one:
                                        scores_one(i, s, 3)
                                    if two:
                                        values(i, s, 3)
                                    nc.tensor.drain().then_inc(z[f"kv_free{s}"], 1)
                        if two:
                            nc.tensor.drain().then_inc(z["pv_end"], 1)
                        if one:
                            pe.wait_ge(z["mx_ready"], n + 1)
                            for qt in range(QT):
                                last = nc.tensor.transpose(ps[0:H, S1, P * qt:P * qt + P], run_max[:, qt, :], ident)
                            last.then_inc(max_t, 1)

                @block.scalar
                def _(act):
                    n = act.value_load(chunk_list[0:1, NCE:NCE + 1], min_val=1, max_val=NC)
                    for stage in range(1, NB + 1):
                        z = stage_sems[stage]
                        act.sem_inc(z["s2_free"], 2)
                        act.sem_inc(z["p_free"], 2)
                        with act.Fori(0, NCE, 2) as i:
                            for s in range(2):
                                with act.If(i + s < n):
                                    for g in range(NG):
                                        k = 4 * (i + s) + g
                                        act.wait_ge(z["s2_ready"], k + 1)
                                        act.wait_ge(z["p_free"], k + 1)
                                        b = S2 + 2 * (g % 2)
                                        nc.scalar.activation(
                                            probs[:, g % 2, :, :].rearrange("k h q -> k (h q)"),
                                            ps[0:KC, b:b + 2, :].rearrange("k b q -> k (b q)"), ACT.Exp
                                        ).then_inc(z["s2_free"], 1)
                        act.wait_ge(z["pv_end"], 1)
                        for b in range(2):
                            last = nc.scalar.copy(oacc[:, stage - 1, 2 * b:2 * b + 2, :].rearrange("p g q -> p (g q)"),
                                                  ps[:, AC + b, :])
                        nc.scalar.drain().then_inc(oacc_saved, 1)

                @block.vector
                def _(dve):
                    own = Chain(dve, dve_own3)
                    n = dve.value_load(chunk_list[0:1, NCE:NCE + 1], min_val=1, max_val=NC)
                    nc.vector.memset(zeros[:, :], 0.0).then_inc(zeros_ready, 1)
                    for stage in range(NB):
                        z = stage_sems[stage]
                        dve.sem_inc(z["s1_free"], 2)
                        dve.sem_inc(z["mx_ready"], 1)
                        own(nc.vector.memset(run_max[:, :, :], -3.0e38))
                        with dve.Fori(0, NCE, 2) as i:
                            for s in range(2):
                                with dve.If(i + s < n):
                                    for b in range(8):
                                        k = 8 * (i + s) + b
                                        dve.wait_ge(z["s1_ready"], k + 1)
                                        head = NP * (b % 2) + b // 2 * 2
                                        dst = mx[:, s, head:head + 2, :]
                                        nc.vector.tensor_reduce(
                                            dst, ps[:, S1 + b % 2, 0:4 * KC].rearrange("p (h t k) -> p h t k", h=2, t=QT),
                                            X, ALU.max).then_inc(z["s1_free"], 1)
                                    dve.wait_ge(z["s1_free"], 8 * (i + s) + 10)
                                    dve.wait_ge(z["mx_ready"], i + s + 1)
                                    nc.vector.tensor_tensor(run_max[:, :, :], run_max[:, :, :],
                                                            mx[:, s, :, :].rearrange("p h t -> p t h"), ALU.max
                                                            ).then_inc(z["mx_ready"], 1)
                        dve.wait_ge(max_t, stage + 1)
                        if stage:
                            dve.wait_ge(max_rows_in, 96 * stage)
                        own(nc.vector.tensor_scalar(neg_f[:, :], ps[0:H, S1, 0:QB], -1.0, None, ALU.mult))
                        own(nc.vector.tensor_copy(neg_p[:, 0, :], neg_f[:, :]))
                        own(nc.vector.tensor_tensor(neg_r[:, :], neg_f[:, :], neg_p[:, 0, :], ALU.subtract))
                        own(nc.vector.tensor_copy(neg_p[:, 1, :], neg_r[:, :]))
                        nc.vector.tensor_tensor(neg_p[:, 2, :], neg_r[:, :], neg_p[:, 1, :], ALU.subtract
                                                ).then_inc(max_rows_ready, 1)

            nc.clear_and_free_semaphores([z for stage in stage_sems for z in stage.values()])
            nc.all_engine_barrier()

            with ExitStack() as ph:
                attn = sb("attn", [P, NT, D], F32, ph)
                attn_t = sb("attn_t", [P, S], F32, ph)
                recip = sb("recip", [P, 2, 2, NP], F32, ph)
                biased = sb("biased", [P, NT, D], F32, ph)
                heads_t, heads_free, attn_ready, at_in_psum, at_ready, y_in_psum, rec_ready = (
                    sem(n) for n in ("heads_t", "heads_free", "attn_ready", "at_in_psum", "at_ready",
                                     "y_in_psum", "rec_ready"))
                dve_own4 = sem("dve_own4")
                block = ph.enter_context(nc.Block())

                @block.tensor
                def _(pe):
                    for t in range(NT):
                        if t >= 2:
                            pe.wait_ge(heads_free, t - 1)
                        for g in range(NG):
                            last = nc.tensor.transpose(ps[:, t % 2, P * g:P * g + P],
                                                       oacc[:, t // QT, g, P * (t % QT):P * (t % QT) + P], ident)
                        last.then_inc(heads_t, 1)
                        if t:
                            pe.wait_ge(heads_free, t)
                            nc.tensor.transpose(ps[:, 2 + (t - 1) // 4, P * ((t - 1) % 4):P * ((t - 1) % 4) + P],
                                                attn[:, t - 1, :], ident).then_inc(at_in_psum, 1)
                    pe.wait_ge(heads_free, NT)
                    nc.tensor.transpose(ps[:, 3, 3 * P:4 * P], attn[:, NT - 1, :], ident).then_inc(at_in_psum, 1)
                    for n in range(2):
                        pe.wait_ge(at_ready, n + 1)
                        for t in range(4):
                            last = nc.tensor.matmul(ps[:, 4 + n, P * t:P * t + P],
                                                    attn_t[:, P * (4 * n + t):P * (4 * n + t) + P], wo[:, :],
                                                    start=True, stop=True)
                        last.then_inc(y_in_psum, 1)

                @block.vector
                def _(dve):
                    own = Chain(dve, dve_own4)
                    for t in range(NT):
                        dve.wait_ge(heads_t, t + 1)
                        v = ps[:, t % 2, :].rearrange("p (q h c) -> p h q c", h=2, c=32)
                        nc.vector.reciprocal(recip[:, t % 2, :, :], v[:, :, :, DK]).then_inc(rec_ready, 1)
                        dve.wait_ge(rec_ready, t + 1)
                        nc.vector.tensor_tensor(attn[:, t, :].rearrange("p (h q d) -> p h q d", h=2, d=DK),
                                                v[:, :, :, 0:DK],
                                                recip[:, t % 2, :, :].unsqueeze(3).broadcast_to([P, 2, NP, DK]),
                                                ALU.mult).then_inc(heads_free, 1)
                    for n in range(2):
                        dve.wait_ge(at_in_psum, 4 * n + 4)
                        nc.vector.tensor_copy(attn_t[:, 512 * n:512 * n + 512], ps[:, 2 + n, :]).then_inc(at_ready, 1)
                    for n in range(2):
                        r = slice(4 * n, 4 * n + 4)
                        dve.wait_ge(y_in_psum, n + 1)
                        own(nc.vector.tensor_tensor(biased[:, r, :], ps[:, 4 + n, :].rearrange("p (t d) -> p t d", d=D),
                                                    bo[:, :].unsqueeze(1).broadcast_to([P, 4, D]), ALU.add))
                        own(nc.vector.scalar_tensor_tensor(
                            x1[:, r, :].rearrange("p t d -> p (t d)"), biased[:, r, :].rearrange("p t d -> p (t d)"),
                            tanhs[:, 0:1], x0[:, r, :].rearrange("p t d -> p (t d)"), ALU.mult, ALU.add))

        x2 = sb("x2", [P, NT, D])
        hT = sb("hT", [P, S])
        x3 = sb("x3", [P, NT, D])
        comb = sb("comb", [P, NT, NE])
        with ExitStack() as win:
            y_sb = sb("y_sb", [P, NT, HF * DH], F32, win)
            with ExitStack() as att:
                q_rot = sb("q_rot", [P, HF, S], F32, att)
                k_rot = sb("k_rot", [P, KV, S], F32, att)
                v_tok = sb("v_tok", [P, NT, KV * DH], F32, att)

                with ExitStack() as ph:
                    h = sb("h", [P, NT, D], F32, ph)
                    norm_w = sb("norm_w", [P, D], F32, ph)
                    wqk = sb("wqk", [P, HF + KV, P], F32, ph)
                    bqk = sb("bqk", [P, HF + KV], F32, ph)
                    wvv = sb("wvv", [P, KV * DH], F32, ph)
                    bvv = sb("bvv", [P, KV * DH], F32, ph)
                    cs = sb("cs", [P, S], F32, ph)
                    k_cs = sb("k_cs", [P, KV, S], F32, ph)
                    in5, cs_in, dve_own5, var5, root5, h_ready, ht_psum, ht_ready = (
                        sem(n) for n in ("in5", "cs_in", "dve_own5", "var5", "root5", "h_ready", "ht_psum", "ht_ready"))
                    v_psum, v_free, qk_psum, qk_free, ks_psum, ks_free = (
                        sem(n) for n in ("v_psum", "v_free", "qk_psum", "qk_free", "ks_psum", "ks_free"))
                    block = ph.enter_context(nc.Block())

                    @block.sync
                    def _(sp):
                        sp.dma_start(norm_w[:, :], a["attn_norm_w"].partition_broadcast(P)).then_inc(in5, 16)
                        sp.dma_start(wqk[:, :, :], a["wqk"]).then_inc(cs_in, 16)
                        sp.dma_start(bqk[:, :], a["bqk"]).then_inc(cs_in, 16)
                        sp.dma_start(wvv[:, :], a["wvv"]).then_inc(cs_in, 16)
                        sp.dma_start(bvv[:, :], a["bvv"].partition_broadcast(P)).then_inc(cs_in, 16)
                        sp.dma_start(cs[:, :], a["cs"]).then_inc(cs_in, 16)

                    @block.scalar
                    def _(act):
                        for n in range(2):
                            act.wait_ge(var5, n + 1)
                            nc.scalar.activation(st[:, 3, :], st[:, 2, :], ACT.Sqrt).then_inc(root5, 1)
                        for n in range(2):
                            act.wait_ge(ht_psum, n + 1)
                            nc.scalar.copy(hT[:, 512 * n:512 * n + 512], ps[:, n, :]).then_inc(ht_ready, 1)
                        for kv in range(KV):
                            for n in range(2):
                                act.wait_ge(ks_psum, 2 * kv + n + 1)
                                nc.scalar.copy(k_rot[:, kv, 512 * n:512 * n + 512], ps[:, n, :]).then_inc(ks_free, 1)

                    @block.vector
                    def _(dve):
                        own = Chain(dve, dve_own5)
                        normalise(own, (root5, 1), None, var5, x1, x2, True)
                        normalise(own, (root5, 2), None, var5, x2, h, False)
                        dve.wait_ge(in5, 16)
                        nc.vector.tensor_tensor(h[:, :, :], h[:, :, :],
                                                norm_w[:, :].unsqueeze(1).broadcast_to([P, NT, D]), ALU.mult
                                                ).then_inc(h_ready, 1)
                        dve.wait_ge(cs_in, 80)
                        for m in range(NT // 2):
                            dve.wait_ge(v_psum, m + 1)
                            nc.vector.tensor_tensor(v_tok[:, 2 * m:2 * m + 2, :],
                                                    ps[:, 2 + m % 2, :].rearrange("p (t d) -> p t d", t=2),
                                                    bvv[:, :].unsqueeze(1).broadcast_to([P, 2, KV * DH]), ALU.add
                                                    ).then_inc(v_free, 1)
                        for m in range(HF + KV):
                            f = HF + m if m < KV else m - KV
                            dst = k_cs[:, m, :] if m < KV else q_rot[:, f, :]
                            for n in range(2):
                                u = 2 * m + n
                                dve.wait_ge(qk_psum, u + 1)
                                nc.vector.scalar_tensor_tensor(dst[:, 512 * n:512 * n + 512], ps[:, 4 + u % 4, :],
                                                               bqk[:, f:f + 1], cs[:, 512 * n:512 * n + 512],
                                                               ALU.add, ALU.mult).then_inc(qk_free, 1)

                    @block.tensor
                    def _(pe):
                        pe.wait_ge(h_ready, 1)
                        for t in range(NT):
                            last = nc.tensor.transpose(ps[:, t // 4, P * (t % 4):P * (t % 4) + P], h[:, t, :], ident)
                            if t % 4 == 3:
                                last.then_inc(ht_psum, 1)
                        pe.wait_ge(cs_in, 80)
                        pe.wait_ge(ht_ready, 2)
                        for m in range(NT // 2):
                            if m >= 2:
                                pe.wait_ge(v_free, m - 1)
                            for t in (2 * m, 2 * m + 1):
                                last = nc.tensor.matmul(ps[:, 2 + m % 2, 256 * (t % 2):256 * (t % 2) + 256],
                                                        hT[:, P * t:P * t + P], wvv[:, :], start=True, stop=True)
                            last.then_inc(v_psum, 1)
                        for m in range(HF + KV):
                            f = HF + m if m < KV else m - KV
                            for n in range(2):
                                u = 2 * m + n
                                if u >= 4:
                                    pe.wait_ge(qk_free, u - 3)
                                nc.tensor.matmul(ps[:, 4 + u % 4, :], wqk[:, f, :], hT[:, 512 * n:512 * n + 512],
                                                 start=True, stop=True).then_inc(qk_psum, 1)
                            if 2 <= m < 2 + KV:
                                for n in range(2):
                                    u = 2 * (m - 2) + n
                                    pe.wait_ge(qk_free, u + 1)
                                    if u >= 2:
                                        pe.wait_ge(ks_free, u - 1)
                                    nc.tensor.matmul(ps[:, n, :], const[:, C_SUM:C_SUM + P],
                                                     k_cs[:, m - 2, 512 * n:512 * n + 512], start=True, stop=True
                                                     ).then_inc(ks_psum, 1)

                with ExitStack() as ph:
                    band = sb("band", [P, 2, 2, 2, P], BF16, ph)
                    identb = sb("identb", [P, P], BF16, ph)
                    sinks = sb("sinks", [P, HF], F32, ph)
                    neg_sinks = sb("neg_sinks", [P, HF], F32, ph)
                    neg4 = sb("neg4", [P, 4], F32, ph)
                    neg_m = sb("neg_m", [P, NT, HF], F32, ph)
                    sums = sb("sums", [P, NT, HF], F32, ph)
                    sink_w = sb("sink_w", [P, 2, HF], F32, ph)
                    pw = sb("pw", [P, 2, 4, 2 * P], F32, ph)
                    pt = sb("pt", [P, 2, 4, 2, P], F32, ph)
                    sink_in, band_ready, dve_own6, s_ready, m_ready, p_ready, t_ready, pt_ready, y_ready, y_free = (
                        sem(n) for n in ("sink_in", "band_ready", "dve_own6", "s_ready", "m_ready", "p_ready",
                                         "t_ready", "pt_ready", "y_ready", "y_free"))
                    red, sink_arg, sink_exp = sem("red"), sem("sink_arg"), sem("sink_exp")
                    block = ph.enter_context(nc.Block())
                    UNITS = NT * KV

                    @block.sync
                    def _(sp):
                        sp.dma_start(sinks[:, :], a["sink"].partition_broadcast(P)).then_inc(sink_in, 16)

                    @block.tensor
                    def _(pe):
                        pe.wait_ge(band_ready, 1)
                        for m in range(UNITS + 2):
                            if m < UNITS:
                                t, g = divmod(m, KV)
                                if m >= 2:
                                    pe.wait_ge(p_ready, m - 1)
                                for b in range(2):
                                    bank = ps[:, 2 * (m % 2) + b, :]
                                    nc.tensor.matmul(bank, identb[:, :],
                                                     band[:, min(t, 1), :, :, :].rearrange("p h k c -> p (h k c)"),
                                                     start=True, stop=False)
                                    for j in range(2):
                                        head = 4 * g + 2 * b + j
                                        c0 = 256 * j + (0 if t else P)
                                        last = nc.tensor.matmul(ps[:, 2 * (m % 2) + b, c0:256 * j + 256],
                                                                q_rot[:, head, P * t:P * t + P],
                                                                k_rot[:, g, P * max(t - 1, 0):P * t + P],
                                                                start=False, stop=j == 1)
                                last.then_inc(s_ready, 1)
                            if 1 <= m <= UNITS:
                                k = m - 1
                                pe.wait_ge(p_ready, k + 1)
                                if k:
                                    pe.wait_ge(pt_ready, k)
                                for j in range(4):
                                    for kt in range(2):
                                        c = 256 * (j % 2) + P * kt
                                        last = nc.tensor.transpose(ps[:, 4 + j // 2, c:c + P],
                                                                   pw[:, k % 2, j, P * kt:P * kt + P], ident)
                                last.then_inc(t_ready, 1)
                            if m >= 2:
                                k = m - 2
                                t, g = divmod(k, KV)
                                pe.wait_ge(pt_ready, k + 1)
                                if g == 0 and t:
                                    pe.wait_ge(y_free, t)
                                for j in range(4):
                                    head = 4 * g + j
                                    for kt in range(0 if t else 1, 2):
                                        last = nc.tensor.matmul(ps[:, 6 + head // 8, DH * (head % 8):DH * (head % 8) + DH],
                                                                pt[:, k % 2, j, kt, :],
                                                                v_tok[:, t - 1 + kt, DH * g:DH * g + DH],
                                                                start=kt == (0 if t else 1), stop=kt == 1)
                                if g == KV - 1:
                                    last.then_inc(y_ready, 1)

                    @block.scalar
                    def _(act):
                        for m in range(UNITS):
                            t, g = divmod(m, KV)
                            act.wait_ge(m_ready, m + 1)
                            if m >= 2:
                                act.wait_ge(t_ready, m - 1)
                            for j in range(4):
                                last = nc.scalar.activation(pw[:, m % 2, j, :],
                                                            ps[:, 2 * (m % 2) + j // 2, 256 * (j % 2):256 * (j % 2) + 256],
                                                            ACT.Exp, bias=neg_m[:, t, 4 * g + j:4 * g + j + 1],
                                                            accum_out=sums[:, t, 4 * g + j:4 * g + j + 1])
                            last.then_inc(p_ready, 1)
                            if g == KV - 1:
                                act.wait_ge(sink_arg, t + 1)
                                nc.scalar.activation(sink_w[:, t % 2, :], sink_w[:, t % 2, :], ACT.Exp
                                                     ).then_inc(sink_exp, 1)

                    @block.vector
                    def _(dve):
                        own = Chain(dve, dve_own6)
                        own(nc.vector.tensor_copy(identb[:, :], ident))
                        for first in range(2):
                            for j in range(2):
                                own(nc.vector.tensor_copy(band[:, first, j, :, :].rearrange("p k c -> p (k c)"),
                                                          const[:, C_BAND:C_BAND + 256]))
                        for j in range(2):
                            own(nc.vector.memset(band[:, 0, j, 0, :], NEG))
                        nc.vector.engine_nop().then_inc(band_ready, 1)
                        dve.wait_ge(sink_in, 16)
                        own(nc.vector.tensor_scalar(neg_sinks[:, :], sinks[:, :], -1.0, None, ALU.mult))
                        for m in range(UNITS + 2):
                            if m < UNITS:
                                t, g = divmod(m, KV)
                                dve.wait_ge(s_ready, m + 1)
                                own(nc.vector.tensor_reduce(
                                    neg4[:, :], ps[:, 2 * (m % 2):2 * (m % 2) + 2, :].rearrange("p b (j c) -> p b j c", j=2),
                                    X, ALU.max, negate=True))
                                nc.vector.tensor_tensor(neg_m[:, t, 4 * g:4 * g + 4], neg4[:, :],
                                                        neg_sinks[:, 4 * g:4 * g + 4], ALU.min).then_inc(m_ready, 1)
                                dve.wait_ge(m_ready, m + 1)
                                if g == KV - 1:
                                    nc.vector.tensor_tensor(sink_w[:, t % 2, :], sinks[:, :], neg_m[:, t, :], ALU.add
                                                            ).then_inc(sink_arg, 1)
                            if 1 <= m <= UNITS:
                                k = m - 1
                                dve.wait_ge(t_ready, k + 1)
                                nc.vector.tensor_copy(pt[:, k % 2, :, :, :].rearrange("p j k c -> p (j k c)"),
                                                      ps[:, 4:6, :].rearrange("p b c -> p (b c)")).then_inc(pt_ready, 1)
                            if m >= 2 and (m - 2) % KV == KV - 1:
                                t = (m - 2) // KV
                                dve.wait_ge(y_ready, t + 1)
                                dve.wait_ge(sink_exp, t + 1)
                                own(nc.vector.tensor_tensor(sums[:, t, :], sums[:, t, :], sink_w[:, t % 2, :], ALU.add))
                                own(nc.vector.reciprocal(sums[:, t, :], sums[:, t, :]))
                                nc.vector.tensor_tensor(y_sb[:, t, :].rearrange("p (h d) -> p h d", d=DH),
                                                        ps[:, 6:8, :].rearrange("p b (h d) -> p (b h) d", d=DH),
                                                        sums[:, t, :].unsqueeze(2).broadcast_to([P, HF, DH]), ALU.mult
                                                        ).then_inc(y_free, 1)

            with ExitStack() as ph:
                wp = sb("wp", [P, HF * DH // P, D], F32, ph)
                bp = sb("bp", [P, D], F32, ph)
                norm2 = sb("norm2", [P, D], F32, ph)
                wg = sb("wg", [P, NE], F32, ph)
                bg = sb("bg", [P, NE], F32, ph)
                h2 = sb("h2", [P, NT, D], F32, ph)
                y_t = sb("y_t", [P, 2, 8, P], F32, ph)
                gl = sb("gl", [P, NT, NE], F32, ph)
                top = sb("top", [P, NT, 8], F32, ph)
                topi = sb("topi", [P, NT, 8], U32, ph)
                topf = sb("topf", [P, NT, 8], F32, ph)
                ew = sb("ew", [P, NT, TOPK], F32, ph)
                esum = sb("esum", [P, 2, NT], F32, ph)
                eq = sb("eq", [P, NT, NE], F32, ph)
                in7, dve_own7, var7, root7, h2_ready, yt_psum, yt_ready, pr_psum, h2t_psum, h2t_ready, gl_psum = (
                    sem(n) for n in ("in7", "dve_own7", "var7", "root7", "h2_ready", "yt_psum", "yt_ready", "pr_psum",
                                     "h2t_psum", "h2t_ready", "gl_psum"))
                ew_arg, ew_exp = sem("ew_arg"), sem("ew_exp")
                block = ph.enter_context(nc.Block())

                @block.sync
                def _(sp):
                    sp.dma_start(wp[:, :, :], a["proj_w"].rearrange("(f p) d -> p f d", p=P)).then_inc(in7, 16)
                    sp.dma_start(bp[:, :], a["proj_b"].partition_broadcast(P)).then_inc(in7, 16)
                    sp.dma_start(norm2[:, :], a["ffn_norm_w"].partition_broadcast(P)).then_inc(in7, 16)
                    sp.dma_start(wg[:, :], a["gate_w"]).then_inc(in7, 16)
                    sp.dma_start(bg[:, :], a["gate_b"].partition_broadcast(P)).then_inc(in7, 16)

                @block.tensor
                def _(pe):
                    pe.wait_ge(in7, 80)
                    for t in range(NT + 1):
                        if t < NT:
                            for f in range(8):
                                b = 2 * (t % 2) + f // 4
                                last = nc.tensor.transpose(ps[:, b, P * (f % 4):P * (f % 4) + P],
                                                           y_sb[:, t, P * f:P * f + P], ident)
                                if f % 4 == 3:
                                    last.then_inc(yt_psum, 1)
                        if t:
                            k = t - 1
                            pe.wait_ge(yt_ready, 2 * k + 2)
                            for f in range(8):
                                last = nc.tensor.matmul(ps[:, 4 + k // 4, P * (k % 4):P * (k % 4) + P],
                                                        y_t[:, k % 2, f, :], wp[:, f, :], start=f == 0, stop=f == 7)
                            last.then_inc(pr_psum, 1)
                    pe.wait_ge(h2_ready, 1)
                    for t in range(NT):
                        last = nc.tensor.transpose(ps[:, t // 4, P * (t % 4):P * (t % 4) + P], h2[:, t, :], ident)
                        if t % 4 == 3:
                            last.then_inc(h2t_psum, 1)
                    for t in range(NT):
                        pe.wait_ge(h2t_ready, t // 4 + 1)
                        last = nc.tensor.matmul(ps[:, 6, NE * t:NE * t + NE], hT[:, P * t:P * t + P], wg[:, :],
                                                start=True, stop=True)
                    last.then_inc(gl_psum, 1)

                @block.scalar
                def _(act):
                    for t in range(NT):
                        for b in range(2):
                            act.wait_ge(yt_psum, 2 * t + b + 1)
                            if t >= 2:
                                act.wait_ge(pr_psum, t - 1)
                            nc.scalar.copy(y_t[:, t % 2, 4 * b:4 * b + 4, :].rearrange("p f c -> p (f c)"),
                                           ps[:, 2 * (t % 2) + b, :]).then_inc(yt_ready, 1)
                    act.wait_ge(var7, 1)
                    nc.scalar.activation(st[:, 3, :], st[:, 2, :], ACT.Sqrt).then_inc(root7, 1)
                    for n in range(2):
                        act.wait_ge(h2t_psum, n + 1)
                        nc.scalar.copy(hT[:, 512 * n:512 * n + 512], ps[:, n, :]).then_inc(h2t_ready, 1)
                    act.wait_ge(ew_arg, 1)
                    nc.scalar.activation(ew[:, :, :], ew[:, :, :], ACT.Exp).then_inc(ew_exp, 1)

                @block.vector
                def _(dve):
                    own = Chain(dve, dve_own7)
                    dve.wait_ge(in7, 80)
                    for n in range(2):
                        r = slice(4 * n, 4 * n + 4)
                        own(nc.vector.tensor_tensor(x3[:, r, :], x2[:, r, :],
                                                    bp[:, :].unsqueeze(1).broadcast_to([P, 4, D]), ALU.add))
                        dve.wait_ge(pr_psum, 4 * n + 4)
                        own(nc.vector.tensor_tensor(x3[:, r, :], ps[:, 4 + n, :].rearrange("p (t d) -> p t d", d=D),
                                                    x3[:, r, :], ALU.add))
                    normalise(own, (root7, 1), None, var7, x3, h2, False)
                    nc.vector.tensor_tensor(h2[:, :, :], h2[:, :, :],
                                            norm2[:, :].unsqueeze(1).broadcast_to([P, NT, D]), ALU.mult
                                            ).then_inc(h2_ready, 1)
                    dve.wait_ge(gl_psum, 1)
                    own(nc.vector.tensor_tensor(gl[:, :, :], ps[:, 6, 0:NT * NE].rearrange("p (t e) -> p t e", e=NE),
                                                bg[:, :].unsqueeze(1).broadcast_to([P, NT, NE]), ALU.add))
                    for t in range(NT):
                        own(nc.vector.max(top[:, t, :], gl[:, t, :]))
                        own(nc.vector.max_index(topi[:, t, :], top[:, t, :], gl[:, t, :]))
                    own(nc.vector.tensor_copy(topf[:, :, :], topi[:, :, :]))
                    nc.vector.tensor_tensor(ew[:, :, :], top[:, :, 0:TOPK], top[:, :, 0:1].broadcast_to([P, NT, TOPK]),
                                            ALU.subtract).then_inc(ew_arg, 1)
                    dve.wait_ge(ew_exp, 1)
                    own(nc.vector.tensor_reduce(esum[:, 0, :], ew[:, :, :], X, ALU.add))
                    own(nc.vector.reciprocal(esum[:, 1, :], esum[:, 0, :]))
                    own(nc.vector.tensor_tensor(ew[:, :, :], ew[:, :, :],
                                                esum[:, 1, :].unsqueeze(2).broadcast_to([P, NT, TOPK]), ALU.mult))
                    eio = const[:, C_EIOTA:C_EIOTA + NE].unsqueeze(1).broadcast_to([P, NT, NE])
                    for j in range(TOPK):
                        dst = comb if j == 0 else eq
                        own(nc.vector.tensor_tensor(dst[:, :, :], eio, topf[:, :, j:j + 1].broadcast_to([P, NT, NE]),
                                                    ALU.is_equal))
                        own(nc.vector.tensor_tensor(dst[:, :, :], dst[:, :, :],
                                                    ew[:, :, j:j + 1].broadcast_to([P, NT, NE]), ALU.mult))
                        if j:
                            own(nc.vector.tensor_tensor(comb[:, :, :], comb[:, :, :], eq[:, :, :], ALU.add))

        with ExitStack() as ph:
            w_up = sb("w_up", [P, 2, 2 * FF], F32, ph)
            w_down = sb("w_down", [P, 2, D], F32, ph)
            silu = sb("silu", [P, 2, 512], F32, ph)
            act_t = sb("act_t", [P, 2, 512], F32, ph)
            part = sb("part", [P, 2, 4, D], F32, ph)
            acc = sb("acc", [P, NT, D], F32, ph)
            w_in = [sem(f"expert_in{n}") for n in range(2)]
            gu_ready, silu_ready, gated, d_ready, d_free, part_free, acc_zero, dve_own8, o_ready, o_out = (
                sem(n) for n in ("gu_ready", "silu_ready", "gated", "d_ready", "d_free", "part_free",
                                 "acc_zero", "dve_own8", "o_ready", "o_out"))
            block = ph.enter_context(nc.Block())
            sp_passed8 = sem("sp_passed8")
            NU = 2 * NE
            G0, U0, D0 = 0, 2, 4

            def turns(eng, body):
                with eng.Fori(0, NE // 2 - 1) as turn:
                    body(turn * 2, False)
                body(NE - 2, True)

            @block.sync
            def _(sp):
                def load(e, s):
                    up = a["W_up"][bass.ds(e, 1)].rearrange("e p n -> (e p) n")
                    down = a["W_down"][bass.ds(e, 1)].rearrange("e p n -> (e p) n")
                    sp.dma_start(w_up[:, s, :], up).then_inc(w_in[s], 16)
                    sp.dma_start(w_down[:, s, :], down).then_inc(w_in[s], 16)

                for s in range(2):
                    load(s, s)

                def body(e, last):
                    if not last:
                        for s in range(2):
                            sp.wait_ge(d_ready, 2 * e + 2 * s + 2)
                            sp.sem_inc(sp_passed8, 1)
                            load(e + 2 + s, s)

                turns(sp, body)
                sp.wait_ge(o_ready, 1)
                sp.dma_start(out.rearrange("b (t p) d -> p (b t) d", p=P), x1[:, :, :]).then_inc(o_out, 16)
                sp.wait_ge(o_out, 16)

            @block.tensor
            def _(pe):
                def up(e, k):
                    s, n = k // 2 % 2, k % 2
                    if n == 0:
                        pe.wait_ge(w_in[s], 16 * (e + k // 2 - s) + 32)
                    pe.wait_ge(gated, 2 * e + k + 1)
                    r = slice(512 * n, 512 * n + 512)
                    nc.tensor.matmul(ps[:, G0 + n, :], w_up[:, s, FF:2 * FF], hT[:, r], start=True, stop=True)
                    nc.tensor.matmul(ps[:, U0 + n, :], w_up[:, s, 0:FF], hT[:, r], start=True, stop=True
                                     ).then_inc(gu_ready, 1)

                def down(e, k):
                    s, n = k // 2, k % 2
                    pe.wait_ge(gated, 2 * e + k + 3)
                    pe.wait_ge(d_free, 2 * e + k + 1)
                    for t in range(4):
                        last = nc.tensor.matmul(ps[:, D0 + n, P * t:P * t + P], act_t[:, n, P * t:P * t + P],
                                                w_down[:, s, :], start=True, stop=True)
                    last.then_inc(d_ready, 1)

                up(0, 0)

                def body(e, last):
                    for k in range(4):
                        if not (last and k == 3):
                            up(e, k + 1)
                        down(e, k)

                turns(pe, body)

            @block.scalar
            def _(act):
                def body(e, last):
                    for k in range(4):
                        act.wait_ge(gu_ready, 2 * e + k + 1)
                        act.wait_ge(gated, 2 * e + k + 1)
                        nc.scalar.activation(silu[:, k % 2, :], ps[:, G0 + k % 2, :], ACT.Silu).then_inc(silu_ready, 1)

                turns(act, body)

            @block.vector
            def _(dve):
                own = Chain(dve, dve_own8)
                dve.sem_inc(gated, 2)
                dve.sem_inc(d_free, 2)

                def gate(e, k):
                    dve.wait_ge(silu_ready, 2 * e + k + 1)
                    nc.vector.tensor_tensor(act_t[:, k % 2, :], silu[:, k % 2, :], ps[:, U0 + k % 2, :], ALU.mult
                                            ).then_inc(gated, 1)

                def weighted(e, k):
                    n = k % 2
                    dve.wait_ge(d_ready, 2 * e + k + 1)
                    dve.wait_ge(part_free, 2 * e + k + 1)
                    weight = comb[:, 4 * n:4 * n + 4, bass.ds(e + k // 2, 1)]
                    nc.vector.tensor_tensor(part[:, n, :, :], ps[:, D0 + n, :].rearrange("p (t d) -> p t d", d=D),
                                            weight.broadcast_to([P, 4, D]), ALU.mult).then_inc(d_free, 1)

                gate(0, 0)

                def body(e, last):
                    for k in range(4):
                        if not (last and k == 3):
                            gate(e, k + 1)
                        weighted(e, k)

                turns(dve, body)
                dve.wait_ge(part_free, NU + 2)
                own(nc.vector.tensor_tensor(x3[:, :, :], x3[:, :, :], acc[:, :, :], ALU.add))
                own(nc.vector.scalar_tensor_tensor(x1[:, :, :].rearrange("p t d -> p (t d)"),
                                                   x3[:, :, :].rearrange("p t d -> p (t d)"), tanhs[:, 1:2],
                                                   x1[:, :, :].rearrange("p t d -> p (t d)"), ALU.mult, ALU.add))
                nc.vector.engine_nop().then_inc(o_ready, 1)

            @block.gpsimd
            def _(pool):
                nc.gpsimd.memset(acc[:, :, :], 0.0).then_inc(acc_zero, 1)
                pool.sem_inc(part_free, 2)
                pool.wait_ge(acc_zero, 1)

                def body(e, last):
                    for k in range(4):
                        n = k % 2
                        pool.wait_ge(d_free, 2 * e + k + 3)
                        pool.wait_ge(part_free, 2 * e + k + 1)
                        nc.gpsimd.tensor_tensor(acc[:, 4 * n:4 * n + 4, :], acc[:, 4 * n:4 * n + 4, :],
                                                part[:, n, :, :], ALU.add).then_inc(part_free, 1)

                turns(pool, body)




def _parts(value):
    out, rest = [], np.float32(value)
    for _ in range(3):
        bits = np.array([rest], np.float32).view(np.uint32)
        high = ((bits + 0x8000) & np.uint32(0xFFFF0000)).view(np.float32)[0]
        out.append(high)
        rest = np.float32(rest - high)
    assert rest == 0
    return out


def _constants():
    c = np.zeros((P, C_END), np.float32)
    r = np.arange(P)
    c[:, C_ID:C_ID + P] = np.eye(P)
    c[:, C_SUM:C_SUM + P] = (r[:, None] % DH == r[None, :] % DH) * float(DH) ** -0.5
    c[:, C_BAND:C_BAND + P] = np.where(r[None, :] >= r[:, None] + P - WIN, 0, NEG)
    c[:, C_BAND + P:C_BAND + 2 * P] = np.where(r[None, :] <= r[:, None], 0, NEG)
    c[:, C_IOTA:C_IOTA + 64] = np.arange(64)
    c[:, C_TRI:C_TRI + 64] = r[:, None] < np.arange(64)[None, :]
    c[:, C_ONES:C_ONES + 128] = 1.0
    c[:, C_START] = KC * r
    c[:, C_EXTS] = c[:, C_EXTT] = 0.0
    for n, m in enumerate(_parts(MASKED)):
        c[n, C_EXTS], c[n, C_EXTT] = m, -m
        c[3 + n, C_EXTT] = 1.0
    c[:, C_EIOTA:C_EIOTA + NE] = np.arange(NE)
    pos = np.arange(S, dtype=np.float32) / np.float32(32.0)
    inv = (1.0 / np.float32(150000.0) ** (np.arange(0, DH, 2, dtype=np.float32) / np.float32(DH))).astype(np.float32)
    freq = (pos[:, None] * inv[None, :]).astype(np.float32)
    sin, cos = np.sin(freq).T, np.cos(freq).T
    cs = np.zeros((P, S), np.float32)
    cs[0:DH:2], cs[1:DH:2] = cos, cos
    cs[DH::2], cs[DH + 1::2] = -sin, sin
    valid = (np.arange(NC * KC) < SK).astype(np.float32)[:, None]
    return c, cs, valid


_OUT = ("out_0_dram", (1, S, D), "float32")


def kernel(x, ctx_1024, mask_Bx1xS2_ik0, g_xattn, g_ffn, L0_xattn_Wq, L0_xattn_bq, L0_xattn_Wk, L0_xattn_bk,
           L0_xattn_Wv, L0_xattn_bv, L0_xattn_Wo, L0_xattn_bo, L0_ffn_attn_norm_w, L0_ffn_ffn_norm_w, L0_ffn_qkv_w,
           L0_ffn_qkv_b, L0_ffn_proj_w, L0_ffn_proj_b, L0_ffn_attn_sink, L0_ffn_gate_w, L0_ffn_gate_b, L0_ffn_W_up,
           L0_ffn_W_down):
    import concourse.bacc as bacc
    from concourse.bass_utils import run_bass_kernel_spmd

    consts, cs, valid = _constants()
    rows = np.array([(NP * half + pair) * DK + d for half in range(2) for d in range(DK) for pair in range(NP)])
    cols = np.array([[DH * f + c for c in range(DH)] + [DH * f + (c ^ 1) for c in range(DH)] for f in range(HF + KV)])
    qkv_w, qkv_b = np.asarray(L0_ffn_qkv_w), np.asarray(L0_ffn_qkv_b)
    ctx_t = np.zeros((D, NC * KC), np.float32)
    ctx_t[:, :SK] = np.asarray(ctx_1024)[0].T
    mask = np.zeros((NC * KC,), np.int32)
    mask[:SK] = np.asarray(mask_Bx1xS2_ik0)[0, 0]
    arrays = {
        "x": x, "ctxT": ctx_t, "mask": mask, "valid": valid, "consts": consts, "cs": cs,
        "g_xattn": g_xattn, "g_ffn": g_ffn,
        "WqT": np.asarray(L0_xattn_Wq)[rows].T, "bq": np.asarray(L0_xattn_bq)[rows][:, None],
        "WkT": np.asarray(L0_xattn_Wk)[rows].T, "bk": np.asarray(L0_xattn_bk)[rows][:, None],
        "WvT": np.asarray(L0_xattn_Wv).T, "bv": L0_xattn_bv, "WoT": np.asarray(L0_xattn_Wo).T, "bo": L0_xattn_bo,
        "attn_norm_w": L0_ffn_attn_norm_w, "ffn_norm_w": L0_ffn_ffn_norm_w,
        "wqk": qkv_w[:, cols], "bqk": qkv_b[cols].T, "wvv": qkv_w[:, (HF + KV) * DH:], "bvv": qkv_b[(HF + KV) * DH:],
        "proj_w": L0_ffn_proj_w, "proj_b": L0_ffn_proj_b, "sink": L0_ffn_attn_sink,
        "gate_w": L0_ffn_gate_w, "gate_b": L0_ffn_gate_b, "W_up": L0_ffn_W_up, "W_down": L0_ffn_W_down,
    }
    arrays = {f"in_{n}": np.ascontiguousarray(v) for n, v in arrays.items()}
    nc = bacc.Bacc("TRN2", target_bir_lowering=False, num_devices=1)
    args = {n[3:]: nc.dram_tensor(n, v.shape, mybir.dt.from_np(v.dtype), kind="ExternalInput").ap()
            for n, v in arrays.items()}
    name, shape, dtype = _OUT
    out = nc.dram_tensor(name, shape, mybir.dt.from_np(np.dtype(dtype)), kind="ExternalOutput").ap()
    build(nc, args, out)
    r = run_bass_kernel_spmd(nc, [arrays], core_ids=[0])
    return r.results[0][name]
```

```python
from contextlib import ExitStack

import numpy as np

import concourse.bass as bass
from concourse import mybir

F32 = mybir.dt.float32
BF16 = mybir.dt.bfloat16
I32 = mybir.dt.int32
U32 = mybir.dt.uint32
ALU = mybir.AluOpType
ACT = mybir.ActivationFunctionType
X = mybir.AxisListType.X

P = 128
S = 1024
D = 128
NT = S // P
SK = 6404
KC = 126
NC = -(-SK // KC)
TURNS, PAIRS = 6, 5
NCE = TURNS * PAIRS * 2
assert NCE >= NC
H = 16
DK = D // H
ROWS = 64
NP = H * ROWS // P
Q_PARTS = [0, 0, 1, 1, 0, 2]
K_PARTS = [0, 1, 0, 1, 2, 0]
EXT = ROWS - DK * len(Q_PARTS)
ROW_MASK = DK * len(Q_PARTS)
ROW_MAX = ROW_MASK + 3
QB = 256
NB = S // QB
QT = QB // P
NG = H // 4
HF = 16
KV = 4
DH = 64
NE = 32
FF = 128
TOPK = 4
WIN = 128
EPS = 1e-5
MASKED = 1e9
NEG = -1e30

C_ID, C_SUM, C_BAND, C_IOTA, C_TRI, C_ONES, C_START, C_EXTS, C_EXTT = 0, 128, 256, 512, 576, 640, 768, 769, 770
C_EIOTA, C_KA, C_KB, C_BA, C_BB, C_ROW4, C_END = 771, 803, 804, 805, 806, 807, 808


def head_of(g, j):
    return divmod(4 * g + j, NP)


def each_chunk(eng, m, body):

    def pairs(first):
        with eng.Fori(0, PAIRS) as pair:
            c = pair * 2 + first
            with eng.If(c < m):
                body(c, 0)
                with eng.If(c + 1 < m):
                    body(c + 1, 1)

    pairs(0)
    with eng.If(m > 2 * PAIRS):
        with eng.Fori(1, TURNS) as turn:
            with eng.If(turn * (2 * PAIRS) < m):
                pairs(turn * (2 * PAIRS))


class Chain:

    def __init__(self, engine, sem):
        self.engine, self.sem, self.count = engine, sem, 0

    def __call__(self, instruction):
        self.count += 1
        instruction.then_inc(self.sem, 1)
        self.engine.wait_ge(self.sem, self.count)


def build(nc, a, out):
    with ExitStack() as root:
        sb_of, sem_of = {}, {}

        def sb(name, shape, dt=F32, ctx=root):
            return ctx.enter_context(nc.sbuf_tensor(name, shape, dt))

        def sem(name):
            return root.enter_context(nc.semaphore(name))

        ps = root.enter_context(nc.psum_tensor("ps", [P, 8, 512], F32))
        const = sb("const", [P, C_END])
        ident = const[:, C_ID:C_ID + P]
        x0 = sb("x0", [P, NT, D])
        x1 = sb("x1", [P, NT, D])
        wrk = sb("wrk", [P, NT, D])
        st = sb("st", [P, 8, NT])
        gates = sb("gates", [P, 2])
        tanhs = sb("tanhs", [P, 2])
        k_dram = nc.dram_tensor("k_scratch", [NCE + 1, P, NP, KC], BF16).ap()
        v_dram = nc.dram_tensor("v_scratch", [NCE + 1, KC, H * (DK + 1)], F32).ap()
        q_dram = nc.dram_tensor("q_scratch", [P, NP, S], BF16).ap()

        def normalise(chain_dve, act_wait, act_signal, dve_signal, src, dst, centre):
            dve = nc.vector
            total, mean, var, root_, rstd = (st[:, n, :] for n in range(5))
            cur = src
            if centre:
                chain_dve(dve.tensor_reduce(total, src[:, :, :], X, ALU.add))
                chain_dve(dve.tensor_scalar(mean, total, 1.0 / D, None, ALU.mult))
                chain_dve(dve.tensor_tensor(dst[:, :, :], src[:, :, :],
                                            mean.unsqueeze(2).broadcast_to([P, NT, D]), ALU.subtract))
                cur = dst
            chain_dve(dve.tensor_tensor(wrk[:, :, :], cur[:, :, :], cur[:, :, :], ALU.mult))
            chain_dve(dve.tensor_reduce(total, wrk[:, :, :], X, ALU.add))
            dve.tensor_scalar(var, total, 1.0 / D, EPS, ALU.mult, ALU.add).then_inc(dve_signal, 1)
            nc.vector.wait_ge(*act_wait)
            chain_dve(dve.reciprocal(rstd, root_))
            chain_dve(dve.tensor_tensor(dst[:, :, :], cur[:, :, :],
                                        rstd.unsqueeze(2).broadcast_to([P, NT, D]), ALU.mult))

        with ExitStack() as cross:
            q_all = sb("q_all", [P, 2, NP, S], BF16, cross)
            chunk_list = sb("chunk_list", [1, NCE + 2], I32, cross)
            oacc = sb("oacc", [P, NB, NG, QB], F32, cross)
            wo = sb("wo", [P, D], F32, cross)
            bo = sb("bo", [P, D], F32, cross)

            with ExitStack() as ph:
                xn = sb("xn", [P, NT, D], F32, ph)
                xT = sb("xT", [P, S], F32, ph)
                qf = sb("qf", [P, S], F32, ph)
                qr = sb("qr", [P, S], F32, ph)
                qp = sb("qp", [P, 3, S], BF16, ph)
                qext = sb("qext", [EXT, S], BF16, ph)
                wq = sb("wq", [P, D], F32, ph)
                bq = sb("bq", [P, 1], F32, ph)
                mask_c = sb("mask_c", [NC, KC], I32, ph)
                mask_f = sb("mask_f", [NC, KC], F32, ph)
                fl = sb("fl", [NC, 4], F32, ph)
                onehot = sb("onehot", [NC, NC], F32, ph)
                consts_in, x_in, wq_in, mask_in, late_in = (sem(n) for n in
                                                             ("consts_in", "x_in", "wq_in", "mask_in", "late_in"))
                dve_own1, var_ready1, root_ready1, xn_ready, flag_ready, pos_ready = (
                    sem(n) for n in ("dve_own1", "var_ready1", "root_ready1", "xn_ready", "flag_ready", "pos_ready"))
                xt_in_psum, xt_ready, q_in_psum, q_parts_ready, q_written, q_loaded, listed = (
                    sem(n) for n in ("xt_in_psum", "xt_ready", "q_in_psum", "q_parts_ready", "q_written",
                                     "q_loaded", "listed"))
                q_zero = sem("q_zero")
                block = ph.enter_context(nc.Block())

                @block.gpsimd
                def _(pool):
                    nc.gpsimd.memset(q_all[:, :, :, :].rearrange("p h n s -> p (h n s)").bitcast(F32), 0.0
                                     ).then_inc(q_zero, 1)

                @block.sync
                def _(sp):
                    sp.dma_start(x0[:, :, :], a["x"].rearrange("b (t p) d -> p (b t) d", p=P)).then_inc(x_in, 16)
                    sp.dma_start(mask_c[:, :], a["mask"].rearrange("(c k) -> c k", k=KC)).then_inc(mask_in, 16)
                    sp.dma_start(const[:, :], a["consts"]).then_inc(consts_in, 16)
                    sp.dma_start(wq[:, :], a["WqT"]).then_inc(wq_in, 16)
                    sp.dma_start(bq[:, :], a["bq"]).then_inc(wq_in, 16)
                    sp.dma_start(gates[:, 0:1], a["g_xattn"].partition_broadcast(P)).then_inc(late_in, 16)
                    sp.dma_start(gates[:, 1:2], a["g_ffn"].partition_broadcast(P)).then_inc(late_in, 16)
                    sp.dma_start(wo[:, :], a["WoT"]).then_inc(late_in, 16)
                    sp.dma_start(bo[:, :], a["bo"].partition_broadcast(P)).then_inc(late_in, 16)
                    sp.wait_ge(q_parts_ready, 1)
                    for half in range(2):
                        for n, part in enumerate(Q_PARTS):
                            r = ROWS * half + DK * n
                            sp.dma_start(q_dram[r:r + DK].rearrange("d p s -> (d p) s"),
                                         qp[64 * half:64 * half + 64, part, :]).then_inc(q_written, 16)
                        r = ROWS * half + ROW_MASK
                        sp.dma_start(q_dram[r:r + EXT, :, :],
                                     qext[:, :].unsqueeze(1).broadcast_to([EXT, NP, S])).then_inc(q_written, 16)
                    sp.wait_ge(q_written, 2 * (len(Q_PARTS) + 1) * 16)
                    sp.wait_ge(q_zero, 1)
                    for half in range(2):
                        r = slice(ROWS * half, ROWS * half + ROWS)
                        sp.dma_start(q_all[r, half, :, :], q_dram[r]).then_inc(q_loaded, 16)
                    sp.wait_ge(q_loaded, 32)
                    sp.wait_ge(late_in, 64)

                @block.vector
                def _(dve):
                    own = Chain(dve, dve_own1)
                    dve.wait_ge(x_in, 16)
                    normalise(own, (root_ready1, 1), None, var_ready1, x0, xn, True)
                    nc.vector.engine_nop().then_inc(xn_ready, 1)
                    dve.wait_ge(mask_in, 16)
                    dve.wait_ge(consts_in, 16)
                    own(nc.vector.tensor_scalar(mask_f[:, :], mask_c[:, :], 0.0, None, ALU.not_equal))
                    own(nc.vector.tensor_reduce(fl[:, 0:1], mask_f[:, :], X, ALU.max))
                    nc.vector.engine_nop().then_inc(flag_ready, 1)
                    dve.wait_ge(pos_ready, 1)
                    own(nc.vector.tensor_scalar(fl[:, 1:2], ps[0:NC, 0, 0:1], 0.0, None, ALU.is_equal))
                    own(nc.vector.tensor_tensor(fl[:, 2:3], fl[:, 0:1], fl[:, 1:2], ALU.max))
                    nc.vector.engine_nop().then_inc(flag_ready, 1)
                    dve.wait_ge(pos_ready, 2)
                    own(nc.vector.tensor_copy(fl[:, 3:4], ps[0:NC, 1, 0:1]))
                    own(nc.vector.tensor_scalar(onehot[:, :], const[0:NC, C_IOTA:C_IOTA + NC],
                                                fl[:, 3:4], fl[:, 2:3], ALU.is_equal, ALU.mult))
                    nc.vector.engine_nop().then_inc(flag_ready, 1)
                    dve.wait_ge(pos_ready, 3)
                    own(nc.vector.memset(chunk_list[:, :], 0))
                    own(nc.vector.tensor_copy(chunk_list[0:1, 0:NC], ps[0:1, 2, 0:NC]))
                    own(nc.vector.tensor_copy(chunk_list[0:1, NCE:NCE + 1], ps[0:1, 3, 0:1]))
                    own(nc.vector.tensor_scalar(chunk_list[0:1, NCE + 1:NCE + 2], ps[0:1, 3, 0:1], -1.0, None,
                                                ALU.add))
                    for n in range(2):
                        dve.wait_ge(xt_in_psum, n + 1)
                        last = nc.vector.tensor_copy(xT[:, 512 * n:512 * n + 512], ps[:, 4 + n, :])
                        last.then_inc(xt_ready, 1)
                    for n in range(2):
                        dve.wait_ge(q_in_psum, n + 1)
                        own(nc.vector.tensor_scalar(qf[:, 512 * n:512 * n + 512], ps[:, 6 + n, :], bq[:, 0:1],
                                                    float(DK) ** -0.5, ALU.add, ALU.mult))
                    own(nc.vector.tensor_copy(qp[:, 0, :], qf[:, :]))
                    own(nc.vector.tensor_tensor(qr[:, :], qf[:, :], qp[:, 0, :], ALU.subtract))
                    own(nc.vector.tensor_copy(qp[:, 1, :], qr[:, :]))
                    own(nc.vector.tensor_tensor(qp[:, 2, :], qr[:, :], qp[:, 1, :], ALU.subtract))
                    own(nc.vector.memset(qext[:, :], 0.0))
                    own(nc.vector.memset(qext[0:3, :], 1.0))
                    nc.vector.engine_nop().then_inc(q_parts_ready, 1)

                @block.scalar
                def _(act):
                    act.wait_ge(var_ready1, 1)
                    nc.scalar.activation(st[:, 3, :], st[:, 2, :], ACT.Sqrt).then_inc(root_ready1, 1)
                    act.wait_ge(late_in, 64)
                    nc.scalar.activation(tanhs[:, :], gates[:, :], ACT.Tanh).then_inc(listed, 1)
                    act.wait_ge(listed, 1)

                @block.tensor
                def _(pe):
                    one = const[0:NC, C_ONES:C_ONES + NC]
                    pe.wait_ge(flag_ready, 1)
                    nc.tensor.matmul(ps[0:NC, 0, 0:1], one, fl[:, 0:1], start=True, stop=True).then_inc(pos_ready, 1)
                    pe.wait_ge(flag_ready, 2)
                    nc.tensor.matmul(ps[0:NC, 1, 0:1], const[0:NC, C_TRI:C_TRI + NC], fl[:, 2:3],
                                     start=True, stop=True).then_inc(pos_ready, 1)
                    pe.wait_ge(flag_ready, 3)
                    nc.tensor.matmul(ps[0:1, 2, 0:NC], const[0:NC, C_START:C_START + 1], onehot[:, :],
                                     start=True, stop=True)
                    nc.tensor.matmul(ps[0:1, 3, 0:1], fl[:, 2:3], const[0:NC, C_ONES:C_ONES + 1],
                                     start=True, stop=True).then_inc(pos_ready, 1)
                    pe.wait_ge(xn_ready, 1)
                    for t in range(NT):
                        last = nc.tensor.transpose(ps[:, 4 + t // 4, P * (t % 4):P * (t % 4) + P], xn[:, t, :], ident)
                        if t % 4 == 3:
                            last.then_inc(xt_in_psum, 1)
                    pe.wait_ge(wq_in, 32)
                    for n in range(2):
                        pe.wait_ge(xt_ready, n + 1)
                        nc.tensor.matmul(ps[:, 6 + n, :], wq[:, :], xT[:, 512 * n:512 * n + 512],
                                         start=True, stop=True).then_inc(q_in_psum, 1)

            with ExitStack() as ph:
                wk = sb("wk", [P, NP, P], F32, ph)
                bk_in = sb("bk_in", [5, NP, P], F32, ph)
                bk = sb("bk", [5, NP, P], BF16, ph)
                bk_high = sb("bk_high", [5, NP, P], BF16, ph)
                wv = sb("wv", [P, D], F32, ph)
                bv = sb("bv", [P, D], F32, ph)
                ctx_in = sb("ctx_in", [P, 2, KC], F32, ph)
                mask_b = sb("mask_b", [P, 2, KC], I32, ph)
                valid = sb("valid", [KC, 2, 1], F32, ph)
                ctx_m = sb("ctx_m", [P, 2, KC], F32, ph)
                rows_m = sb("rows_m", [5, 2, KC], BF16, ph)
                unmasked = sb("unmasked", [P, 2, KC], F32, ph)
                k_high = sb("k_high", [P, 2, NP * KC], BF16, ph)
                k_rest = sb("k_rest", [P, 2, NP * KC], F32, ph)
                k_mid = sb("k_mid", [P, 2, NP * KC], BF16, ph)
                k_out = sb("k_out", [P, 2, NP * KC], BF16, ph)
                vv = sb("vv", [KC, 2, H, DK + 1], F32, ph)
                pool_passed = sem("pool_passed")
                w_in, sp_passed2, act_passed, bk_ready = (sem(n) for n in ("wkv_in", "sp_passed2", "act_passed",
                                                                          "bk_ready"))
                unmasked_ready, dve_own2 = sem("unmasked_ready"), sem("dve_own2")
                chunk_in = [sem(f"chunk_in{n}") for n in range(2)]
                valid_in = [sem(f"valid_in{n}") for n in range(2)]
                kv_written = [sem(f"kv_written{n}") for n in range(2)]
                masked, k_in_psum, v_in_psum, high_ready, rest_ready, mid_ready, k_ready, v_ready = (
                    sem(n) for n in ("masked", "k_in_psum", "v_in_psum", "high_ready", "rest_ready", "mid_ready",
                                     "k_ready", "v_ready"))
                block = ph.enter_context(nc.Block())

                def kbanks(s):
                    return ps[:, 2 * s:2 * s + 2, 0:4 * KC]

                def flat(t, s):
                    return t[:, s, :].rearrange("p (b n) -> p b n", b=2)

                @block.sync
                def _(sp):
                    sp.dma_start(wk[:, :, :], a["wk"]).then_inc(w_in, 16)
                    sp.dma_start(bk_in[:, :, :], a["bkx"]).then_inc(w_in, 16)
                    sp.dma_start(wv[:, :], a["WvT"]).then_inc(w_in, 16)
                    sp.dma_start(bv[:, :], a["bv"].partition_broadcast(P)).then_inc(w_in, 16)
                    n = sp.value_load(chunk_list[0:1, NCE:NCE + 1], min_val=1, max_val=NC)
                    for s in range(2):
                        sp.sem_inc(kv_written[s], 16)

                    def load(c, s):
                        off = sp.value_load(chunk_list[0:1, bass.ds(c, 1)], min_val=0, max_val=(NC - 1) * KC)
                        sp.dma_start(ctx_in[:, s, :], a["ctxT"][:, bass.ds(off, KC)]).then_inc(chunk_in[s], 16)
                        sp.dma_start(mask_b[:, s, :], a["mask"][bass.ds(off, KC)].partition_broadcast(P)
                                     ).then_inc(chunk_in[s], 16)
                        return off

                    def load_valid(off, s):
                        sp.dma_start(valid[:, s, :], a["valid"][bass.ds(off, KC), :]).then_inc(valid_in[s], 16)

                    def body(c, s):
                        sp.wait_ge(masked, c + 1)
                        sp.sem_inc(sp_passed2, 1)
                        sp.wait_ge(v_in_psum, c + 1)
                        sp.sem_inc(sp_passed2, 1)
                        off = load(c + 2, s)
                        sp.wait_ge(v_ready, c + 3)
                        sp.sem_inc(sp_passed2, 1)
                        load_valid(off, s)
                        sp.wait_ge(k_ready, c + 3)
                        sp.sem_inc(sp_passed2, 1)
                        sp.dma_start(k_dram[bass.ds(c, 1)].rearrange("c r p k -> (c r) (p k)"), k_out[:, s, :]
                                     ).then_inc(kv_written[s], 16)
                        sp.dma_start(v_dram[bass.ds(c, 1)].rearrange("c k n -> (c k) n"),
                                     vv[:, s, :, :].rearrange("k h d -> k (h d)")).then_inc(kv_written[s], 16)

                    for s in range(2):
                        load_valid(load(s, s), s)
                    each_chunk(sp, n, body)
                    for z, each, first in ((kv_written, 32, 16), (chunk_in, 32, 32), (valid_in, 16, 16)):
                        sp.wait_ge(z[0], (n + 1) // 2 * each + first)
                        sp.sem_inc(sp_passed2, 1)
                        sp.wait_ge(z[1], n // 2 * each + first)
                        sp.sem_inc(sp_passed2, 1)

                @block.tensor
                def _(pe):
                    n = pe.value_load(chunk_list[0:1, NCE:NCE + 1], min_val=1, max_val=NC)
                    pe.wait_ge(w_in, 64)
                    pe.wait_ge(bk_ready, 1)

                    def body(c, s):
                        pe.wait_ge(chunk_in[s], (c - s) * 16 + 32)
                        pe.wait_ge(v_ready, c + 1)
                        nc.tensor.matmul(ps[0:KC, 4 + s, 0:D], ctx_in[:, s, :], wv[:, :],
                                         start=True, stop=True).then_inc(v_in_psum, 1)
                        pe.wait_ge(masked, c + 1)
                        pe.wait_ge(rest_ready, c * 2 + 2)
                        for p in range(NP):
                            bank = ps[:, 2 * s + p // 4, KC * (p % 4):KC * (p % 4) + KC]
                            nc.tensor.matmul(bank, wk[:, p, :], ctx_m[:, s, :], start=True, stop=False)
                            last = nc.tensor.matmul(bank, bk[:, p, :], rows_m[:, s, :], start=False, stop=True)
                        last.then_inc(k_in_psum, 1)

                    each_chunk(pe, n, body)

                @block.scalar
                def _(act):
                    n = act.value_load(chunk_list[0:1, NCE:NCE + 1], min_val=1, max_val=NC)
                    def body(c, s):
                        act.wait_ge(k_in_psum, c + 1)
                        act.wait_ge(rest_ready, c * 2 + 2)
                        nc.scalar.copy(flat(k_high, s), kbanks(s)).then_inc(high_ready, 1)
                        act.wait_ge(k_ready, c + 1)
                        for b in range(2):
                            act.wait_ge(rest_ready, c * 2 + (b + 5))
                            nc.scalar.copy(flat(k_mid, s)[:, b, :], flat(k_rest, s)[:, b, :]).then_inc(mid_ready, 1)

                    each_chunk(act, n, body)

                @block.gpsimd
                def _(pool):
                    n = pool.value_load(chunk_list[0:1, NCE:NCE + 1], min_val=1, max_val=NC)
                    pool.wait_ge(w_in, 64)

                    def body(c, s):
                        pool.wait_ge(chunk_in[s], (c - s) * 16 + 32)
                        pool.sem_inc(pool_passed, 1)
                        pool.wait_ge(rest_ready, c * 2 + 2)
                        pool.sem_inc(pool_passed, 1)
                        nc.gpsimd.tensor_scalar(unmasked[:, s, :], mask_b[:, s, :], 0.0, 0.0, ALU.is_equal,
                                                ALU.is_equal).then_inc(unmasked_ready, 1)
                        pool.wait_ge(unmasked_ready, c + 1)
                        nc.gpsimd.tensor_tensor(ctx_m[:, s, :], ctx_in[:, s, :], unmasked[:, s, :], ALU.mult)
                        nc.gpsimd.tensor_scalar(rows_m[:, s, :], unmasked[0:5, s, :], const[0:5, C_ROW4:C_ROW4 + 1],
                                                None, ALU.max).then_inc(masked, 1)

                    each_chunk(pool, n, body)

                @block.vector
                def _(dve):
                    own = Chain(dve, dve_own2)
                    n = dve.value_load(chunk_list[0:1, NCE:NCE + 1], min_val=1, max_val=NC)
                    for z, start in ((rest_ready, 4), (k_ready, 2), (v_ready, 2)):
                        dve.sem_inc(z, start)
                    dve.wait_ge(w_in, 64)
                    ka, kb = const[0:5, C_BA:C_BA + 1], const[0:5, C_BB:C_BB + 1]
                    own(nc.vector.tensor_copy(bk_high[:, :, :], bk_in[:, :, :]))
                    own(nc.vector.scalar_tensor_tensor(bk_in[:, :, :], bk_high[:, :, :], ka, bk_in[:, :, :],
                                                       ALU.mult, ALU.add))
                    own(nc.vector.tensor_copy(bk_high[:, :, :], bk_in[:, :, :]))
                    nc.vector.scalar_tensor_tensor(bk[:, :, :], bk_high[:, :, :], kb, bk_in[:, :, :],
                                                   ALU.mult, ALU.add).then_inc(bk_ready, 1)

                    def body(c, s):
                        dve.wait_ge(high_ready, c + 1)
                        dve.wait_ge(k_ready, c + 2)
                        for b in range(2):
                            nc.vector.scalar_tensor_tensor(flat(k_rest, s)[:, b, :], flat(k_high, s)[:, b, :],
                                                           const[:, C_KA:C_KA + 1], kbanks(s)[:, b, :],
                                                           ALU.mult, ALU.add).then_inc(rest_ready, 1)
                        dve.wait_ge(v_in_psum, c + 1)
                        dve.wait_ge(valid_in[s], (c - s) * 8 + 16)
                        dve.wait_ge(kv_written[s], (c - s) * 16 + 16)
                        nc.vector.scalar_tensor_tensor(vv[:, s, :, 0:DK],
                                                       bv[0:KC, :].rearrange("k (h d) -> k h d", d=DK),
                                                       valid[:, s, :],
                                                       ps[0:KC, 4 + s, 0:D].rearrange("k (h d) -> k h d", d=DK),
                                                       ALU.mult, ALU.add)
                        nc.vector.tensor_copy(vv[:, s, :, DK:DK + 1],
                                              valid[:, s, :].unsqueeze(1).broadcast_to([KC, H, 1])
                                              ).then_inc(v_ready, 1)
                        for b in range(2):
                            dve.wait_ge(mid_ready, c * 2 + (b + 1))
                            last = nc.vector.scalar_tensor_tensor(flat(k_out, s)[:, b, :], flat(k_mid, s)[:, b, :],
                                                                  const[:, C_KB:C_KB + 1], flat(k_rest, s)[:, b, :],
                                                                  ALU.mult, ALU.add)
                        last.then_inc(k_ready, 1)

                    each_chunk(dve, n, body)

            with ExitStack() as ph:
                k_first = sb("k_first", [P, NP, KC], BF16, ph)
                k_last = sb("k_last", [P, NP, KC], BF16, ph)
                v_last = sb("v_last", [KC, H, DK + 1], F32, ph)
                k_one = sb("k_one", [P, 2, NP, KC], BF16, ph)
                k_two = sb("k_two", [P, 2, NP, KC], BF16, ph)
                v_two = sb("v_two", [KC, 2, H, DK + 1], F32, ph)
                probs = sb("probs", [KC, 2, 4, QB], F32, ph)
                zeros = sb("zeros", [P, 512], BF16, ph)
                mx = sb("mx", [P, 2, H, QT], F32, ph)
                run_max = sb("run_max", [P, QT, H], F32, ph)
                neg_f = sb("neg_f", [H, QB], F32, ph)
                neg_r = sb("neg_r", [H, QB], F32, ph)
                neg_p = sb("neg_p", [H, 3, QB], BF16, ph)
                dve_own3, zeros_ready, ends_in, sp_passed = (sem(n) for n in ("dve_own3", "zeros_ready", "ends_in",
                                                                             "sp_passed"))
                max_t, max_rows_ready, max_rows_in = sem("max_t"), sem("max_rows_ready"), sem("max_rows_in")
                oacc_saved = sem("oacc_saved")
                stage_sems = []
                for s in range(NB + 1):
                    names = ["k_one_in0", "k_one_in1", "kv_two_in0", "kv_two_in1", "s1_ready", "s1_free", "mx_ready",
                             "s2_ready", "s2_free", "p_free"]
                    stage_sems.append({n: nc.alloc_semaphore(name=f"{n}_st{s}") for n in names})
                S1, S2, AC = 0, 4, 6
                S1_START, P_START = 6, 6
                block = ph.enter_context(nc.Block())

                def s2_banks(stage):
                    return 2 if stage < NB else 4

                def s2_bank(stage, i):
                    return S2 + i % 2 if stage < NB else i % 4


                @block.sync
                def _(sp):
                    n = sp.value_load(chunk_list[0:1, NCE:NCE + 1], min_val=1, max_val=NC)
                    m = sp.value_load(chunk_list[0:1, NCE + 1:NCE + 2], min_val=0, max_val=NC - 1)

                    def load_k(dst, c, z):
                        sp.dma_start(dst, k_dram[bass.ds(c, 1)].rearrange("c r p k -> (c r) p k")).then_inc(z, 16)

                    def load_v(dst, c, z):
                        sp.dma_start(dst, v_dram[bass.ds(c, 1)].rearrange("c k n -> (c k) n")).then_inc(z, 16)

                    load_k(k_first[:, :, :], 0, ends_in)
                    load_k(k_last[:, :, :], m, ends_in)
                    load_v(v_last[:, :, :].rearrange("k h d -> k (h d)"), m, ends_in)
                    for stage in range(NB + 1):
                        z = stage_sems[stage]
                        one, two = stage < NB, stage > 0
                        def body(c, s):
                            if one:
                                sp.wait_ge(z["s1_free"], c * 4 + S1_START)
                                sp.sem_inc(sp_passed, 1)
                                load_k(k_one[:, s, :, :], c + 1, z[f"k_one_in{s}"])
                            if two:
                                sp.wait_ge(z["p_free"], c * 4 + P_START - 4)
                                sp.sem_inc(sp_passed, 1)
                                load_k(k_two[:, s, :, :], c, z[f"kv_two_in{s}"])
                                load_v(v_two[:, s, :, :].rearrange("k h d -> k (h d)"), c, z[f"kv_two_in{s}"])

                        each_chunk(sp, m, body)
                        if one:
                            sp.wait_ge(max_rows_ready, stage + 1)
                            for j in range(3):
                                for half in range(2):
                                    r = ROWS * half + ROW_MAX + j
                                    sp.dma_start(q_all[r:r + 1, half, :, QB * stage:QB * stage + QB],
                                                 neg_p[NP * half:NP * half + NP, j, :]).then_inc(max_rows_in, 16)
                    sp.wait_ge(max_rows_in, NB * 96)

                @block.tensor
                def _(pe):
                    n = pe.value_load(chunk_list[0:1, NCE:NCE + 1], min_val=1, max_val=NC)
                    m = pe.value_load(chunk_list[0:1, NCE + 1:NCE + 2], min_val=0, max_val=NC - 1)
                    pe.wait_ge(zeros_ready, 1)
                    pe.wait_ge(ends_in, 48)
                    for stage in range(NB + 1):
                        z = stage_sems[stage]
                        one, two = stage < NB, stage > 0
                        q2 = QB * (stage - 1)

                        def scores_one(c, k_tile, g, stage=stage):
                            z, q1 = stage_sems[stage], QB * stage
                            pe.wait_ge(z["s1_free"], c * 4 + (g + S1_START - 1))
                            for j in range(4):
                                half, pair = head_of(g, j)
                                for qt in range(QT):
                                    q, col = q1 + P * qt, KC * (2 * (j % 2) + qt)
                                    last = nc.tensor.matmul(ps[:, S1 + 2 * (g % 2) + j // 2, col:col + KC],
                                                            q_all[:, half, pair, q:q + P], k_tile(pair),
                                                            start=True, stop=True)
                            last.then_inc(z["s1_ready"], 1)

                        def scores_two(c, k_tile, g):
                            for b in range(2):
                                pe.wait_ge(z["s2_free"], c * 8 + (2 * g + b + 1))
                                for j in range(2):
                                    half, pair = head_of(g, 2 * b + j)
                                    last = nc.tensor.matmul(ps[0:KC, s2_bank(stage, 2 * g + b), QB * j:QB * j + QB], k_tile(pair),
                                                            q_all[:, half, pair, q2:q2 + QB], start=True, stop=True)
                                last.then_inc(z["s2_ready"], 1)

                        def values(c, v_tile, g):
                            pe.wait_ge(z["s2_free"], c * 8 + (2 * g + 2 + s2_banks(stage)))
                            for j in range(4):
                                last = nc.tensor.matmul(
                                    ps[32 * j:32 * j + DK + 1, AC + g // 2, QB * (g % 2):QB * (g % 2) + QB],
                                    v_tile(4 * g + j), probs[:, g % 2, j, :], start=False, stop=True,
                                    skip_group_check=True, tile_position=(0, 32 * j))
                            last.then_inc(z["p_free"], 1)

                        def first(pair):
                            return k_first[:, pair, :]

                        def last_k(pair):
                            return k_last[:, pair, :]

                        if stage == 0:
                            for g in range(NG):
                                scores_one(0, first, g)
                        if two:
                            if stage > 1:
                                pe.wait_ge(oacc_saved, stage - 1)
                            for b in range(2):
                                nc.tensor.matmul(ps[:, AC + b, :], zeros[:, 0:P], zeros[:, :], start=True, stop=True)
                            pe.wait_ge(max_rows_in, 96 * stage)

                        def body(c, s):
                            def k1(pair):
                                return k_one[:, s, pair, :]

                            def k2(pair):
                                return k_two[:, s, pair, :]

                            def v2(head):
                                return v_two[:, s, head, :]

                            if two:
                                pe.wait_ge(z[f"kv_two_in{s}"], (c - s) * 16 + 32)
                            for g in range(NG):
                                if two:
                                    scores_two(c, k2, g)
                                    if g:
                                        values(c, v2, g - 1)
                                if one:
                                    if g == 0:
                                        pe.wait_ge(z[f"k_one_in{s}"], (c - s) * 8 + 16)
                                    scores_one(c + 1, k1, g)
                            if two:
                                values(c, v2, NG - 1)

                        each_chunk(pe, m, body)
                        if one:
                            pe.wait_ge(z["mx_ready"], n + 1)
                            for qt in range(QT):
                                last = nc.tensor.transpose(ps[0:H, S1, P * qt:P * qt + P], run_max[:, qt, :], ident)
                            last.then_inc(max_t, 1)
                        for g in range(NG + 1):
                            if two and g < NG:
                                scores_two(m, last_k, g)
                            if two and g:
                                values(m, lambda head: v_last[:, head, :], g - 1)
                            if stage + 1 < NB and g < NG:
                                scores_one(0, first, g, stage + 1)

                @block.scalar
                def _(act):
                    n = act.value_load(chunk_list[0:1, NCE:NCE + 1], min_val=1, max_val=NC)
                    m = act.value_load(chunk_list[0:1, NCE + 1:NCE + 2], min_val=0, max_val=NC - 1)
                    act.sem_inc(stage_sems[1]["s2_free"], s2_banks(1))
                    act.sem_inc(stage_sems[1]["p_free"], P_START)
                    for stage in range(1, NB + 1):
                        z = stage_sems[stage]

                        def body(c, s):
                            for g in range(NG):
                                act.wait_ge(z["p_free"], c * 4 + (g + P_START - 1))
                                for b in range(2):
                                    act.wait_ge(z["s2_ready"], c * 8 + (2 * g + b + 1))
                                    nc.scalar.activation(
                                        probs[:, g % 2, 2 * b:2 * b + 2, :].rearrange("k h q -> k (h q)"),
                                        ps[0:KC, s2_bank(stage, 2 * g + b), :], ACT.Exp).then_inc(z["s2_free"], 1)

                        each_chunk(act, m, body)
                        if stage < NB:
                            act.wait_ge(z["p_free"], m * 4 + P_START)
                            act.sem_inc(stage_sems[stage + 1]["p_free"], P_START)
                        body(m, 0)
                        act.wait_ge(z["p_free"], n * 4 + P_START)
                        if stage < NB:
                            act.sem_inc(stage_sems[stage + 1]["s2_free"], s2_banks(stage + 1))
                        nc.scalar.copy(oacc[:, stage - 1, :, :].rearrange("p (b g) q -> p b (g q)", b=2),
                                       ps[:, AC:AC + 2, :]).then_inc(oacc_saved, 1)

                @block.vector
                def _(dve):
                    own = Chain(dve, dve_own3)
                    n = dve.value_load(chunk_list[0:1, NCE:NCE + 1], min_val=1, max_val=NC)
                    m = dve.value_load(chunk_list[0:1, NCE + 1:NCE + 2], min_val=0, max_val=NC - 1)
                    nc.vector.memset(zeros[:, :], 0.0).then_inc(zeros_ready, 1)

                    def open_stage(stage):
                        own(nc.vector.memset(run_max[:, :, :], -3.0e38))
                        dve.sem_inc(stage_sems[stage]["mx_ready"], 1)
                        dve.sem_inc(stage_sems[stage]["s1_free"], S1_START)

                    open_stage(0)
                    for stage in range(NB):
                        z = stage_sems[stage]

                        def reduce(c, s):
                            for g in range(NG):
                                dve.wait_ge(z["s1_ready"], c * 4 + (g + 1))
                                b = S1 + 2 * (g % 2)
                                nc.vector.tensor_reduce(
                                    mx[:, s, 4 * g:4 * g + 4, :].rearrange("p h t -> p (h t)"),
                                    ps[:, b:b + 2, 0:4 * KC].rearrange("p b (n k) -> p b n k", k=KC),
                                    X, ALU.max).then_inc(z["s1_free"], 1)
                            dve.wait_ge(z["s1_free"], c * 4 + (4 + S1_START))
                            dve.wait_ge(z["mx_ready"], c + 1)
                            nc.vector.tensor_tensor(run_max[:, :, :], run_max[:, :, :],
                                                    mx[:, s, :, :].rearrange("p h t -> p t h"), ALU.max
                                                    ).then_inc(z["mx_ready"], 1)

                        reduce(0, 1)
                        each_chunk(dve, m, lambda c, s: reduce(c + 1, s))
                        dve.wait_ge(max_t, stage + 1)
                        if stage:
                            dve.wait_ge(max_rows_in, 96 * stage)
                        own(nc.vector.tensor_scalar(neg_f[:, :], ps[0:H, S1, 0:QB], -1.0, None, ALU.mult))
                        if stage + 1 < NB:
                            open_stage(stage + 1)
                        own(nc.vector.tensor_copy(neg_p[:, 0, :], neg_f[:, :]))
                        own(nc.vector.tensor_tensor(neg_r[:, :], neg_f[:, :], neg_p[:, 0, :], ALU.subtract))
                        own(nc.vector.tensor_copy(neg_p[:, 1, :], neg_r[:, :]))
                        nc.vector.tensor_tensor(neg_p[:, 2, :], neg_r[:, :], neg_p[:, 1, :], ALU.subtract
                                                ).then_inc(max_rows_ready, 1)

            nc.clear_and_free_semaphores([z for stage in stage_sems for z in stage.values()])
            nc.all_engine_barrier()

            with ExitStack() as ph:
                attn = sb("attn", [P, NT, D], F32, ph)
                attn_t = sb("attn_t", [P, S], F32, ph)
                recip = sb("recip", [P, 2, H], F32, ph)
                biased = sb("biased", [P, NT, D], F32, ph)
                heads_t, heads_free, attn_ready, at_in_psum, at_ready, y_in_psum, rec_ready = (
                    sem(n) for n in ("heads_t", "heads_free", "attn_ready", "at_in_psum", "at_ready",
                                     "y_in_psum", "rec_ready"))
                dve_own4 = sem("dve_own4")
                block = ph.enter_context(nc.Block())

                @block.tensor
                def _(pe):
                    for t in range(NT):
                        if t >= 2:
                            pe.wait_ge(heads_free, t - 1)
                        for g in range(NG):
                            last = nc.tensor.transpose(ps[:, t % 2, P * g:P * g + P],
                                                       oacc[:, t // QT, g, P * (t % QT):P * (t % QT) + P], ident)
                        last.then_inc(heads_t, 1)
                        if t:
                            pe.wait_ge(heads_free, t)
                            nc.tensor.transpose(ps[:, 2 + (t - 1) // 4, P * ((t - 1) % 4):P * ((t - 1) % 4) + P],
                                                attn[:, t - 1, :], ident).then_inc(at_in_psum, 1)
                    pe.wait_ge(heads_free, NT)
                    nc.tensor.transpose(ps[:, 3, 3 * P:4 * P], attn[:, NT - 1, :], ident).then_inc(at_in_psum, 1)
                    for n in range(2):
                        pe.wait_ge(at_ready, n + 1)
                        for t in range(4):
                            last = nc.tensor.matmul(ps[:, 4 + n, P * t:P * t + P],
                                                    attn_t[:, P * (4 * n + t):P * (4 * n + t) + P], wo[:, :],
                                                    start=True, stop=True)
                        last.then_inc(y_in_psum, 1)

                @block.vector
                def _(dve):
                    own = Chain(dve, dve_own4)
                    for t in range(NT):
                        dve.wait_ge(heads_t, t + 1)
                        v = ps[:, t % 2, :].rearrange("p (h c) -> p h c", c=32)
                        nc.vector.reciprocal(recip[:, t % 2, :], v[:, :, DK]).then_inc(rec_ready, 1)
                        dve.wait_ge(rec_ready, t + 1)
                        nc.vector.tensor_tensor(attn[:, t, :].rearrange("p (h d) -> p h d", d=DK), v[:, :, 0:DK],
                                                recip[:, t % 2, :].unsqueeze(2).broadcast_to([P, H, DK]),
                                                ALU.mult).then_inc(heads_free, 1)
                    for n in range(2):
                        dve.wait_ge(at_in_psum, 4 * n + 4)
                        nc.vector.tensor_copy(attn_t[:, 512 * n:512 * n + 512], ps[:, 2 + n, :]).then_inc(at_ready, 1)
                    for n in range(2):
                        r = slice(4 * n, 4 * n + 4)
                        dve.wait_ge(y_in_psum, n + 1)
                        own(nc.vector.tensor_tensor(biased[:, r, :], ps[:, 4 + n, :].rearrange("p (t d) -> p t d", d=D),
                                                    bo[:, :].unsqueeze(1).broadcast_to([P, 4, D]), ALU.add))
                        own(nc.vector.scalar_tensor_tensor(
                            x1[:, r, :].rearrange("p t d -> p (t d)"), biased[:, r, :].rearrange("p t d -> p (t d)"),
                            tanhs[:, 0:1], x0[:, r, :].rearrange("p t d -> p (t d)"), ALU.mult, ALU.add))

        x2 = sb("x2", [P, NT, D])
        hT = sb("hT", [P, S])
        x3 = sb("x3", [P, NT, D])
        comb = sb("comb", [P, NT, NE])
        with ExitStack() as win:
            y_sb = sb("y_sb", [P, NT, HF * DH], F32, win)
            with ExitStack() as att:
                q_rot = sb("q_rot", [P, HF, S], F32, att)
                k_rot = sb("k_rot", [P, KV, S], F32, att)
                v_tok = sb("v_tok", [P, NT, KV * DH], F32, att)

                with ExitStack() as ph:
                    h = sb("h", [P, NT, D], F32, ph)
                    norm_w = sb("norm_w", [P, D], F32, ph)
                    wqk = sb("wqk", [P, HF + KV, P], F32, ph)
                    bqk = sb("bqk", [P, HF + KV], F32, ph)
                    wvv = sb("wvv", [P, KV * DH], F32, ph)
                    bvv = sb("bvv", [P, KV * DH], F32, ph)
                    cs = sb("cs", [P, S], F32, ph)
                    k_cs = sb("k_cs", [P, KV, S], F32, ph)
                    in5, cs_in, dve_own5, var5, root5, h_ready, ht_psum, ht_ready = (
                        sem(n) for n in ("in5", "cs_in", "dve_own5", "var5", "root5", "h_ready", "ht_psum", "ht_ready"))
                    v_psum, v_free, qk_psum, qk_free, ks_psum, ks_free = (
                        sem(n) for n in ("v_psum", "v_free", "qk_psum", "qk_free", "ks_psum", "ks_free"))
                    block = ph.enter_context(nc.Block())

                    @block.sync
                    def _(sp):
                        sp.dma_start(norm_w[:, :], a["attn_norm_w"].partition_broadcast(P)).then_inc(in5, 16)
                        sp.dma_start(wqk[:, :, :], a["wqk"]).then_inc(cs_in, 16)
                        sp.dma_start(bqk[:, :], a["bqk"]).then_inc(cs_in, 16)
                        sp.dma_start(wvv[:, :], a["wvv"]).then_inc(cs_in, 16)
                        sp.dma_start(bvv[:, :], a["bvv"].partition_broadcast(P)).then_inc(cs_in, 16)
                        sp.dma_start(cs[:, :], a["cs"]).then_inc(cs_in, 16)

                    @block.scalar
                    def _(act):
                        for n in range(2):
                            act.wait_ge(var5, n + 1)
                            nc.scalar.activation(st[:, 3, :], st[:, 2, :], ACT.Sqrt).then_inc(root5, 1)
                        for n in range(2):
                            act.wait_ge(ht_psum, n + 1)
                            nc.scalar.copy(hT[:, 512 * n:512 * n + 512], ps[:, n, :]).then_inc(ht_ready, 1)
                        for kv in range(KV):
                            for n in range(2):
                                act.wait_ge(ks_psum, 2 * kv + n + 1)
                                nc.scalar.copy(k_rot[:, kv, 512 * n:512 * n + 512], ps[:, n, :]).then_inc(ks_free, 1)

                    @block.vector
                    def _(dve):
                        own = Chain(dve, dve_own5)
                        normalise(own, (root5, 1), None, var5, x1, x2, True)
                        normalise(own, (root5, 2), None, var5, x2, h, False)
                        dve.wait_ge(in5, 16)
                        nc.vector.tensor_tensor(h[:, :, :], h[:, :, :],
                                                norm_w[:, :].unsqueeze(1).broadcast_to([P, NT, D]), ALU.mult
                                                ).then_inc(h_ready, 1)
                        dve.wait_ge(cs_in, 80)
                        for m in range(NT // 2):
                            dve.wait_ge(v_psum, m + 1)
                            nc.vector.tensor_tensor(v_tok[:, 2 * m:2 * m + 2, :],
                                                    ps[:, 2 + m % 2, :].rearrange("p (t d) -> p t d", t=2),
                                                    bvv[:, :].unsqueeze(1).broadcast_to([P, 2, KV * DH]), ALU.add
                                                    ).then_inc(v_free, 1)
                        for m in range(HF + KV):
                            f = HF + m if m < KV else m - KV
                            dst = k_cs[:, m, :] if m < KV else q_rot[:, f, :]
                            for n in range(2):
                                u = 2 * m + n
                                dve.wait_ge(qk_psum, u + 1)
                                nc.vector.scalar_tensor_tensor(dst[:, 512 * n:512 * n + 512], ps[:, 4 + u % 4, :],
                                                               bqk[:, f:f + 1], cs[:, 512 * n:512 * n + 512],
                                                               ALU.add, ALU.mult).then_inc(qk_free, 1)

                    @block.tensor
                    def _(pe):
                        pe.wait_ge(h_ready, 1)
                        for t in range(NT):
                            last = nc.tensor.transpose(ps[:, t // 4, P * (t % 4):P * (t % 4) + P], h[:, t, :], ident)
                            if t % 4 == 3:
                                last.then_inc(ht_psum, 1)
                        pe.wait_ge(cs_in, 80)
                        pe.wait_ge(ht_ready, 2)
                        for m in range(NT // 2):
                            if m >= 2:
                                pe.wait_ge(v_free, m - 1)
                            for t in (2 * m, 2 * m + 1):
                                last = nc.tensor.matmul(ps[:, 2 + m % 2, 256 * (t % 2):256 * (t % 2) + 256],
                                                        hT[:, P * t:P * t + P], wvv[:, :], start=True, stop=True)
                            last.then_inc(v_psum, 1)
                        for m in range(HF + KV):
                            f = HF + m if m < KV else m - KV
                            for n in range(2):
                                u = 2 * m + n
                                if u >= 4:
                                    pe.wait_ge(qk_free, u - 3)
                                nc.tensor.matmul(ps[:, 4 + u % 4, :], wqk[:, f, :], hT[:, 512 * n:512 * n + 512],
                                                 start=True, stop=True).then_inc(qk_psum, 1)
                            if 2 <= m < 2 + KV:
                                for n in range(2):
                                    u = 2 * (m - 2) + n
                                    pe.wait_ge(qk_free, u + 1)
                                    if u >= 2:
                                        pe.wait_ge(ks_free, u - 1)
                                    nc.tensor.matmul(ps[:, n, :], const[:, C_SUM:C_SUM + P],
                                                     k_cs[:, m - 2, 512 * n:512 * n + 512], start=True, stop=True
                                                     ).then_inc(ks_psum, 1)

                with ExitStack() as ph:
                    band = sb("band", [P, 2, 2, 2, P], BF16, ph)
                    identb = sb("identb", [P, P], BF16, ph)
                    sinks = sb("sinks", [P, HF], F32, ph)
                    neg_sinks = sb("neg_sinks", [P, HF], F32, ph)
                    neg4 = sb("neg4", [P, 4], F32, ph)
                    neg_m = sb("neg_m", [P, NT, HF], F32, ph)
                    sums = sb("sums", [P, NT, HF], F32, ph)
                    sink_w = sb("sink_w", [P, 2, HF], F32, ph)
                    pw = sb("pw", [P, 2, 4, 2 * P], F32, ph)
                    pt = sb("pt", [P, 2, 4, 2, P], F32, ph)
                    sink_in, band_ready, dve_own6, s_ready, m_ready, p_ready, t_ready, pt_ready, y_ready, y_free = (
                        sem(n) for n in ("sink_in", "band_ready", "dve_own6", "s_ready", "m_ready", "p_ready",
                                         "t_ready", "pt_ready", "y_ready", "y_free"))
                    red, sink_arg, sink_exp = sem("red"), sem("sink_arg"), sem("sink_exp")
                    block = ph.enter_context(nc.Block())
                    UNITS = NT * KV

                    @block.sync
                    def _(sp):
                        sp.dma_start(sinks[:, :], a["sink"].partition_broadcast(P)).then_inc(sink_in, 16)

                    @block.tensor
                    def _(pe):
                        pe.wait_ge(band_ready, 1)
                        for m in range(UNITS + 2):
                            if m < UNITS:
                                t, g = divmod(m, KV)
                                if m >= 2:
                                    pe.wait_ge(p_ready, m - 1)
                                for b in range(2):
                                    bank = ps[:, 2 * (m % 2) + b, :]
                                    nc.tensor.matmul(bank, identb[:, :],
                                                     band[:, min(t, 1), :, :, :].rearrange("p h k c -> p (h k c)"),
                                                     start=True, stop=False)
                                    for j in range(2):
                                        head = 4 * g + 2 * b + j
                                        c0 = 256 * j + (0 if t else P)
                                        last = nc.tensor.matmul(ps[:, 2 * (m % 2) + b, c0:256 * j + 256],
                                                                q_rot[:, head, P * t:P * t + P],
                                                                k_rot[:, g, P * max(t - 1, 0):P * t + P],
                                                                start=False, stop=j == 1)
                                last.then_inc(s_ready, 1)
                            if 1 <= m <= UNITS:
                                k = m - 1
                                pe.wait_ge(p_ready, k + 1)
                                if k:
                                    pe.wait_ge(pt_ready, k)
                                for j in range(4):
                                    for kt in range(2):
                                        c = 256 * (j % 2) + P * kt
                                        last = nc.tensor.transpose(ps[:, 4 + j // 2, c:c + P],
                                                                   pw[:, k % 2, j, P * kt:P * kt + P], ident)
                                last.then_inc(t_ready, 1)
                            if m >= 2:
                                k = m - 2
                                t, g = divmod(k, KV)
                                pe.wait_ge(pt_ready, k + 1)
                                if g == 0 and t:
                                    pe.wait_ge(y_free, t)
                                for j in range(4):
                                    head = 4 * g + j
                                    for kt in range(0 if t else 1, 2):
                                        last = nc.tensor.matmul(ps[:, 6 + head // 8, DH * (head % 8):DH * (head % 8) + DH],
                                                                pt[:, k % 2, j, kt, :],
                                                                v_tok[:, t - 1 + kt, DH * g:DH * g + DH],
                                                                start=kt == (0 if t else 1), stop=kt == 1)
                                if g == KV - 1:
                                    last.then_inc(y_ready, 1)

                    @block.scalar
                    def _(act):
                        for m in range(UNITS):
                            t, g = divmod(m, KV)
                            act.wait_ge(m_ready, m + 1)
                            if m >= 2:
                                act.wait_ge(t_ready, m - 1)
                            for j in range(4):
                                last = nc.scalar.activation(pw[:, m % 2, j, :],
                                                            ps[:, 2 * (m % 2) + j // 2, 256 * (j % 2):256 * (j % 2) + 256],
                                                            ACT.Exp, bias=neg_m[:, t, 4 * g + j:4 * g + j + 1],
                                                            accum_out=sums[:, t, 4 * g + j:4 * g + j + 1])
                            last.then_inc(p_ready, 1)
                            if g == KV - 1:
                                act.wait_ge(sink_arg, t + 1)
                                nc.scalar.activation(sink_w[:, t % 2, :], sink_w[:, t % 2, :], ACT.Exp
                                                     ).then_inc(sink_exp, 1)

                    @block.vector
                    def _(dve):
                        own = Chain(dve, dve_own6)
                        own(nc.vector.tensor_copy(identb[:, :], ident))
                        for first in range(2):
                            for j in range(2):
                                own(nc.vector.tensor_copy(band[:, first, j, :, :].rearrange("p k c -> p (k c)"),
                                                          const[:, C_BAND:C_BAND + 256]))
                        for j in range(2):
                            own(nc.vector.memset(band[:, 0, j, 0, :], NEG))
                        nc.vector.engine_nop().then_inc(band_ready, 1)
                        dve.wait_ge(sink_in, 16)
                        own(nc.vector.tensor_scalar(neg_sinks[:, :], sinks[:, :], -1.0, None, ALU.mult))
                        for m in range(UNITS + 2):
                            if m < UNITS:
                                t, g = divmod(m, KV)
                                dve.wait_ge(s_ready, m + 1)
                                own(nc.vector.tensor_reduce(
                                    neg4[:, :], ps[:, 2 * (m % 2):2 * (m % 2) + 2, :].rearrange("p b (j c) -> p b j c", j=2),
                                    X, ALU.max, negate=True))
                                nc.vector.tensor_tensor(neg_m[:, t, 4 * g:4 * g + 4], neg4[:, :],
                                                        neg_sinks[:, 4 * g:4 * g + 4], ALU.min).then_inc(m_ready, 1)
                                dve.wait_ge(m_ready, m + 1)
                                if g == KV - 1:
                                    nc.vector.tensor_tensor(sink_w[:, t % 2, :], sinks[:, :], neg_m[:, t, :], ALU.add
                                                            ).then_inc(sink_arg, 1)
                            if 1 <= m <= UNITS:
                                k = m - 1
                                dve.wait_ge(t_ready, k + 1)
                                nc.vector.tensor_copy(pt[:, k % 2, :, :, :].rearrange("p j k c -> p (j k c)"),
                                                      ps[:, 4:6, :].rearrange("p b c -> p (b c)")).then_inc(pt_ready, 1)
                            if m >= 2 and (m - 2) % KV == KV - 1:
                                t = (m - 2) // KV
                                dve.wait_ge(y_ready, t + 1)
                                dve.wait_ge(sink_exp, t + 1)
                                own(nc.vector.tensor_tensor(sums[:, t, :], sums[:, t, :], sink_w[:, t % 2, :], ALU.add))
                                own(nc.vector.reciprocal(sums[:, t, :], sums[:, t, :]))
                                nc.vector.tensor_tensor(y_sb[:, t, :].rearrange("p (h d) -> p h d", d=DH),
                                                        ps[:, 6:8, :].rearrange("p b (h d) -> p (b h) d", d=DH),
                                                        sums[:, t, :].unsqueeze(2).broadcast_to([P, HF, DH]), ALU.mult
                                                        ).then_inc(y_free, 1)

            with ExitStack() as ph:
                wp = sb("wp", [P, HF * DH // P, D], F32, ph)
                bp = sb("bp", [P, D], F32, ph)
                norm2 = sb("norm2", [P, D], F32, ph)
                wg = sb("wg", [P, NE], F32, ph)
                bg = sb("bg", [P, NE], F32, ph)
                h2 = sb("h2", [P, NT, D], F32, ph)
                y_t = sb("y_t", [P, 2, 8, P], F32, ph)
                gl = sb("gl", [P, NT, NE], F32, ph)
                top = sb("top", [P, NT, 8], F32, ph)
                topi = sb("topi", [P, NT, 8], U32, ph)
                topf = sb("topf", [P, NT, 8], F32, ph)
                ew = sb("ew", [P, NT, TOPK], F32, ph)
                esum = sb("esum", [P, 2, NT], F32, ph)
                eq = sb("eq", [P, NT, NE], F32, ph)
                in7, dve_own7, var7, root7, h2_ready, yt_psum, yt_ready, pr_psum, h2t_psum, h2t_ready, gl_psum = (
                    sem(n) for n in ("in7", "dve_own7", "var7", "root7", "h2_ready", "yt_psum", "yt_ready", "pr_psum",
                                     "h2t_psum", "h2t_ready", "gl_psum"))
                ew_arg, ew_exp = sem("ew_arg"), sem("ew_exp")
                block = ph.enter_context(nc.Block())

                @block.sync
                def _(sp):
                    sp.dma_start(wp[:, :, :], a["proj_w"].rearrange("(f p) d -> p f d", p=P)).then_inc(in7, 16)
                    sp.dma_start(bp[:, :], a["proj_b"].partition_broadcast(P)).then_inc(in7, 16)
                    sp.dma_start(norm2[:, :], a["ffn_norm_w"].partition_broadcast(P)).then_inc(in7, 16)
                    sp.dma_start(wg[:, :], a["gate_w"]).then_inc(in7, 16)
                    sp.dma_start(bg[:, :], a["gate_b"].partition_broadcast(P)).then_inc(in7, 16)

                @block.tensor
                def _(pe):
                    pe.wait_ge(in7, 80)
                    for t in range(NT + 1):
                        if t < NT:
                            for f in range(8):
                                b = 2 * (t % 2) + f // 4
                                last = nc.tensor.transpose(ps[:, b, P * (f % 4):P * (f % 4) + P],
                                                           y_sb[:, t, P * f:P * f + P], ident)
                                if f % 4 == 3:
                                    last.then_inc(yt_psum, 1)
                        if t:
                            k = t - 1
                            pe.wait_ge(yt_ready, 2 * k + 2)
                            for f in range(8):
                                last = nc.tensor.matmul(ps[:, 4 + k // 4, P * (k % 4):P * (k % 4) + P],
                                                        y_t[:, k % 2, f, :], wp[:, f, :], start=f == 0, stop=f == 7)
                            last.then_inc(pr_psum, 1)
                    pe.wait_ge(h2_ready, 1)
                    for t in range(NT):
                        last = nc.tensor.transpose(ps[:, t // 4, P * (t % 4):P * (t % 4) + P], h2[:, t, :], ident)
                        if t % 4 == 3:
                            last.then_inc(h2t_psum, 1)
                    for t in range(NT):
                        pe.wait_ge(h2t_ready, t // 4 + 1)
                        last = nc.tensor.matmul(ps[:, 6, NE * t:NE * t + NE], hT[:, P * t:P * t + P], wg[:, :],
                                                start=True, stop=True)
                    last.then_inc(gl_psum, 1)

                @block.scalar
                def _(act):
                    for t in range(NT):
                        for b in range(2):
                            act.wait_ge(yt_psum, 2 * t + b + 1)
                            if t >= 2:
                                act.wait_ge(pr_psum, t - 1)
                            nc.scalar.copy(y_t[:, t % 2, 4 * b:4 * b + 4, :].rearrange("p f c -> p (f c)"),
                                           ps[:, 2 * (t % 2) + b, :]).then_inc(yt_ready, 1)
                    act.wait_ge(var7, 1)
                    nc.scalar.activation(st[:, 3, :], st[:, 2, :], ACT.Sqrt).then_inc(root7, 1)
                    for n in range(2):
                        act.wait_ge(h2t_psum, n + 1)
                        nc.scalar.copy(hT[:, 512 * n:512 * n + 512], ps[:, n, :]).then_inc(h2t_ready, 1)
                    act.wait_ge(ew_arg, 1)
                    nc.scalar.activation(ew[:, :, :], ew[:, :, :], ACT.Exp).then_inc(ew_exp, 1)

                @block.vector
                def _(dve):
                    own = Chain(dve, dve_own7)
                    dve.wait_ge(in7, 80)
                    for n in range(2):
                        r = slice(4 * n, 4 * n + 4)
                        own(nc.vector.tensor_tensor(x3[:, r, :], x2[:, r, :],
                                                    bp[:, :].unsqueeze(1).broadcast_to([P, 4, D]), ALU.add))
                        dve.wait_ge(pr_psum, 4 * n + 4)
                        own(nc.vector.tensor_tensor(x3[:, r, :], ps[:, 4 + n, :].rearrange("p (t d) -> p t d", d=D),
                                                    x3[:, r, :], ALU.add))
                    normalise(own, (root7, 1), None, var7, x3, h2, False)
                    nc.vector.tensor_tensor(h2[:, :, :], h2[:, :, :],
                                            norm2[:, :].unsqueeze(1).broadcast_to([P, NT, D]), ALU.mult
                                            ).then_inc(h2_ready, 1)
                    dve.wait_ge(gl_psum, 1)
                    own(nc.vector.tensor_tensor(gl[:, :, :], ps[:, 6, 0:NT * NE].rearrange("p (t e) -> p t e", e=NE),
                                                bg[:, :].unsqueeze(1).broadcast_to([P, NT, NE]), ALU.add))
                    for t in range(NT):
                        own(nc.vector.max(top[:, t, :], gl[:, t, :]))
                        own(nc.vector.max_index(topi[:, t, :], top[:, t, :], gl[:, t, :]))
                    own(nc.vector.tensor_copy(topf[:, :, :], topi[:, :, :]))
                    nc.vector.tensor_tensor(ew[:, :, :], top[:, :, 0:TOPK], top[:, :, 0:1].broadcast_to([P, NT, TOPK]),
                                            ALU.subtract).then_inc(ew_arg, 1)
                    dve.wait_ge(ew_exp, 1)
                    own(nc.vector.tensor_reduce(esum[:, 0, :], ew[:, :, :], X, ALU.add))
                    own(nc.vector.reciprocal(esum[:, 1, :], esum[:, 0, :]))
                    own(nc.vector.tensor_tensor(ew[:, :, :], ew[:, :, :],
                                                esum[:, 1, :].unsqueeze(2).broadcast_to([P, NT, TOPK]), ALU.mult))
                    eio = const[:, C_EIOTA:C_EIOTA + NE].unsqueeze(1).broadcast_to([P, NT, NE])
                    for j in range(TOPK):
                        dst = comb if j == 0 else eq
                        own(nc.vector.tensor_tensor(dst[:, :, :], eio, topf[:, :, j:j + 1].broadcast_to([P, NT, NE]),
                                                    ALU.is_equal))
                        own(nc.vector.tensor_tensor(dst[:, :, :], dst[:, :, :],
                                                    ew[:, :, j:j + 1].broadcast_to([P, NT, NE]), ALU.mult))
                        if j:
                            own(nc.vector.tensor_tensor(comb[:, :, :], comb[:, :, :], eq[:, :, :], ALU.add))

        with ExitStack() as ph:
            w_up = sb("w_up", [P, 2, 2 * FF], F32, ph)
            w_down = sb("w_down", [P, 2, D], F32, ph)
            silu = sb("silu", [P, 2, 512], F32, ph)
            act_t = sb("act_t", [P, 2, 512], F32, ph)
            part = sb("part", [P, 2, 4, D], F32, ph)
            acc = sb("acc", [P, NT, D], F32, ph)
            w_in = [sem(f"expert_in{n}") for n in range(2)]
            gu_ready, silu_ready, gated, d_ready, d_free, part_free, acc_zero, dve_own8, o_ready, o_out = (
                sem(n) for n in ("gu_ready", "silu_ready", "gated", "d_ready", "d_free", "part_free",
                                 "acc_zero", "dve_own8", "o_ready", "o_out"))
            block = ph.enter_context(nc.Block())
            sp_passed8 = sem("sp_passed8")
            NU = 2 * NE
            G0, U0, D0 = 0, 2, 4

            def turns(eng, body):
                with eng.Fori(0, NE // 2 - 1) as turn:
                    body(turn * 2, False)
                body(NE - 2, True)

            @block.sync
            def _(sp):
                def load(e, s):
                    up = a["W_up"][bass.ds(e, 1)].rearrange("e p n -> (e p) n")
                    down = a["W_down"][bass.ds(e, 1)].rearrange("e p n -> (e p) n")
                    sp.dma_start(w_up[:, s, :], up).then_inc(w_in[s], 16)
                    sp.dma_start(w_down[:, s, :], down).then_inc(w_in[s], 16)

                for s in range(2):
                    load(s, s)

                def body(e, last):
                    if not last:
                        for s in range(2):
                            sp.wait_ge(d_ready, 2 * e + 2 * s + 2)
                            sp.sem_inc(sp_passed8, 1)
                            load(e + 2 + s, s)

                turns(sp, body)
                sp.wait_ge(o_ready, 1)
                sp.dma_start(out.rearrange("b (t p) d -> p (b t) d", p=P), x1[:, :, :]).then_inc(o_out, 16)
                sp.wait_ge(o_out, 16)

            @block.tensor
            def _(pe):
                def up(e, k):
                    s, n = k // 2 % 2, k % 2
                    if n == 0:
                        pe.wait_ge(w_in[s], 16 * (e + k // 2 - s) + 32)
                    pe.wait_ge(gated, 2 * e + k + 1)
                    r = slice(512 * n, 512 * n + 512)
                    nc.tensor.matmul(ps[:, G0 + n, :], w_up[:, s, FF:2 * FF], hT[:, r], start=True, stop=True)
                    nc.tensor.matmul(ps[:, U0 + n, :], w_up[:, s, 0:FF], hT[:, r], start=True, stop=True
                                     ).then_inc(gu_ready, 1)

                def down(e, k):
                    s, n = k // 2, k % 2
                    pe.wait_ge(gated, 2 * e + k + 3)
                    pe.wait_ge(d_free, 2 * e + k + 1)
                    for t in range(4):
                        last = nc.tensor.matmul(ps[:, D0 + n, P * t:P * t + P], act_t[:, n, P * t:P * t + P],
                                                w_down[:, s, :], start=True, stop=True)
                    last.then_inc(d_ready, 1)

                up(0, 0)

                def body(e, last):
                    for k in range(4):
                        if not (last and k == 3):
                            up(e, k + 1)
                        down(e, k)

                turns(pe, body)

            @block.scalar
            def _(act):
                def body(e, last):
                    for k in range(4):
                        act.wait_ge(gu_ready, 2 * e + k + 1)
                        act.wait_ge(gated, 2 * e + k + 1)
                        nc.scalar.activation(silu[:, k % 2, :], ps[:, G0 + k % 2, :], ACT.Silu).then_inc(silu_ready, 1)

                turns(act, body)

            @block.vector
            def _(dve):
                own = Chain(dve, dve_own8)
                dve.sem_inc(gated, 2)
                dve.sem_inc(d_free, 2)

                def gate(e, k):
                    dve.wait_ge(silu_ready, 2 * e + k + 1)
                    nc.vector.tensor_tensor(act_t[:, k % 2, :], silu[:, k % 2, :], ps[:, U0 + k % 2, :], ALU.mult
                                            ).then_inc(gated, 1)

                def weighted(e, k):
                    n = k % 2
                    dve.wait_ge(d_ready, 2 * e + k + 1)
                    dve.wait_ge(part_free, 2 * e + k + 1)
                    weight = comb[:, 4 * n:4 * n + 4, bass.ds(e + k // 2, 1)]
                    nc.vector.tensor_tensor(part[:, n, :, :], ps[:, D0 + n, :].rearrange("p (t d) -> p t d", d=D),
                                            weight.broadcast_to([P, 4, D]), ALU.mult).then_inc(d_free, 1)

                gate(0, 0)

                def body(e, last):
                    for k in range(4):
                        if not (last and k == 3):
                            gate(e, k + 1)
                        weighted(e, k)

                turns(dve, body)
                dve.wait_ge(part_free, NU + 2)
                own(nc.vector.tensor_tensor(x3[:, :, :], x3[:, :, :], acc[:, :, :], ALU.add))
                own(nc.vector.scalar_tensor_tensor(x1[:, :, :].rearrange("p t d -> p (t d)"),
                                                   x3[:, :, :].rearrange("p t d -> p (t d)"), tanhs[:, 1:2],
                                                   x1[:, :, :].rearrange("p t d -> p (t d)"), ALU.mult, ALU.add))
                nc.vector.engine_nop().then_inc(o_ready, 1)

            @block.gpsimd
            def _(pool):
                nc.gpsimd.memset(acc[:, :, :], 0.0).then_inc(acc_zero, 1)
                pool.sem_inc(part_free, 2)
                pool.wait_ge(acc_zero, 1)

                def body(e, last):
                    for k in range(4):
                        n = k % 2
                        pool.wait_ge(d_free, 2 * e + k + 3)
                        pool.wait_ge(part_free, 2 * e + k + 1)
                        nc.gpsimd.tensor_tensor(acc[:, 4 * n:4 * n + 4, :], acc[:, 4 * n:4 * n + 4, :],
                                                part[:, n, :, :], ALU.add).then_inc(part_free, 1)

                turns(pool, body)




def _parts(value):
    out, rest = [], np.float32(value)
    for _ in range(3):
        bits = np.array([rest], np.float32).view(np.uint32)
        high = ((bits + 0x8000) & np.uint32(0xFFFF0000)).view(np.float32)[0]
        out.append(high)
        rest = np.float32(rest - high)
    assert rest == 0
    return out


def _constants():
    c = np.zeros((P, C_END), np.float32)
    rows = np.arange(P)
    c[:, C_ID:C_ID + P] = np.eye(P)
    c[:, C_SUM:C_SUM + P] = (rows[:, None] % DH == rows[None, :] % DH) * float(DH) ** -0.5
    c[:, C_BAND:C_BAND + P] = np.where(rows[None, :] >= rows[:, None] + P - WIN, 0, NEG)
    c[:, C_BAND + P:C_BAND + 2 * P] = np.where(rows[None, :] <= rows[:, None], 0, NEG)
    c[:, C_IOTA:C_IOTA + 64] = np.arange(64)
    c[:, C_TRI:C_TRI + 64] = rows[:, None] < np.arange(64)[None, :]
    c[:, C_ONES:C_ONES + 128] = 1.0
    c[:, C_START] = KC * rows
    c[:, C_EXTS] = c[:, C_EXTT] = 0.0
    for n, m in enumerate(_parts(MASKED)):
        for half in range(2):
            r = ROWS * half + ROW_MASK + n
            c[r, C_EXTS], c[r, C_EXTT] = m, -m
            c[r + 3, C_EXTT] = 1.0
    c[1:3, C_BA], c[2, C_BB], c[4, C_ROW4] = -1.0, -1.0, 1.0
    for half in range(2):
        for n, part in enumerate(K_PARTS):
            c[ROWS * half + DK * n:ROWS * half + DK * n + DK, C_KA] = -float(part > 0)
            c[ROWS * half + DK * n:ROWS * half + DK * n + DK, C_KB] = -float(part > 1)
    c[:, C_EIOTA:C_EIOTA + NE] = np.arange(NE)
    pos = np.arange(S, dtype=np.float32) / np.float32(32.0)
    inv = (1.0 / np.float32(150000.0) ** (np.arange(0, DH, 2, dtype=np.float32) / np.float32(DH))).astype(np.float32)
    freq = (pos[:, None] * inv[None, :]).astype(np.float32)
    sin, cos = np.sin(freq).T, np.cos(freq).T
    cs = np.zeros((P, S), np.float32)
    cs[0:DH:2], cs[1:DH:2] = cos, cos
    cs[DH::2], cs[DH + 1::2] = -sin, sin
    valid = (np.arange(NC * KC) < SK).astype(np.float32)[:, None]
    return c, cs, valid


_OUT = ("out_0_dram", (1, S, D), "float32")


def kernel(x, ctx_1024, mask_Bx1xS2_ik0, g_xattn, g_ffn, L0_xattn_Wq, L0_xattn_bq, L0_xattn_Wk, L0_xattn_bk,
           L0_xattn_Wv, L0_xattn_bv, L0_xattn_Wo, L0_xattn_bo, L0_ffn_attn_norm_w, L0_ffn_ffn_norm_w, L0_ffn_qkv_w,
           L0_ffn_qkv_b, L0_ffn_proj_w, L0_ffn_proj_b, L0_ffn_attn_sink, L0_ffn_gate_w, L0_ffn_gate_b, L0_ffn_W_up,
           L0_ffn_W_down):
    import concourse.bacc as bacc
    from concourse.bass_utils import run_bass_kernel_spmd

    consts, cs, valid = _constants()
    rows = np.array([(NP * half + pair) * DK + d for half in range(2) for d in range(DK) for pair in range(NP)])
    cols = np.array([[DH * f + c for c in range(DH)] + [DH * f + (c ^ 1) for c in range(DH)] for f in range(HF + KV)])
    qkv_w, qkv_b = np.asarray(L0_ffn_qkv_w), np.asarray(L0_ffn_qkv_b)
    ctx_t = np.zeros((D, NC * KC), np.float32)
    ctx_t[:, :SK] = np.asarray(ctx_1024)[0].T
    mask = np.zeros((NC * KC,), np.int32)
    mask[:SK] = np.asarray(mask_Bx1xS2_ik0)[0, 0]
    wk, bk = np.asarray(L0_xattn_Wk), np.asarray(L0_xattn_bk)
    wk_rows, bk_rows = np.zeros((D, NP, P), np.float32), np.zeros((5, NP, P), np.float32)
    for half in range(2):
        for n in range(len(K_PARTS)):
            for pair in range(NP):
                r, h = ROWS * half + DK * n, (NP * half + pair) * DK
                wk_rows[:, pair, r:r + DK] = wk[h:h + DK].T
                bk_rows[0:3, pair, r:r + DK] = bk[h:h + DK]
        r = slice(ROWS * half + ROW_MASK, ROWS * half + ROWS)
        bk_rows[3, :, r], bk_rows[4, :, r] = consts[r, C_EXTS], consts[r, C_EXTT]
    arrays = {
        "x": x, "ctxT": ctx_t, "mask": mask, "valid": valid, "consts": consts, "cs": cs,
        "g_xattn": g_xattn, "g_ffn": g_ffn,
        "WqT": np.asarray(L0_xattn_Wq)[rows].T, "bq": np.asarray(L0_xattn_bq)[rows][:, None],
        "wk": wk_rows, "bkx": bk_rows,
        "WvT": np.asarray(L0_xattn_Wv).T, "bv": L0_xattn_bv, "WoT": np.asarray(L0_xattn_Wo).T, "bo": L0_xattn_bo,
        "attn_norm_w": L0_ffn_attn_norm_w, "ffn_norm_w": L0_ffn_ffn_norm_w,
        "wqk": qkv_w[:, cols], "bqk": qkv_b[cols].T, "wvv": qkv_w[:, (HF + KV) * DH:], "bvv": qkv_b[(HF + KV) * DH:],
        "proj_w": L0_ffn_proj_w, "proj_b": L0_ffn_proj_b, "sink": L0_ffn_attn_sink,
        "gate_w": L0_ffn_gate_w, "gate_b": L0_ffn_gate_b, "W_up": L0_ffn_W_up, "W_down": L0_ffn_W_down,
    }
    arrays = {f"in_{n}": np.ascontiguousarray(v) for n, v in arrays.items()}
    nc = bacc.Bacc("TRN2", target_bir_lowering=False, num_devices=1)
    args = {n[3:]: nc.dram_tensor(n, v.shape, mybir.dt.from_np(v.dtype), kind="ExternalInput").ap()
            for n, v in arrays.items()}
    name, shape, dtype = _OUT
    out = nc.dram_tensor(name, shape, mybir.dt.from_np(np.dtype(dtype)), kind="ExternalOutput").ap()
    build(nc, args, out)
    r = run_bass_kernel_spmd(nc, [arrays], core_ids=[0])
    return r.results[0][name]
```

```python
from contextlib import ExitStack

import numpy as np

import concourse.bass as bass
from concourse import mybir

F32 = mybir.dt.float32
F32R = mybir.dt.float32r
BF16 = mybir.dt.bfloat16
I32 = mybir.dt.int32
U32 = mybir.dt.uint32
ALU = mybir.AluOpType
ACT = mybir.ActivationFunctionType
X = mybir.AxisListType.X

P = 128
S = 1024
D = 128
NT = S // P
SK = 6404
KC = 126
NC = -(-SK // KC)
TURNS, PAIRS = 6, 5
NCE = TURNS * PAIRS * 2
assert NCE >= NC
H = 16
DK = D // H
ROWS = 64
NP = H * ROWS // P
Q_PARTS = [0, 0, 1, 1, 0, 2]
K_PARTS = [0, 1, 0, 1, 2, 0]
EXT = ROWS - DK * len(Q_PARTS)
ROW_MASK = DK * len(Q_PARTS)
ROW_MAX = ROW_MASK + 3
QB = 256
NB = S // QB
QT = QB // P
NG = H // 4
HF = 16
KV = 4
DH = 64
NE = 32
FF = 128
TOPK = 4
EB = 4
WIN = 128
EPS = 1e-5
MASKED = 1e9
NEG = -1e30

C_ID, C_SUM, C_BAND, C_IOTA, C_TRI, C_ONES, C_START, C_EXTS, C_EXTT = 0, 128, 256, 512, 576, 640, 768, 769, 770
C_EIOTA, C_KA, C_KB, C_BA, C_BB, C_ROW4, C_END = 771, 803, 804, 805, 806, 807, 808


def head_of(g, j):
    return divmod(4 * g + j, NP)


def each_chunk(eng, m, body):

    def pairs(first):
        with eng.Fori(0, PAIRS) as pair:
            c = pair * 2 + first
            with eng.If(c < m):
                body(c, 0)
                with eng.If(c + 1 < m):
                    body(c + 1, 1)

    pairs(0)
    with eng.If(m > 2 * PAIRS):
        with eng.Fori(1, TURNS) as turn:
            with eng.If(turn * (2 * PAIRS) < m):
                pairs(turn * (2 * PAIRS))


class Chain:

    def __init__(self, engine, sem):
        self.engine, self.sem, self.count = engine, sem, 0

    def __call__(self, instruction):
        self.count += 1
        instruction.then_inc(self.sem, 1)
        self.engine.wait_ge(self.sem, self.count)


def build(nc, a, out):
    with ExitStack() as root:
        def sb(name, shape, dt=F32, ctx=root):
            return ctx.enter_context(nc.sbuf_tensor(name, shape, dt))

        def sem(name):
            return root.enter_context(nc.semaphore(name))

        ps = root.enter_context(nc.psum_tensor("ps", [P, 8, 512], F32))
        const = sb("const", [P, C_END])
        ident = const[:, C_ID:C_ID + P]
        x0 = sb("x0", [P, NT, D])
        x1 = sb("x1", [P, NT, D])
        stats = sb("stats", [P, NT, 6])
        mv = sb("mv", [P, NT, 2])
        st = sb("st", [P, 8, NT])
        gates = sb("gates", [P, 2])
        tanhs = sb("tanhs", [P, 2])
        k_dram = nc.dram_tensor("k_scratch", [NCE + 1, P, NP, KC], BF16).ap()
        v_dram = nc.dram_tensor("v_scratch", [NCE + 1, KC, H * (DK + 1)], F32).ap()
        c_dram = nc.dram_tensor("expert_weight_scratch", [NE, S], F32).ap()
        q_dram = nc.dram_tensor("q_scratch", [P, NP, S], BF16).ap()

        norm_w = sb("norm_w", [P, D])
        bqk = sb("bqk", [P, HF + KV])
        wvv = sb("wvv", [P, KV * DH])
        bvv = sb("bvv", [P, KV * DH])
        cs = sb("cs", [P, S])
        sinks = sb("sinks", [P, HF])
        wp = sb("wp", [P, HF * DH // P, D])
        bp = sb("bp", [P, D])
        norm2 = sb("norm2", [P, D])
        wg = sb("wg", [P, NE])
        bg = sb("bg", [P, NE])
        w_raw = sb("w_raw", [P, EB, 2 * FF + D])
        zeros = sb("zeros", [P, 512], BF16)
        band = sb("band", [P, 2, 2, 2, P], BF16)
        identb = sb("identb", [P, P], BF16)
        neg_sinks = sb("neg_sinks", [P, HF])
        in5, cs_in, sink_in, in7 = (sem(n) for n in ("in5", "cs_in", "sink_in", "in7"))
        expert_in = [sem(f"expert_in{n}") for n in range(EB)]

        def load_expert(eng, e, s):
            up = a["W_up"][bass.ds(e, 1)].rearrange("e p n -> (e p) n")
            down = a["W_down"][bass.ds(e, 1)].rearrange("e p n -> (e p) n")
            eng.dma_start(w_raw[:, s, 0:2 * FF], up).then_inc(expert_in[s], 16)
            eng.dma_start(w_raw[:, s, 2 * FF:2 * FF + D], down).then_inc(expert_in[s], 16)

        def moments(own, src, tiles):
            for t in tiles:
                last = nc.vector.bn_stats(stats[:, t, :], src[:, t, :])
            own(last)
            for t in tiles:
                last = nc.vector.bn_aggr(mv[:, t, :], stats[:, t, :])
            own(last)

        def layer_norm(own, root_is_ready, var_is_ready, src, dst):
            moments(own, src, range(NT))
            nc.vector.tensor_scalar(st[:, 2, :], mv[:, :, 1], EPS, None, ALU.add).then_inc(var_is_ready, 1)
            nc.vector.wait_ge(*root_is_ready)
            own(nc.vector.reciprocal(st[:, 4, :], st[:, 3, :]))
            for t in range(NT):
                last = nc.vector.tensor_scalar(dst[:, t, :], src[:, t, :], mv[:, t, 0:1], st[:, 4, t:t + 1],
                                               ALU.subtract, ALU.mult)
            own(last)

        def rms_scale(own, root_is_ready, src, dst, weight, done):
            nc.vector.wait_ge(*root_is_ready)
            own(nc.vector.reciprocal(st[:, 5, :], st[:, 3, :]))
            for t in range(NT):
                last = nc.vector.scalar_tensor_tensor(dst[:, t, :], src[:, t, :], st[:, 5, t:t + 1], weight[:, :],
                                                      ALU.mult, ALU.mult)
                if t % 4 == 3:
                    last.then_inc(done, 1)

        with ExitStack() as cross:
            q_all = sb("q_all", [P, 2, NP, S], BF16, cross)
            chunk_list = sb("chunk_list", [1, NCE + 2], I32, cross)
            oacc = sb("oacc", [P, NB, NG, QB], F32, cross)
            wo = sb("wo", [P, D], F32, cross)
            bo = sb("bo", [P, D], F32, cross)

            wk = sb("wk", [P, NP, P], F32, cross)
            bk_in = sb("bk_in", [5, NP, P], F32, cross)
            bk = sb("bk", [P, NP, P], BF16, cross)
            rows_m = sb("rows_m", [P, 2, KC], BF16, cross)
            wv = sb("wv", [P, D], F32, cross)
            bv = sb("bv", [P, D], F32, cross)
            ctx_in = sb("ctx_in", [P, 2, KC], F32, cross)
            mask_b = sb("mask_b", [P, 2, KC], I32, cross)
            valid = sb("valid", [KC, 2, 1], F32, cross)
            k_out = sb("k_out", [P, 2, NP * KC], BF16, cross)
            vv = sb("vv", [KC, 2, H, DK + 1], F32, cross)
            k_first = sb("k_first", [P, NP, KC], BF16, cross)
            qp = sb("qp", [P, 3, S], BF16, cross)
            qext = sb("qext", [EXT, S], BF16, cross)
            w_in, bk_in_ready, bk_ready, q_zero, q_written, q_loaded = (
                sem(n) for n in ("wkv_in", "bk_in_ready", "bk_ready", "q_zero", "q_written", "q_loaded"))
            chunk_in = [sem(f"chunk_in{n}") for n in range(2)]
            valid_in = [sem(f"valid_in{n}") for n in range(2)]
            kv_written = [sem(f"kv_written{n}") for n in range(2)]
            k_first_in = sem("k_first_in")

            def load_chunk(eng, c, s):
                off = eng.value_load(chunk_list[0:1, bass.ds(c, 1)], min_val=0, max_val=(NC - 1) * KC)
                eng.dma_start(ctx_in[:, s, :], a["ctxT"][:, bass.ds(off, KC)]).then_inc(chunk_in[s], 16)
                eng.dma_start(mask_b[:, s, :], a["mask"][bass.ds(off, KC)].partition_broadcast(P)
                              ).then_inc(chunk_in[s], 16)
                return off

            def load_valid(eng, off, s):
                eng.dma_start(valid[:, s, :], a["valid"][bass.ds(off, KC), :]).then_inc(valid_in[s], 16)

            with ExitStack() as ph:
                xn = sb("xn", [P, NT, D], F32, ph)
                xT = sb("xT", [P, S], F32, ph)
                qf = sb("qf", [P, S], F32, ph)
                qr = sb("qr", [P, S], F32, ph)
                wq = sb("wq", [P, D], F32, ph)
                bq = sb("bq", [P, 1], F32, ph)
                mask_c = sb("mask_c", [NC, KC], I32, ph)
                mask_f = sb("mask_f", [NC, KC], F32, ph)
                fl = sb("fl", [NC, 4], F32, ph)
                onehot = sb("onehot", [NC, NC], F32, ph)
                consts_in, x_in, wq_in, mask_in, late_in = (sem(n) for n in
                                                             ("consts_in", "x_in", "wq_in", "mask_in", "late_in"))
                dve_own1, var_ready1, root_ready1, xn_ready, flag_ready, pos_ready = (
                    sem(n) for n in ("dve_own1", "var_ready1", "root_ready1", "xn_ready", "flag_ready", "pos_ready"))
                xt_in_psum, xt_ready, q_in_psum, q_parts_ready, tanh_ready, list_ready, q_ready = (
                    sem(n) for n in ("xt_in_psum", "xt_ready", "q_in_psum", "q_parts_ready", "tanh_ready",
                                     "list_ready", "q_ready"))
                q_high, q_mid, bk_step, ext_ready = (sem(n) for n in ("q_high", "q_mid", "bk_step", "ext_ready"))
                bk_high = sb("bk_high", [5, NP, P], BF16, ph)
                bk_sub = sb("bk_sub", [5, NP, P], F32, ph)
                block = ph.enter_context(nc.Block())

                @block.gpsimd
                def _(pool):
                    nc.gpsimd.memset(qext[:, :], 0.0)
                    nc.gpsimd.memset(bk[:, :, :].rearrange("p n r -> p (n r)").bitcast(F32), 0.0)
                    nc.gpsimd.memset(rows_m[:, :, :], 0.0).then_inc(ext_ready, 1)
                    pool.wait_ge(ext_ready, 1)
                    nc.gpsimd.memset(qext[0:3, :], 1.0).then_inc(ext_ready, 1)
                    for n, col in enumerate((C_BA, C_BB)):
                        pool.wait_ge(bk_step, 3 * n + 1)
                        nc.gpsimd.tensor_scalar(bk_sub[:, :, :], bk_high[:, :, :], const[0:5, col:col + 1], None,
                                                ALU.mult).then_inc(bk_step, 1)
                        pool.wait_ge(bk_step, 3 * n + 2)
                        nc.gpsimd.tensor_tensor((bk_in, bk)[n][0:5, :, :], bk_in[:, :, :], bk_sub[:, :, :], ALU.add
                                                ).then_inc((bk_step, bk_ready)[n], 1)
                    nc.gpsimd.memset(q_all[:, :, :, :].rearrange("p h n s -> p (h n s)").bitcast(F32), 0.0
                                     ).then_inc(q_zero, 1)

                @block.sync
                def _(sp):
                    sp.dma_start(x0[:, :, :], a["x"].rearrange("b (t p) d -> p (b t) d", p=P)).then_inc(x_in, 16)
                    sp.dma_start(mask_c[:, :], a["mask"].rearrange("(c k) -> c k", k=KC)).then_inc(mask_in, 16)
                    sp.dma_start(const[:, :], a["consts"]).then_inc(consts_in, 16)
                    sp.dma_start(wq[:, :], a["WqT"]).then_inc(wq_in, 16)
                    sp.dma_start(bq[:, :], a["bq"]).then_inc(wq_in, 16)
                    sp.dma_start(bk_in[:, :, :], a["bkx"]).then_inc(bk_in_ready, 16)
                    sp.dma_start(wk[:, :, :], a["wk"]).then_inc(w_in, 16)
                    sp.dma_start(wv[:, :], a["WvT"]).then_inc(w_in, 16)
                    sp.dma_start(bv[:, :], a["bv"].partition_broadcast(P)).then_inc(w_in, 16)
                    sp.dma_start(gates[:, 0:1], a["g_xattn"].partition_broadcast(P)).then_inc(late_in, 16)
                    sp.dma_start(gates[:, 1:2], a["g_ffn"].partition_broadcast(P)).then_inc(late_in, 16)
                    sp.dma_start(wo[:, :], a["WoT"]).then_inc(late_in, 16)
                    sp.dma_start(bo[:, :], a["bo"].partition_broadcast(P)).then_inc(late_in, 16)
                    sp.wait_ge(list_ready, 1)
                    for s in range(2):
                        load_valid(sp, load_chunk(sp, s, s), s)
                    sp.wait_ge(q_parts_ready, 2)
                    sp.wait_ge(ext_ready, 2)
                    for half in range(2):
                        for n, part in enumerate(Q_PARTS):
                            r = ROWS * half + DK * n
                            sp.dma_start(q_dram[r:r + DK].rearrange("d p s -> (d p) s"),
                                         qp[64 * half:64 * half + 64, part, :]).then_inc(q_written, 16)
                        r = ROWS * half + ROW_MASK
                        sp.dma_start(q_dram[r:r + EXT, :, :],
                                     qext[:, :].unsqueeze(1).broadcast_to([EXT, NP, S])).then_inc(q_written, 16)

                @block.vector
                def _(dve):
                    own = Chain(dve, dve_own1)
                    dve.wait_ge(x_in, 16)
                    layer_norm(own, (root_ready1, 1), var_ready1, x0, xn)
                    nc.vector.engine_nop().then_inc(xn_ready, 1)
                    dve.wait_ge(mask_in, 16)
                    dve.wait_ge(consts_in, 16)
                    own(nc.vector.tensor_scalar(mask_f[:, :], mask_c[:, :], 0.0, None, ALU.not_equal))
                    own(nc.vector.tensor_reduce(fl[:, 0:1], mask_f[:, :], X, ALU.max))
                    nc.vector.engine_nop().then_inc(flag_ready, 1)
                    dve.wait_ge(pos_ready, 1)
                    own(nc.vector.tensor_scalar(fl[:, 1:2], ps[0:NC, 0, 0:1], 0.0, None, ALU.is_equal))
                    own(nc.vector.tensor_tensor(fl[:, 2:3], fl[:, 0:1], fl[:, 1:2], ALU.max))
                    nc.vector.engine_nop().then_inc(flag_ready, 1)
                    dve.wait_ge(pos_ready, 2)
                    own(nc.vector.tensor_copy(fl[:, 3:4], ps[0:NC, 1, 0:1]))
                    own(nc.vector.tensor_scalar(onehot[:, :], const[0:NC, C_IOTA:C_IOTA + NC],
                                                fl[:, 3:4], fl[:, 2:3], ALU.is_equal, ALU.mult))
                    nc.vector.engine_nop().then_inc(flag_ready, 1)
                    dve.wait_ge(pos_ready, 3)
                    own(nc.vector.memset(chunk_list[:, :], 0))
                    own(nc.vector.tensor_copy(chunk_list[0:1, 0:NC], ps[0:1, 2, 0:NC]))
                    own(nc.vector.tensor_copy(chunk_list[0:1, NCE:NCE + 1], ps[0:1, 3, 0:1]))
                    own(nc.vector.tensor_scalar(chunk_list[0:1, NCE + 1:NCE + 2], ps[0:1, 3, 0:1], -1.0, None,
                                                ALU.add))
                    nc.vector.engine_nop().then_inc(list_ready, 1)
                    for n in range(2):
                        dve.wait_ge(xt_in_psum, n + 1)
                        last = nc.vector.tensor_copy(xT[:, 512 * n:512 * n + 512], ps[:, 4 + n, :])
                        last.then_inc(xt_ready, 1)
                    for n in range(2):
                        dve.wait_ge(q_in_psum, n + 1)
                        own(nc.vector.tensor_scalar(qf[:, 512 * n:512 * n + 512], ps[:, 6 + n, :], bq[:, 0:1],
                                                    float(DK) ** -0.5, ALU.add, ALU.mult))
                        nc.vector.engine_nop().then_inc(q_ready, 1)
                    for n in range(2):
                        r = slice(512 * n, 512 * n + 512)
                        dve.wait_ge(q_high, n + 1)
                        nc.vector.tensor_tensor(qr[:, r], qf[:, r], qp[:, 0, r], ALU.subtract).then_inc(q_ready, 1)
                    for n in range(2):
                        r = slice(512 * n, 512 * n + 512)
                        dve.wait_ge(q_mid, n + 1)
                        nc.vector.tensor_tensor(qp[:, 2, r], qr[:, r], qp[:, 1, r], ALU.subtract
                                                ).then_inc(q_parts_ready, 1)

                @block.scalar
                def _(act):
                    act.wait_ge(var_ready1, 1)
                    nc.scalar.activation(st[:, 3, :], st[:, 2, :], ACT.Sqrt).then_inc(root_ready1, 1)
                    act.wait_ge(bk_in_ready, 16)
                    act.wait_ge(consts_in, 16)
                    nc.scalar.copy(bk_high[:, :, :], bk_in[:, :, :]).then_inc(bk_step, 1)
                    act.wait_ge(bk_step, 3)
                    nc.scalar.copy(bk_high[:, :, :], bk_in[:, :, :]).then_inc(bk_step, 1)
                    for n in range(2):
                        act.wait_ge(q_ready, n + 1)
                        nc.scalar.copy(qp[:, 0, 512 * n:512 * n + 512], qf[:, 512 * n:512 * n + 512]
                                       ).then_inc(q_high, 1)
                    for n in range(2):
                        act.wait_ge(q_ready, n + 3)
                        nc.scalar.copy(qp[:, 1, 512 * n:512 * n + 512], qr[:, 512 * n:512 * n + 512]
                                       ).then_inc(q_mid, 1)
                    act.wait_ge(late_in, 64)
                    nc.scalar.activation(tanhs[:, :], gates[:, :], ACT.Tanh).then_inc(tanh_ready, 1)
                    act.wait_ge(tanh_ready, 1)

                @block.tensor
                def _(pe):
                    one = const[0:NC, C_ONES:C_ONES + NC]
                    pe.wait_ge(flag_ready, 1)
                    nc.tensor.matmul(ps[0:NC, 0, 0:1], one, fl[:, 0:1], start=True, stop=True).then_inc(pos_ready, 1)
                    pe.wait_ge(flag_ready, 2)
                    nc.tensor.matmul(ps[0:NC, 1, 0:1], const[0:NC, C_TRI:C_TRI + NC], fl[:, 2:3],
                                     start=True, stop=True).then_inc(pos_ready, 1)
                    pe.wait_ge(flag_ready, 3)
                    nc.tensor.matmul(ps[0:1, 2, 0:NC], const[0:NC, C_START:C_START + 1], onehot[:, :],
                                     start=True, stop=True)
                    nc.tensor.matmul(ps[0:1, 3, 0:1], fl[:, 2:3], const[0:NC, C_ONES:C_ONES + 1],
                                     start=True, stop=True).then_inc(pos_ready, 1)
                    pe.wait_ge(xn_ready, 1)
                    for t in range(NT):
                        last = nc.tensor.transpose(ps[:, 4 + t // 4, P * (t % 4):P * (t % 4) + P], xn[:, t, :], ident)
                        if t % 4 == 3:
                            last.then_inc(xt_in_psum, 1)
                    pe.wait_ge(wq_in, 32)
                    for n in range(2):
                        pe.wait_ge(xt_ready, n + 1)
                        nc.tensor.matmul(ps[:, 6 + n, :], wq[:, :], xT[:, 512 * n:512 * n + 512],
                                         start=True, stop=True).then_inc(q_in_psum, 1)

            with ExitStack() as ph:
                ctx_m = sb("ctx_m", [P, 2, KC], F32, ph)
                unmasked = sb("unmasked", [P, 2, KC], F32, ph)
                k_high = sb("k_high", [P, 2, NP * KC], BF16, ph)
                k_rest = sb("k_rest", [P, 2, NP * KC], F32, ph)
                k_mid = sb("k_mid", [P, 2, NP * KC], BF16, ph)
                pool_passed = sem("pool_passed")
                sp_passed2, act_passed = sem("sp_passed2"), sem("act_passed")
                unmasked_ready = sem("unmasked_ready")
                masked, k_in_psum, v_in_psum, high_ready, rest_ready, mid_ready, k_ready, v_ready = (
                    sem(n) for n in ("masked", "k_in_psum", "v_in_psum", "high_ready", "rest_ready", "mid_ready",
                                     "k_ready", "v_ready"))
                block = ph.enter_context(nc.Block())

                def kbanks(s):
                    return ps[:, 2 * s:2 * s + 2, 0:4 * KC]

                def flat(t, s):
                    return t[:, s, :].rearrange("p (b n) -> p b n", b=2)

                @block.sync
                def _(sp):
                    n = sp.value_load(chunk_list[0:1, NCE:NCE + 1], min_val=1, max_val=NC)
                    for s in range(2):
                        sp.sem_inc(kv_written[s], 16)

                    def body(c, s):
                        sp.wait_ge(v_ready, c + 3)
                        sp.sem_inc(sp_passed2, 1)
                        off = sp.value_load(chunk_list[0:1, bass.ds(c + 2, 1)], min_val=0, max_val=(NC - 1) * KC)
                        load_valid(sp, off, s)
                        sp.wait_ge(k_ready, c + 3)
                        sp.sem_inc(sp_passed2, 1)
                        sp.dma_start(k_dram[bass.ds(c, 1)].rearrange("c r p k -> (c r) (p k)"), k_out[:, s, :]
                                     ).then_inc(kv_written[s], 16)
                        sp.dma_start(v_dram[bass.ds(c, 1)].rearrange("c k n -> (c k) n"),
                                     vv[:, s, :, :].rearrange("k h d -> k (h d)")).then_inc(kv_written[s], 16)

                    sp.wait_ge(q_written, 2 * (len(Q_PARTS) + 1) * 16)
                    sp.wait_ge(q_zero, 1)
                    for half in range(2):
                        r = slice(ROWS * half, ROWS * half + ROWS)
                        sp.dma_start(q_all[r, half, :, :], q_dram[r]).then_inc(q_loaded, 16)
                    each_chunk(sp, n, body)
                    sp.wait_ge(kv_written[0], 48)
                    sp.dma_start(k_first[:, :, :], k_dram[0]).then_inc(k_first_in, 16)
                    sp.wait_ge(q_loaded, 32)

                @block.tensor
                def _(pe):
                    n = pe.value_load(chunk_list[0:1, NCE:NCE + 1], min_val=1, max_val=NC)
                    pe.wait_ge(w_in, 48)
                    pe.wait_ge(bk_ready, 1)

                    def body(c, s):
                        pe.wait_ge(chunk_in[s], (c - s) * 16 + 32)
                        pe.wait_ge(v_ready, c + 1)
                        nc.tensor.matmul(ps[0:KC, 4 + s, 0:D], ctx_in[:, s, :], wv[:, :],
                                         start=True, stop=True).then_inc(v_in_psum, 1)
                        pe.wait_ge(masked, c + 1)
                        pe.wait_ge(rest_ready, c * 2 + 2)
                        for p in range(NP):
                            bank = ps[:, 2 * s + p // 4, KC * (p % 4):KC * (p % 4) + KC]
                            nc.tensor.matmul(bank, wk[:, p, :], ctx_m[:, s, :], start=True, stop=False)
                            last = nc.tensor.matmul(bank, bk[:, p, :], rows_m[:, s, :], start=False, stop=True)
                        last.then_inc(k_in_psum, 1)

                    each_chunk(pe, n, body)

                @block.scalar
                def _(act):
                    n = act.value_load(chunk_list[0:1, NCE:NCE + 1], min_val=1, max_val=NC)

                    def body(c, s):
                        act.wait_ge(k_in_psum, c + 1)
                        act.sem_inc(act_passed, 1)
                        act.wait_ge(rest_ready, c * 2 + 2)
                        nc.scalar.copy(flat(k_high, s), kbanks(s)).then_inc(high_ready, 1)
                        load_chunk(act, c + 2, s)
                        act.wait_ge(k_ready, c + 1)
                        for b in range(2):
                            act.wait_ge(rest_ready, c * 2 + (b + 5))
                            nc.scalar.copy(flat(k_mid, s)[:, b, :], flat(k_rest, s)[:, b, :]).then_inc(mid_ready, 1)

                    each_chunk(act, n, body)

                @block.gpsimd
                def _(pool):
                    n = pool.value_load(chunk_list[0:1, NCE:NCE + 1], min_val=1, max_val=NC)
                    pool.wait_ge(w_in, 48)

                    def body(c, s):
                        pool.wait_ge(chunk_in[s], (c - s) * 16 + 32)
                        pool.sem_inc(pool_passed, 1)
                        pool.wait_ge(rest_ready, c * 2 + 2)
                        pool.sem_inc(pool_passed, 1)
                        nc.gpsimd.tensor_scalar(unmasked[:, s, :], mask_b[:, s, :], 0.0, 0.0, ALU.is_equal,
                                                ALU.is_equal).then_inc(unmasked_ready, 1)
                        pool.wait_ge(unmasked_ready, c + 1)
                        nc.gpsimd.tensor_tensor(ctx_m[:, s, :], ctx_in[:, s, :], unmasked[:, s, :], ALU.mult)
                        nc.gpsimd.tensor_scalar(rows_m[0:5, s, :], unmasked[0:5, s, :], const[0:5, C_ROW4:C_ROW4 + 1],
                                                None, ALU.max).then_inc(masked, 1)

                    each_chunk(pool, n, body)

                @block.vector
                def _(dve):
                    n = dve.value_load(chunk_list[0:1, NCE:NCE + 1], min_val=1, max_val=NC)
                    for z, start in ((rest_ready, 4), (k_ready, 2), (v_ready, 2)):
                        dve.sem_inc(z, start)
                    dve.wait_ge(w_in, 48)

                    def body(c, s):
                        dve.wait_ge(high_ready, c + 1)
                        dve.wait_ge(k_ready, c + 2)
                        for b in range(2):
                            nc.vector.scalar_tensor_tensor(flat(k_rest, s)[:, b, :], flat(k_high, s)[:, b, :],
                                                           const[:, C_KA:C_KA + 1], kbanks(s)[:, b, :],
                                                           ALU.mult, ALU.add).then_inc(rest_ready, 1)
                        dve.wait_ge(v_in_psum, c + 1)
                        dve.wait_ge(valid_in[s], (c - s) * 8 + 16)
                        dve.wait_ge(kv_written[s], (c - s) * 16 + 16)
                        nc.vector.scalar_tensor_tensor(vv[:, s, :, 0:DK],
                                                       bv[0:KC, :].rearrange("k (h d) -> k h d", d=DK),
                                                       valid[:, s, :],
                                                       ps[0:KC, 4 + s, 0:D].rearrange("k (h d) -> k h d", d=DK),
                                                       ALU.mult, ALU.add)
                        nc.vector.tensor_copy(vv[:, s, :, DK:DK + 1],
                                              valid[:, s, :].unsqueeze(1).broadcast_to([KC, H, 1])
                                              ).then_inc(v_ready, 1)
                        for b in range(2):
                            dve.wait_ge(mid_ready, c * 2 + (b + 1))
                            last = nc.vector.scalar_tensor_tensor(flat(k_out, s)[:, b, :], flat(k_mid, s)[:, b, :],
                                                                  const[:, C_KB:C_KB + 1], flat(k_rest, s)[:, b, :],
                                                                  ALU.mult, ALU.add)
                        last.then_inc(k_ready, 1)

                    each_chunk(dve, n, body)

            with ExitStack() as ph:
                k_last = sb("k_last", [P, NP, KC], BF16, ph)
                v_last = sb("v_last", [KC, H, DK + 1], F32, ph)
                k_one = sb("k_one", [P, 2, NP, KC], BF16, ph)
                k_two = sb("k_two", [P, 2, NP, KC], BF16, ph)
                v_two = sb("v_two", [KC, 2, H, DK + 1], F32, ph)
                probs = sb("probs", [KC, 2, 4, QB], F32, ph)
                mx = sb("mx", [P, 2, H, QT], F32, ph)
                run_max = sb("run_max", [P, QT, H], F32, ph)
                neg_f = sb("neg_f", [H, QB], F32, ph)
                neg_r = sb("neg_r", [H, QB], F32, ph)
                neg_p = sb("neg_p", [H, 3, QB], BF16, ph)
                dve_own3, zeros_ready, ends_in, sp_passed = (sem(n) for n in ("dve_own3", "zeros_ready", "ends_in",
                                                                             "sp_passed"))
                max_t, max_rows_ready = sem("max_t"), sem("max_rows_ready")
                max_rows_in = [sem(f"max_rows_in{half}") for half in range(2)]
                oacc_saved, prepared = sem("oacc_saved"), sem("prepared")
                stage_sems = []
                for s in range(NB + 1):
                    names = ["k_one_in0", "k_one_in1", "kv_two_in0", "kv_two_in1", "s1_ready", "s1_free", "mx_ready",
                             "s2_ready", "s2_free", "p_free"]
                    stage_sems.append({n: nc.alloc_semaphore(name=f"{n}_st{s}") for n in names})
                S1, S2, AC = 0, 4, 6
                S1_START, P_START = 6, 6
                block = ph.enter_context(nc.Block())

                def store_maxima(eng, stage, half):
                    for j in range(3):
                        r = ROWS * half + ROW_MAX + j
                        eng.dma_start(q_all[r:r + 1, half, :, QB * stage:QB * stage + QB],
                                      neg_p[NP * half:NP * half + NP, j, :]).then_inc(max_rows_in[half], 16)

                def s2_banks(stage):
                    return 2 if stage < NB else 4

                def s2_bank(stage, i):
                    return S2 + i % 2 if stage < NB else i % 4


                @block.sync
                def _(sp):
                    n = sp.value_load(chunk_list[0:1, NCE:NCE + 1], min_val=1, max_val=NC)
                    m = sp.value_load(chunk_list[0:1, NCE + 1:NCE + 2], min_val=0, max_val=NC - 1)

                    def load_k(dst, c, z):
                        sp.dma_start(dst, k_dram[bass.ds(c, 1)].rearrange("c r p k -> (c r) p k")).then_inc(z, 16)

                    def load_v(dst, c, z):
                        sp.dma_start(dst, v_dram[bass.ds(c, 1)].rearrange("c k n -> (c k) n")).then_inc(z, 16)

                    for z, each, first in ((kv_written, 32, 16), (chunk_in, 32, 32), (valid_in, 16, 16)):
                        sp.wait_ge(z[0], (n + 1) // 2 * each + first)
                        sp.sem_inc(sp_passed, 1)
                        sp.wait_ge(z[1], n // 2 * each + first)
                        sp.sem_inc(sp_passed, 1)
                    load_k(k_last[:, :, :], m, ends_in)
                    load_v(v_last[:, :, :].rearrange("k h d -> k (h d)"), m, ends_in)
                    for stage in range(NB + 1):
                        z = stage_sems[stage]
                        one, two = stage < NB, stage > 0

                        def body(c, s):
                            if one:
                                sp.wait_ge(z["s1_free"], c * 4 + S1_START)
                                sp.sem_inc(sp_passed, 1)
                                load_k(k_one[:, s, :, :], c + 1, z[f"k_one_in{s}"])
                            if two:
                                sp.wait_ge(z["p_free"], c * 4 + P_START - 4)
                                sp.sem_inc(sp_passed, 1)
                                load_k(k_two[:, s, :, :], c, z[f"kv_two_in{s}"])
                                load_v(v_two[:, s, :, :].rearrange("k h d -> k (h d)"), c, z[f"kv_two_in{s}"])

                        each_chunk(sp, m, body)
                        if one:
                            sp.wait_ge(max_rows_ready, stage + 1)
                            store_maxima(sp, stage, 0)
                    for s in range(EB):
                        load_expert(sp, s, s)
                    sp.wait_ge(max_rows_in[0], NB * 48)

                @block.gpsimd
                def _(pool):
                    pool.wait_ge(ends_in, 32)
                    pool.dma_start(norm_w[:, :], a["attn_norm_w"].partition_broadcast(P)).then_inc(in5, 16)
                    for dst, src in ((bqk[:, :], a["bqk"]), (wvv[:, :], a["wvv"]),
                                     (bvv[:, :], a["bvv"].partition_broadcast(P)), (cs[:, :], a["cs"])):
                        pool.dma_start(dst, src).then_inc(cs_in, 16)
                    pool.dma_start(sinks[:, :], a["sink"].partition_broadcast(P)).then_inc(sink_in, 16)
                    for dst, src in ((wp[:, :, :], a["proj_w"]),
                                     (bp[:, :], a["proj_b"].partition_broadcast(P)),
                                     (norm2[:, :], a["ffn_norm_w"].partition_broadcast(P)),
                                     (wg[:, :], a["gate_w"]), (bg[:, :], a["gate_b"].partition_broadcast(P))):
                        pool.dma_start(dst, src).then_inc(in7, 16)
                    nc.gpsimd.tensor_copy(identb[:, :], ident)
                    for first in range(2):
                        for j in range(2):
                            nc.gpsimd.tensor_copy(band[:, first, j, :, :].rearrange("p k c -> p (k c)"),
                                                  const[:, C_BAND:C_BAND + 256]).then_inc(prepared, 1)
                    pool.wait_ge(prepared, 4)
                    for j in range(2):
                        nc.gpsimd.memset(band[:, 0, j, 0, :], NEG)
                    nc.gpsimd.tensor_scalar(bo[:, :], bo[:, :], tanhs[:, 0:1], None, ALU.mult).then_inc(prepared, 1)
                    pool.wait_ge(prepared, 5)
                    nc.gpsimd.tensor_tensor(x0[:, :, :], x0[:, :, :],
                                            bo[:, :].unsqueeze(1).broadcast_to([P, NT, D]), ALU.add)
                    pool.wait_ge(sink_in, 16)
                    nc.gpsimd.tensor_scalar(neg_sinks[:, :], sinks[:, :], -1.0, None, ALU.mult).then_inc(prepared, 1)
                    for stage in range(NB):
                        pool.wait_ge(max_rows_ready, stage + 1)
                        store_maxima(pool, stage, 1)
                    pool.wait_ge(max_rows_in[1], NB * 48)
                    pool.wait_ge(prepared, 6)

                @block.tensor
                def _(pe):
                    n = pe.value_load(chunk_list[0:1, NCE:NCE + 1], min_val=1, max_val=NC)
                    m = pe.value_load(chunk_list[0:1, NCE + 1:NCE + 2], min_val=0, max_val=NC - 1)
                    pe.wait_ge(zeros_ready, 1)
                    pe.wait_ge(k_first_in, 16)
                    for stage in range(NB + 1):
                        z = stage_sems[stage]
                        one, two = stage < NB, stage > 0
                        q2 = QB * (stage - 1)

                        def scores_one(c, k_tile, g, stage=stage, heads=range(4)):
                            z, q1 = stage_sems[stage], QB * stage
                            if 0 in heads:
                                pe.wait_ge(z["s1_free"], c * 4 + (g + S1_START - 1))
                            for j in heads:
                                half, pair = head_of(g, j)
                                for qt in range(QT):
                                    q, col = q1 + P * qt, KC * (2 * (j % 2) + qt)
                                    last = nc.tensor.matmul(ps[:, S1 + 2 * (g % 2) + j // 2, col:col + KC],
                                                            q_all[:, half, pair, q:q + P], k_tile(pair),
                                                            start=True, stop=True)
                            if 3 in heads:
                                last.then_inc(z["s1_ready"], 1)

                        def scores_two(c, k_tile, g, banks=range(2)):
                            for b in banks:
                                pe.wait_ge(z["s2_free"], c * 8 + (2 * g + b + 1))
                                for j in range(2):
                                    half, pair = head_of(g, 2 * b + j)
                                    bank = s2_bank(stage, 2 * g + b)
                                    last = nc.tensor.matmul(ps[0:KC, bank, QB * j:QB * j + QB], k_tile(pair),
                                                            q_all[:, half, pair, q2:q2 + QB], start=True, stop=True)
                                last.then_inc(z["s2_ready"], 1)

                        def values(c, v_tile, g):
                            pe.wait_ge(z["s2_free"], c * 8 + (2 * g + 2 + s2_banks(stage)))
                            for j in range(4):
                                last = nc.tensor.matmul(
                                    ps[32 * j:32 * j + DK + 1, AC + g // 2, QB * (g % 2):QB * (g % 2) + QB],
                                    v_tile(4 * g + j), probs[:, g % 2, j, :], start=False, stop=True,
                                    skip_group_check=True, tile_position=(0, 32 * j))
                            last.then_inc(z["p_free"], 1)

                        def first(pair):
                            return k_first[:, pair, :]

                        def last_k(pair):
                            return k_last[:, pair, :]

                        if stage == 0:
                            for g in range(NG):
                                scores_one(0, first, g)
                        if two:
                            if stage > 1:
                                pe.wait_ge(oacc_saved, stage - 1)
                            for b in range(2):
                                nc.tensor.matmul(ps[:, AC + b, :], zeros[:, 0:P], zeros[:, :], start=True, stop=True)
                            for half in range(2):
                                pe.wait_ge(max_rows_in[half], 48 * stage)

                        def body(c, s):
                            def k1(pair):
                                return k_one[:, s, pair, :]

                            def k2(pair):
                                return k_two[:, s, pair, :]

                            def v2(head):
                                return v_two[:, s, head, :]

                            if two:
                                pe.wait_ge(z[f"kv_two_in{s}"], (c - s) * 16 + 32)
                            for g in range(NG):
                                if one and g == 1:
                                    scores_one(c + 1, k1, g, heads=(0, 1))
                                if two:
                                    scores_two(c, k2, g, range(1 if g == 1 and one else 2))
                                    if g > 1 or g and not one:
                                        values(c, v2, g - 1)
                                if one:
                                    if g == 0:
                                        pe.wait_ge(z[f"k_one_in{s}"], (c - s) * 8 + 16)
                                    scores_one(c + 1, k1, g, heads=(2, 3) if g == 1 else range(4))
                                if two and one and g == 1:
                                    scores_two(c, k2, g, (1,))
                                    values(c, v2, g - 1)
                            if two:
                                values(c, v2, NG - 1)

                        each_chunk(pe, m, body)
                        if one:
                            pe.wait_ge(z["mx_ready"], n + 1)
                            for qt in range(QT):
                                last = nc.tensor.transpose(ps[0:H, S1, P * qt:P * qt + P], run_max[:, qt, :], ident)
                            last.then_inc(max_t, 1)
                        if stage == 1:
                            pe.wait_ge(ends_in, 32)
                        for g in range(NG + 1):
                            if two and g < NG:
                                scores_two(m, last_k, g)
                            if two and g:
                                values(m, lambda head: v_last[:, head, :], g - 1)
                            if stage + 1 < NB and g < NG:
                                scores_one(0, first, g, stage + 1)

                @block.scalar
                def _(act):
                    n = act.value_load(chunk_list[0:1, NCE:NCE + 1], min_val=1, max_val=NC)
                    m = act.value_load(chunk_list[0:1, NCE + 1:NCE + 2], min_val=0, max_val=NC - 1)
                    act.sem_inc(stage_sems[1]["s2_free"], s2_banks(1))
                    act.sem_inc(stage_sems[1]["p_free"], P_START)
                    for stage in range(1, NB + 1):
                        z = stage_sems[stage]

                        def body(c, s):
                            for g in range(NG):
                                act.wait_ge(z["p_free"], c * 4 + (g + P_START - 1))
                                for b in range(2):
                                    act.wait_ge(z["s2_ready"], c * 8 + (2 * g + b + 1))
                                    nc.scalar.activation(
                                        probs[:, g % 2, 2 * b:2 * b + 2, :].rearrange("k h q -> k (h q)"),
                                        ps[0:KC, s2_bank(stage, 2 * g + b), :], ACT.Exp).then_inc(z["s2_free"], 1)

                        each_chunk(act, m, body)
                        if stage < NB:
                            act.wait_ge(z["p_free"], m * 4 + P_START)
                            act.sem_inc(stage_sems[stage + 1]["p_free"], P_START)
                        body(m, 0)
                        act.wait_ge(z["p_free"], n * 4 + P_START)
                        if stage < NB:
                            act.sem_inc(stage_sems[stage + 1]["s2_free"], s2_banks(stage + 1))
                        nc.scalar.copy(oacc[:, stage - 1, :, :].rearrange("p (b g) q -> p b (g q)", b=2),
                                       ps[:, AC:AC + 2, :]).then_inc(oacc_saved, 1)

                @block.vector
                def _(dve):
                    own = Chain(dve, dve_own3)
                    n = dve.value_load(chunk_list[0:1, NCE:NCE + 1], min_val=1, max_val=NC)
                    m = dve.value_load(chunk_list[0:1, NCE + 1:NCE + 2], min_val=0, max_val=NC - 1)
                    nc.vector.memset(zeros[:, :], 0.0).then_inc(zeros_ready, 1)

                    def open_stage(stage):
                        own(nc.vector.memset(run_max[:, :, :], -3.0e38))
                        dve.sem_inc(stage_sems[stage]["mx_ready"], 1)
                        dve.sem_inc(stage_sems[stage]["s1_free"], S1_START)

                    open_stage(0)
                    for stage in range(NB):
                        z = stage_sems[stage]

                        def reduce(c, s):
                            for g in range(NG):
                                dve.wait_ge(z["s1_ready"], c * 4 + (g + 1))
                                b = S1 + 2 * (g % 2)
                                nc.vector.tensor_reduce(
                                    mx[:, s, 4 * g:4 * g + 4, :].rearrange("p h t -> p (h t)"),
                                    ps[:, b:b + 2, 0:4 * KC].rearrange("p b (n k) -> p b n k", k=KC),
                                    X, ALU.max).then_inc(z["s1_free"], 1)
                            dve.wait_ge(z["s1_free"], c * 4 + (4 + S1_START))
                            dve.wait_ge(z["mx_ready"], c + 1)
                            nc.vector.tensor_tensor(run_max[:, :, :], run_max[:, :, :],
                                                    mx[:, s, :, :].rearrange("p h t -> p t h"), ALU.max
                                                    ).then_inc(z["mx_ready"], 1)

                        reduce(0, 1)
                        each_chunk(dve, m, lambda c, s: reduce(c + 1, s))
                        dve.wait_ge(max_t, stage + 1)
                        if stage:
                            for half in range(2):
                                dve.wait_ge(max_rows_in[half], 48 * stage)
                        own(nc.vector.tensor_scalar(neg_f[:, :], ps[0:H, S1, 0:QB], -1.0, None, ALU.mult))
                        if stage + 1 < NB:
                            open_stage(stage + 1)
                        own(nc.vector.tensor_copy(neg_p[:, 0, :], neg_f[:, :]))
                        own(nc.vector.tensor_tensor(neg_r[:, :], neg_f[:, :], neg_p[:, 0, :], ALU.subtract))
                        own(nc.vector.tensor_copy(neg_p[:, 1, :], neg_r[:, :]))
                        nc.vector.tensor_tensor(neg_p[:, 2, :], neg_r[:, :], neg_p[:, 1, :], ALU.subtract
                                                ).then_inc(max_rows_ready, 1)

            nc.clear_and_free_semaphores([z for stage in stage_sems for z in stage.values()])
            nc.all_engine_barrier()

            with ExitStack() as ph:
                attn = sb("attn", [P, NT, D], F32, ph)
                attn_t = sb("attn_t", [P, S], F32, ph)
                recip = sb("recip", [P, 2, H], F32, ph)
                heads_t, heads_free, at_in_psum, at_ready, y_in_psum, rec_ready = (
                    sem(n) for n in ("heads_t", "heads_free", "at_in_psum", "at_ready",
                                     "y_in_psum", "rec_ready"))
                dve_own4 = sem("dve_own4")
                block = ph.enter_context(nc.Block())

                @block.tensor
                def _(pe):
                    for t in range(NT):
                        if t >= 2:
                            pe.wait_ge(heads_free, t - 1)
                        for g in range(NG):
                            last = nc.tensor.transpose(ps[:, t % 2, P * g:P * g + P],
                                                       oacc[:, t // QT, g, P * (t % QT):P * (t % QT) + P], ident)
                        last.then_inc(heads_t, 1)
                        if t:
                            pe.wait_ge(heads_free, t)
                            nc.tensor.transpose(ps[:, 2 + (t - 1) // 4, P * ((t - 1) % 4):P * ((t - 1) % 4) + P],
                                                attn[:, t - 1, :], ident).then_inc(at_in_psum, 1)
                    pe.wait_ge(heads_free, NT)
                    nc.tensor.transpose(ps[:, 3, 3 * P:4 * P], attn[:, NT - 1, :], ident).then_inc(at_in_psum, 1)
                    for n in range(2):
                        pe.wait_ge(at_ready, n + 1)
                        for t in range(4):
                            last = nc.tensor.matmul(ps[:, 4 + n, P * t:P * t + P],
                                                    attn_t[:, P * (4 * n + t):P * (4 * n + t) + P], wo[:, :],
                                                    start=True, stop=True)
                        last.then_inc(y_in_psum, 1)

                @block.vector
                def _(dve):
                    own = Chain(dve, dve_own4)
                    for t in range(NT):
                        dve.wait_ge(heads_t, t + 1)
                        v = ps[:, t % 2, :].rearrange("p (h c) -> p h c", c=32)
                        nc.vector.reciprocal(recip[:, t % 2, :], v[:, :, DK]).then_inc(rec_ready, 1)
                        dve.wait_ge(rec_ready, t + 1)
                        nc.vector.tensor_tensor(attn[:, t, :].rearrange("p (h d) -> p h d", d=DK), v[:, :, 0:DK],
                                                recip[:, t % 2, :].unsqueeze(2).broadcast_to([P, H, DK]),
                                                ALU.mult).then_inc(heads_free, 1)
                    for n in range(2):
                        dve.wait_ge(at_in_psum, 4 * n + 4)
                        nc.vector.tensor_copy(attn_t[:, 512 * n:512 * n + 512], ps[:, 2 + n, :]).then_inc(at_ready, 1)
                    for n in range(2):
                        r = slice(4 * n, 4 * n + 4)
                        dve.wait_ge(y_in_psum, n + 1)
                        own(nc.vector.scalar_tensor_tensor(
                            x1[:, r, :].rearrange("p t d -> p (t d)"), ps[:, 4 + n, :], tanhs[:, 0:1],
                            x0[:, r, :].rearrange("p t d -> p (t d)"), ALU.mult, ALU.add))

        x2 = sb("x2", [P, NT, D])
        hT = sb("hT", [P, S])
        x3 = sb("x3", [P, NT, D])
        comb = sb("comb", [P, NT, NE])
        with ExitStack() as win:
            y_t = sb("y_t", [P, HF // 2, S], F32, win)
            with ExitStack() as att:
                q_rot = sb("q_rot", [P, HF, S], F32, att)
                k_rot = sb("k_rot", [P, KV, S], F32, att)
                v_tok = sb("v_tok", [P, NT, KV * DH], F32, att)

                with ExitStack() as ph:
                    h = sb("h", [P, NT, D], F32, ph)
                    k_cs = sb("k_cs", [P, 2, S], F32, ph)
                    wqk = y_t[:, :, :].rearrange("p t n -> p (t n)")[:, 0:(HF + KV) * P].rearrange(
                        "p (f n) -> p f n", n=P)
                    wqk_low = sb("wqk_low", [P, HF + KV, P], F32R, ph)
                    wqk_high = sb("wqk_high", [P, HF + KV, P], F32R, ph)
                    ht_high = sb("ht_high", [P, S], F32R, ph)
                    ht_low = sb("ht_low", [P, S], F32R, ph)
                    WB = 5
                    wqk_in, wqk_high_ready, wqk_ready, ht_high_ready, ht_low_ready = (
                        sem(n) for n in ("wqk_in", "wqk_high_ready", "wqk_ready", "ht_high_ready", "ht_low_ready"))
                    dve_own5, var5, root5, h_ready, ht_psum, ht_ready = (
                        sem(n) for n in ("dve_own5", "var5", "root5", "h_ready", "ht_psum", "ht_ready"))
                    v_psum, v_free, qk_psum, qk_free, ks_psum, ks_free = (
                        sem(n) for n in ("v_psum", "v_free", "qk_psum", "qk_free", "ks_psum", "ks_free"))
                    block = ph.enter_context(nc.Block())

                    @block.sync
                    def _(sp):
                        sp.dma_start(wqk, a["wqk"]).then_inc(wqk_in, 16)

                    @block.gpsimd
                    def _(pool):
                        pool.wait_ge(wqk_in, 16)
                        for b in range((HF + KV) // WB):
                            f = slice(WB * (3 - b), WB * (3 - b) + WB)
                            nc.gpsimd.tensor_copy(wqk_high[:, f, :], wqk[:, f, :]).then_inc(wqk_high_ready, 1)
                            pool.wait_ge(wqk_high_ready, b + 1)
                            nc.gpsimd.tensor_tensor(wqk_low[:, f, :], wqk[:, f, :], wqk_high[:, f, :].bitcast(F32),
                                                    ALU.subtract).then_inc(wqk_ready, 1)
                        pool.wait_ge(wqk_ready, (HF + KV) // WB)

                    @block.scalar
                    def _(act):
                        for n in range(2):
                            act.wait_ge(var5, n + 1)
                            nc.scalar.activation(st[:, 3, :], st[:, 2, :], ACT.Sqrt).then_inc(root5, 1)
                        for n in range(2):
                            act.wait_ge(ht_psum, n + 1)
                            nc.scalar.copy(ht_high[:, 512 * n:512 * n + 512], ps[:, n, :]).then_inc(ht_high_ready, 1)
                            nc.scalar.copy(hT[:, 512 * n:512 * n + 512], ps[:, n, :]).then_inc(ht_ready, 1)
                        for kv in range(KV):
                            for n in range(2):
                                act.wait_ge(ks_psum, 2 * kv + n + 1)
                                nc.scalar.copy(k_rot[:, kv, 512 * n:512 * n + 512], ps[:, n, :]).then_inc(ks_free, 1)

                    @block.vector
                    def _(dve):
                        own = Chain(dve, dve_own5)
                        layer_norm(own, (root5, 1), var5, x1, x2)
                        own(nc.vector.tensor_tensor(st[:, 6, :], st[:, 4, :], st[:, 4, :], ALU.mult))
                        own(nc.vector.tensor_tensor(st[:, 6, :], st[:, 6, :], mv[:, :, 1], ALU.mult))
                        nc.vector.tensor_scalar(st[:, 2, :], st[:, 6, :], EPS, None, ALU.add).then_inc(var5, 1)
                        dve.wait_ge(in5, 16)
                        rms_scale(own, (root5, 2), x2, h, norm_w, h_ready)
                        for n in range(2):
                            r = slice(512 * n, 512 * n + 512)
                            dve.wait_ge(ht_high_ready, n + 1)
                            dve.wait_ge(ht_ready, n + 1)
                            nc.vector.tensor_tensor(ht_low[:, r], hT[:, r], ht_high[:, r].bitcast(F32),
                                                    ALU.subtract).then_inc(ht_low_ready, 1)
                        dve.wait_ge(cs_in, 64)
                        for m in range(NT // 2):
                            dve.wait_ge(v_psum, m + 1)
                            nc.vector.tensor_tensor(v_tok[:, 2 * m:2 * m + 2, :],
                                                    ps[:, 2 + m % 2, :].rearrange("p (t d) -> p t d", t=2),
                                                    bvv[:, :].unsqueeze(1).broadcast_to([P, 2, KV * DH]), ALU.add
                                                    ).then_inc(v_free, 1)
                        for m in range(HF + KV):
                            f = HF + m if m < KV else m - KV
                            dst = k_cs[:, m % 2, :] if m < KV else q_rot[:, f, :]
                            for n in range(2):
                                u = 2 * m + n
                                dve.wait_ge(qk_psum, u + 1)
                                if 2 <= m < KV:
                                    dve.wait_ge(ks_psum, 2 * (m - 2) + n + 1)
                                nc.vector.scalar_tensor_tensor(dst[:, 512 * n:512 * n + 512], ps[:, 4 + u % 4, :],
                                                               bqk[:, f:f + 1], cs[:, 512 * n:512 * n + 512],
                                                               ALU.add, ALU.mult).then_inc(qk_free, 1)

                    @block.tensor
                    def _(pe):
                        for t in range(NT):
                            pe.wait_ge(h_ready, t // 4 + 1)
                            last = nc.tensor.transpose(ps[:, t // 4, P * (t % 4):P * (t % 4) + P], h[:, t, :], ident)
                            if t % 4 == 3:
                                last.then_inc(ht_psum, 1)
                        pe.wait_ge(cs_in, 64)
                        pe.wait_ge(ht_ready, 2)
                        for m in range(NT // 2):
                            if m >= 2:
                                pe.wait_ge(v_free, m - 1)
                            for t in (2 * m, 2 * m + 1):
                                last = nc.tensor.matmul(ps[:, 2 + m % 2, 256 * (t % 2):256 * (t % 2) + 256],
                                                        hT[:, P * t:P * t + P], wvv[:, :], start=True, stop=True)
                            last.then_inc(v_psum, 1)
                        for m in range(HF + KV):
                            f = HF + m if m < KV else m - KV
                            for n in range(2):
                                u = 2 * m + n
                                if u >= 4:
                                    pe.wait_ge(qk_free, u - 3)
                                r = slice(512 * n, 512 * n + 512)
                                pe.wait_ge(ht_low_ready, 2)
                                pe.wait_ge(wqk_ready, 4 - f // WB)
                                bank = ps[:, 4 + u % 4, :]
                                nc.tensor.matmul(bank, wqk_high[:, f, :], ht_high[:, r], start=True, stop=False)
                                nc.tensor.matmul(bank, wqk_low[:, f, :], ht_high[:, r], start=False, stop=False)
                                nc.tensor.matmul(bank, wqk_high[:, f, :], ht_low[:, r], start=False, stop=True
                                                 ).then_inc(qk_psum, 1)
                            if 1 <= m < 1 + KV:
                                for n in range(2):
                                    u = 2 * (m - 1) + n
                                    pe.wait_ge(qk_free, u + 1)
                                    if u >= 2:
                                        pe.wait_ge(ks_free, u - 1)
                                    nc.tensor.matmul(ps[:, n, :], const[:, C_SUM:C_SUM + P],
                                                     k_cs[:, (m - 1) % 2, 512 * n:512 * n + 512],
                                                     start=True, stop=True
                                                     ).then_inc(ks_psum, 1)

                with ExitStack() as ph:
                    neg4 = sb("neg4", [P, 4], F32, ph)
                    neg_m = sb("neg_m", [P, NT, HF], F32, ph)
                    sums = sb("sums", [P, NT, HF], F32, ph)
                    recips = sb("recips", [P, 2, 4], F32, ph)
                    sink_w = sb("sink_w", [P, 2, 4], F32, ph)
                    pw = sb("pw", [P, 2, 4, 2 * P], F32, ph)
                    pn = sb("pn", [P, 2, 4, 2 * P], F32, ph)
                    pt = sb("pt", [P, 2, 4, 2, P], F32, ph)
                    dve_own6, s_ready, m_ready, p_ready, rec_ready6, norm_ready, t_ready, pt_ready, y_ready, y_saved = (
                        sem(n) for n in ("dve_own6", "s_ready", "m_ready", "p_ready", "rec_ready6", "norm_ready",
                                         "t_ready", "pt_ready", "y_ready", "y_saved"))
                    sink_arg, sink_exp = sem("sink_arg"), sem("sink_exp")
                    block = ph.enter_context(nc.Block())
                    UNITS = NT * KV
                    STEPS = UNITS + 3

                    @block.tensor
                    def _(pe):
                        for m in range(STEPS):
                            if m < UNITS:
                                t, g = divmod(m, KV)
                                if m >= 2:
                                    pe.wait_ge(p_ready, m - 1)
                                for b in range(2):
                                    bank = ps[:, 2 * (m % 2) + b, :]
                                    nc.tensor.matmul(bank, identb[:, :],
                                                     band[:, min(t, 1), :, :, :].rearrange("p h k c -> p (h k c)"),
                                                     start=True, stop=False)
                                    for j in range(2):
                                        head = 4 * g + 2 * b + j
                                        c0 = 256 * j + (0 if t else P)
                                        last = nc.tensor.matmul(ps[:, 2 * (m % 2) + b, c0:256 * j + 256],
                                                                q_rot[:, head, P * t:P * t + P],
                                                                k_rot[:, g, P * max(t - 1, 0):P * t + P],
                                                                start=False, stop=j == 1)
                                last.then_inc(s_ready, 1)
                            if 2 <= m < UNITS + 2:
                                k = m - 2
                                pe.wait_ge(norm_ready, k + 1)
                                if k:
                                    pe.wait_ge(pt_ready, k)
                                for j in range(4):
                                    for kt in range(2):
                                        c = 256 * (j % 2) + P * kt
                                        last = nc.tensor.transpose(ps[:, 4 + j // 2, c:c + P],
                                                                   pn[:, k % 2, j, P * kt:P * kt + P], ident)
                                last.then_inc(t_ready, 1)
                            if m >= 3:
                                k = m - 3
                                t, g = divmod(k, KV)
                                pe.wait_ge(pt_ready, k + 1)
                                if k >= 2:
                                    pe.wait_ge(y_saved, k - 1)
                                first = 0 if t else 1
                                for kt in range(first, 2):
                                    for half in range(2):
                                        last = nc.tensor.matmul(ps[DH * half:DH * half + DH, 6 + k % 2, 0:2 * P],
                                                                v_tok[:, t - 1 + kt, DH * g:DH * g + DH],
                                                                pt[:, k % 2, 2 * half:2 * half + 2, kt, :],
                                                                start=kt == first, stop=kt == 1,
                                                                skip_group_check=True, tile_position=(0, DH * half))
                                last.then_inc(y_ready, 1)

                    @block.scalar
                    def _(act):
                        for m in range(STEPS):
                            if m < UNITS:
                                t, g = divmod(m, KV)
                                act.wait_ge(m_ready, m + 1)
                                if m >= 2:
                                    act.wait_ge(norm_ready, m - 1)
                                for j in range(4):
                                    last = nc.scalar.activation(
                                        pw[:, m % 2, j, :],
                                        ps[:, 2 * (m % 2) + j // 2, 256 * (j % 2):256 * (j % 2) + 256],
                                        ACT.Exp, bias=neg_m[:, t, 4 * g + j:4 * g + j + 1],
                                        accum_out=sums[:, t, 4 * g + j:4 * g + j + 1])
                                last.then_inc(p_ready, 1)
                                act.wait_ge(sink_arg, m + 1)
                                nc.scalar.activation(sink_w[:, m % 2, :], sink_w[:, m % 2, :], ACT.Exp
                                                     ).then_inc(sink_exp, 1)
                            if m >= 3:
                                k = m - 3
                                t, g = divmod(k, KV)
                                act.wait_ge(y_ready, k + 1)
                                nc.scalar.copy(y_t[:, 2 * g:2 * g + 2, P * t:P * t + P],
                                               ps[:, 6 + k % 2, 0:2 * P].rearrange("p (b q) -> p b q", b=2)
                                               ).then_inc(y_saved, 1)

                    @block.gpsimd
                    def _(pool):
                        for m in range(UNITS):
                            pool.wait_ge(rec_ready6, m + 1)
                            if m >= 2:
                                pool.wait_ge(t_ready, m - 1)
                            nc.gpsimd.tensor_tensor(pn[:, m % 2, :, :], pw[:, m % 2, :, :],
                                                    recips[:, m % 2, :].unsqueeze(2).broadcast_to([P, 4, 2 * P]),
                                                    ALU.mult).then_inc(norm_ready, 1)

                    @block.vector
                    def _(dve):
                        own = Chain(dve, dve_own6)
                        for m in range(STEPS):
                            if m < UNITS:
                                t, g = divmod(m, KV)
                                r = slice(4 * g, 4 * g + 4)
                                dve.wait_ge(s_ready, m + 1)
                                banks = ps[:, 2 * (m % 2):2 * (m % 2) + 2, :]
                                own(nc.vector.tensor_reduce(neg4[:, :], banks.rearrange("p b (j c) -> p b j c", j=2),
                                                            X, ALU.max, negate=True))
                                nc.vector.tensor_tensor(neg_m[:, t, r], neg4[:, :], neg_sinks[:, r], ALU.min
                                                        ).then_inc(m_ready, 1)
                                dve.wait_ge(m_ready, m + 1)
                                nc.vector.tensor_tensor(sink_w[:, m % 2, :], sinks[:, r], neg_m[:, t, r], ALU.add
                                                        ).then_inc(sink_arg, 1)
                            if 1 <= m <= UNITS:
                                k = m - 1
                                t, g = divmod(k, KV)
                                r = slice(4 * g, 4 * g + 4)
                                dve.wait_ge(p_ready, k + 1)
                                dve.wait_ge(sink_exp, k + 1)
                                own(nc.vector.tensor_tensor(sums[:, t, r], sums[:, t, r], sink_w[:, k % 2, :], ALU.add))
                                if k >= 2:
                                    dve.wait_ge(norm_ready, k - 1)
                                nc.vector.reciprocal(recips[:, k % 2, :], sums[:, t, r]).then_inc(rec_ready6, 1)
                            if 2 <= m < UNITS + 2:
                                k = m - 2
                                dve.wait_ge(t_ready, k + 1)
                                if k >= 2:
                                    dve.wait_ge(y_ready, k - 1)
                                nc.vector.tensor_copy(pt[:, k % 2, :, :, :].rearrange("p j k c -> p (j k c)"),
                                                      ps[:, 4:6, :].rearrange("p b c -> p (b c)")).then_inc(pt_ready, 1)

            h_high = sb("h_high", [P, S], F32R, win)
            h_low = sb("h_low", [P, S], F32R, win)
            w_high = sb("w_high", [P, EB, 2 * FF + D], F32R, win)
            w_low = sb("w_low", [P, EB, 2 * FF + D], F32R, win)
            c_rows = sb("c_rows", [P, EB, S], F32, win)
            c_t = sb("c_t", [NE, S], F32, win)
            w_high_ready, w_low_ready, c_written = (sem(n) for n in ("w_high_ready", "w_low_ready", "c_written"))
            c_in = [sem(f"c_in{n}") for n in range(EB)]

            def load_c(eng, e, s):
                eng.dma_start(c_rows[:, s, :], c_dram[bass.ds(e, 1)].rearrange("e s -> (e s)").partition_broadcast(P)
                              ).then_inc(c_in[s], 16)

            g_ready, u_ready, gated = (sem(n) for n in ("g_ready", "u_ready", "gated"))
            G0, U0, A0 = 0, 2, 4

            def three(bank, w, a_h, a_l, s, start, signal):
                nc.tensor.matmul(bank, w_high[:, s, w], a_h, start=start, stop=False, skip_group_check=True)
                nc.tensor.matmul(bank, w_low[:, s, w], a_h, start=False, stop=False, skip_group_check=True)
                nc.tensor.matmul(bank, w_high[:, s, w], a_l, start=False, stop=True, skip_group_check=True
                                 ).then_inc(signal, 1)

            def up(k):
                s, n = k // 2 % EB, k % 2
                r = slice(512 * n, 512 * n + 512)
                three(ps[:, G0 + n, :], slice(FF, 2 * FF), h_high[:, r], h_low[:, r], s, True, g_ready)
                three(ps[:, U0 + n, :], slice(0, FF), h_high[:, r], h_low[:, r], s, True, u_ready)

            with ExitStack() as ph:
                h2 = sb("h2", [P, NT, D], F32, ph)
                gl = sb("gl", [P, NT, NE], F32, ph)
                top = sb("top", [P, NT, 8], F32, ph)
                topi = sb("topi", [P, NT, 8], U32, ph)
                topf = sb("topf", [P, NT, 8], F32, ph)
                ew = sb("ew", [P, NT, TOPK], F32, ph)
                esum = sb("esum", [P, 2, NT], F32, ph)
                picks = sb("picks", [P, NT, TOPK, NE], F32, ph)
                dve_own7, var7, root7, h2_ready, pr_psum, h2t_psum, h2t_ready, gl_psum = (
                    sem(n) for n in ("dve_own7", "var7", "root7", "h2_ready", "pr_psum",
                                     "h2t_psum", "h2t_ready", "gl_psum"))
                ew_arg, ew_exp = sem("ew_arg"), sem("ew_exp")
                h_high_ready, h_low_ready, comb_ready, ct_psum, ct_ready = (
                    sem(n) for n in ("h_high_ready", "h_low_ready", "comb_ready", "ct_psum", "ct_ready"))
                block = ph.enter_context(nc.Block())

                @block.sync
                def _(sp):
                    sp.wait_ge(ct_ready, 2)
                    sp.dma_start(c_dram, c_t[:, :]).then_inc(c_written, 16)

                @block.gpsimd
                def _(pool):
                    for s in range(2):
                        pool.wait_ge(w_high_ready, s + 1)
                        nc.gpsimd.tensor_tensor(w_low[:, s, :], w_raw[:, s, :], w_high[:, s, :].bitcast(F32),
                                                ALU.subtract).then_inc(w_low_ready, 1)
                    for n in range(2):
                        pool.wait_ge(h_high_ready, n + 1)
                        nc.gpsimd.tensor_tensor(h_low[:, 512 * n:512 * n + 512], hT[:, 512 * n:512 * n + 512],
                                                h_high[:, 512 * n:512 * n + 512].bitcast(F32), ALU.subtract
                                                ).then_inc(h_low_ready, 1)
                    pool.wait_ge(w_low_ready, 2)
                    pool.wait_ge(h_low_ready, 2)

                @block.tensor
                def _(pe):
                    pe.wait_ge(in7, 80)
                    for t in range(NT):
                        for f in range(HF // 2):
                            last = nc.tensor.matmul(ps[:, 4 + t // 4, P * (t % 4):P * (t % 4) + P],
                                                    y_t[:, f, P * t:P * t + P], wp[:, f, :],
                                                    start=f == 0, stop=f == HF // 2 - 1)
                        last.then_inc(pr_psum, 1)
                    for t in range(NT):
                        pe.wait_ge(h2_ready, t // 4 + 1)
                        last = nc.tensor.transpose(ps[:, t // 4, P * (t % 4):P * (t % 4) + P], h2[:, t, :], ident)
                        if t % 4 == 3:
                            last.then_inc(h2t_psum, 1)
                    for t in range(NT):
                        pe.wait_ge(h2t_ready, t // 4 + 1)
                        last = nc.tensor.matmul(ps[:, 6, NE * t:NE * t + NE], hT[:, P * t:P * t + P], wg[:, :],
                                                start=True, stop=True)
                    last.then_inc(gl_psum, 1)
                    pe.wait_ge(h_high_ready, 2)
                    pe.wait_ge(h_low_ready, 2)
                    pe.wait_ge(w_low_ready, 1)
                    up(0)
                    up(1)
                    pe.wait_ge(comb_ready, 1)
                    for t in range(NT):
                        last = nc.tensor.transpose(ps[0:NE, (5, 7)[t // 4], P * (t % 4):P * (t % 4) + P],
                                                   comb[:, t, :], ident)
                        if t % 4 == 3:
                            last.then_inc(ct_psum, 1)

                @block.scalar
                def _(act):
                    for s in range(2):
                        act.wait_ge(expert_in[s], 32)
                        nc.scalar.copy(w_high[:, s, :], w_raw[:, s, :]).then_inc(w_high_ready, 1)
                    act.wait_ge(var7, 1)
                    nc.scalar.activation(st[:, 3, :], st[:, 2, :], ACT.Sqrt).then_inc(root7, 1)
                    for n in range(2):
                        act.wait_ge(h2t_psum, n + 1)
                        nc.scalar.copy(hT[:, 512 * n:512 * n + 512], ps[:, n, :]).then_inc(h2t_ready, 1)
                        nc.scalar.copy(h_high[:, 512 * n:512 * n + 512], ps[:, n, :]).then_inc(h_high_ready, 1)
                    act.wait_ge(ew_arg, 1)
                    nc.scalar.activation(ew[:, :, :], ew[:, :, :], ACT.Exp).then_inc(ew_exp, 1)

                @block.vector
                def _(dve):
                    own = Chain(dve, dve_own7)
                    dve.wait_ge(in7, 80)
                    for n in range(2):
                        r = slice(4 * n, 4 * n + 4)
                        own(nc.vector.tensor_tensor(x3[:, r, :], x2[:, r, :],
                                                    bp[:, :].unsqueeze(1).broadcast_to([P, 4, D]), ALU.add))
                        dve.wait_ge(pr_psum, 4 * n + 4)
                        own(nc.vector.tensor_tensor(x3[:, r, :], ps[:, 4 + n, :].rearrange("p (t d) -> p t d", d=D),
                                                    x3[:, r, :], ALU.add))
                        moments(own, x3, range(4 * n, 4 * n + 4))
                    own(nc.vector.tensor_tensor(st[:, 6, :], mv[:, :, 0], mv[:, :, 0], ALU.mult))
                    own(nc.vector.tensor_tensor(st[:, 6, :], st[:, 6, :], mv[:, :, 1], ALU.add))
                    nc.vector.tensor_scalar(st[:, 2, :], st[:, 6, :], EPS, None, ALU.add).then_inc(var7, 1)
                    rms_scale(own, (root7, 1), x3, h2, norm2, h2_ready)
                    dve.wait_ge(gl_psum, 1)
                    own(nc.vector.tensor_tensor(gl[:, :, :], ps[:, 6, 0:NT * NE].rearrange("p (t e) -> p t e", e=NE),
                                                bg[:, :].unsqueeze(1).broadcast_to([P, NT, NE]), ALU.add))
                    for t in range(NT):
                        last = nc.vector.max(top[:, t, :], gl[:, t, :])
                    own(last)
                    for t in range(NT):
                        last = nc.vector.max_index(topi[:, t, :], top[:, t, :], gl[:, t, :])
                    own(last)
                    own(nc.vector.tensor_copy(topf[:, :, :], topi[:, :, :]))
                    nc.vector.tensor_tensor(ew[:, :, :], top[:, :, 0:TOPK], top[:, :, 0:1].broadcast_to([P, NT, TOPK]),
                                            ALU.subtract).then_inc(ew_arg, 1)
                    dve.wait_ge(ew_exp, 1)
                    own(nc.vector.tensor_reduce(esum[:, 0, :], ew[:, :, :], X, ALU.add))
                    own(nc.vector.reciprocal(esum[:, 1, :], esum[:, 0, :]))
                    own(nc.vector.tensor_tensor(ew[:, :, :], ew[:, :, :],
                                                esum[:, 1, :].unsqueeze(2).broadcast_to([P, NT, TOPK]), ALU.mult))
                    all_picks = [P, NT, TOPK, NE]
                    own(nc.vector.tensor_tensor(
                        picks[:, :, :, :],
                        const[:, C_EIOTA:C_EIOTA + NE].unsqueeze(1).unsqueeze(1).broadcast_to(all_picks),
                        topf[:, :, 0:TOPK].unsqueeze(3).broadcast_to(all_picks), ALU.is_equal))
                    own(nc.vector.tensor_tensor(picks[:, :, :, :], picks[:, :, :, :],
                                                ew[:, :, :].unsqueeze(3).broadcast_to(all_picks), ALU.mult))
                    own(nc.vector.tensor_reduce(comb[:, :, :], picks[:, :, :, :].rearrange("p t j e -> p t e j"),
                                                X, ALU.add))
                    nc.vector.engine_nop().then_inc(comb_ready, 1)
                    for n in range(2):
                        dve.wait_ge(ct_psum, n + 1)
                        nc.vector.tensor_copy(c_t[:, 512 * n:512 * n + 512], ps[0:NE, (5, 7)[n], :]
                                              ).then_inc(ct_ready, 1)

            with ExitStack() as ph:
                silu = sb("silu", [P, 2, 512], F32, ph)
                scaled = sb("scaled", [P, 2, 512], F32, ph)
                act_f = sb("act_f", [P, 2, 512], F32, ph)
                a_high = sb("a_high", [P, 2, 512], F32R, ph)
                a_low = sb("a_low", [P, 2, 512], F32R, ph)
                acc_t = sb("acc_t", [P, S], F32, ph)
                scaled_ready, d_done, low_ready8 = (sem(n) for n in ("scaled_ready", "d_done", "low_ready8"))
                silu_ready, high_ready8 = sem("silu_ready"), sem("high_ready8")
                acc_ready, acc_back, dve_own8, o_ready, o_out, sp_passed8, pool_passed8 = (
                    sem(n) for n in ("acc_ready", "acc_back", "dve_own8", "o_ready", "o_out", "sp_passed8",
                                     "pool_passed8"))
                block = ph.enter_context(nc.Block())
                UE = 2 * EB

                def turns(eng, body):
                    with eng.Fori(0, NE // EB - 1) as turn:
                        body(turn * EB, False)
                    body(NE - EB, True)

                def slots(last):
                    return EB - 2 if last else EB

                @block.sync
                def _(sp):
                    sp.wait_ge(c_written, 16)
                    for s in range(EB):
                        load_c(sp, s, s)

                    def body(e, last):
                        if not last:
                            for s in range(EB):
                                sp.wait_ge(w_low_ready, e + (s + 1))
                                sp.sem_inc(sp_passed8, 1)
                                load_expert(sp, e + EB + s, s)
                                sp.wait_ge(scaled_ready, 2 * e + (2 * s + 4))
                                sp.sem_inc(sp_passed8, 1)
                                load_c(sp, e + EB + s, s)

                    turns(sp, body)
                    sp.wait_ge(o_ready, 1)
                    sp.dma_start(out.rearrange("b (t p) d -> p (b t) d", p=P), x1[:, :, :]).then_inc(o_out, 16)
                    sp.wait_ge(o_out, 16)

                @block.tensor
                def _(pe):
                    def down(e, k):
                        s, n = k // 2, k % 2
                        pe.wait_ge(low_ready8, 2 * e + (k + 3))
                        three(ps[:, A0 + n, :], slice(2 * FF, 2 * FF + D), a_high[:, n, :], a_low[:, n, :], s,
                              False, d_done)

                    for n in range(2):
                        nc.tensor.matmul(ps[:, A0 + n, :], zeros[:, 0:P], zeros[:, :], start=True, stop=True)

                    def body(e, last):
                        for k in range(UE):
                            if not (last and k >= UE - 2):
                                if k % 2 == 0:
                                    pe.wait_ge(w_low_ready, e + (k // 2 + 2))
                                pe.wait_ge(gated, 2 * e + (k + 3))
                                up(k + 2)
                            down(e, k)

                    turns(pe, body)
                    for t in range(NT):
                        pe.wait_ge(acc_ready, 2)
                        last = nc.tensor.transpose(ps[:, G0 + t // 4, P * (t % 4):P * (t % 4) + P],
                                                   acc_t[:, P * t:P * t + P], ident)
                        if t % 4 == 3:
                            last.then_inc(acc_back, 1)

                @block.scalar
                def _(act):
                    def gate(e, k):
                        act.wait_ge(g_ready, 2 * e + (k + 1))
                        act.wait_ge(scaled_ready, 2 * e + (k + 1))
                        nc.scalar.activation(silu[:, k % 2, :], ps[:, G0 + k % 2, :], ACT.Silu).then_inc(silu_ready, 1)

                    gate(0, 0)

                    def body(e, last):
                        for k in range(UE):
                            if not (last and k == UE - 1):
                                gate(e, k + 1)
                            act.wait_ge(gated, 2 * e + (k + 3))
                            act.wait_ge(d_done, 2 * e + (k + 1))
                            nc.scalar.copy(a_high[:, k % 2, :], act_f[:, k % 2, :]).then_inc(high_ready8, 1)
                            if k % 2 == 0 and k // 2 < slots(last):
                                s = (k // 2 + 2) % EB
                                act.wait_ge(expert_in[s], 32 // EB * (e + (k // 2 + 2 - s)) + 32)
                                nc.scalar.copy(w_high[:, s, :], w_raw[:, s, :]).then_inc(w_high_ready, 1)

                    turns(act, body)
                    act.wait_ge(d_done, 2 * NE + 2)
                    nc.scalar.copy(acc_t[:, 0:512], ps[:, A0, :]).then_inc(acc_ready, 1)

                @block.gpsimd
                def _(pool):
                    def body(e, last):
                        for k in range(UE):
                            s, n = k // 2, k % 2
                            if n == 0:
                                pool.wait_ge(c_in[s], 16 // EB * e + 16)
                                pool.sem_inc(pool_passed8, 1)
                            pool.wait_ge(silu_ready, 2 * e + (k + 1))
                            pool.wait_ge(gated, 2 * e + (k + 1))
                            nc.gpsimd.tensor_tensor(scaled[:, n, :], silu[:, n, :], c_rows[:, s, 512 * n:512 * n + 512],
                                                    ALU.mult).then_inc(scaled_ready, 1)

                    turns(pool, body)

                @block.vector
                def _(dve):
                    own = Chain(dve, dve_own8)
                    for z in (scaled_ready, gated, d_done, low_ready8):
                        dve.sem_inc(z, 2)

                    def gate(e, k):
                        dve.wait_ge(low_ready8, 2 * e + (k + 1))
                        dve.wait_ge(u_ready, 2 * e + (k + 1))
                        dve.wait_ge(scaled_ready, 2 * e + (k + 3))
                        nc.vector.tensor_tensor(act_f[:, k % 2, :], scaled[:, k % 2, :], ps[:, U0 + k % 2, :], ALU.mult
                                                ).then_inc(gated, 1)

                    def body(e, last):
                        for k in range(UE):
                            gate(e, k)
                            if k % 2 == 1 and k // 2 < slots(last):
                                s = (k // 2 + 2) % EB
                                dve.wait_ge(w_high_ready, e + (k // 2 + 3))
                                nc.vector.tensor_tensor(w_low[:, s, :], w_raw[:, s, :], w_high[:, s, :].bitcast(F32),
                                                        ALU.subtract).then_inc(w_low_ready, 1)
                            dve.wait_ge(high_ready8, 2 * e + (k + 1))
                            nc.vector.tensor_tensor(a_low[:, k % 2, :], act_f[:, k % 2, :],
                                                    a_high[:, k % 2, :].bitcast(F32), ALU.subtract
                                                    ).then_inc(low_ready8, 1)

                    turns(dve, body)
                    dve.wait_ge(d_done, 2 * NE + 2)
                    nc.vector.tensor_copy(acc_t[:, 512:1024], ps[:, A0 + 1, :]).then_inc(acc_ready, 1)
                    for n in range(2):
                        r = slice(4 * n, 4 * n + 4)
                        dve.wait_ge(acc_back, n + 1)
                        own(nc.vector.tensor_tensor(x3[:, r, :], ps[:, G0 + n, :].rearrange("p (t d) -> p t d", d=D),
                                                    x3[:, r, :], ALU.add))
                        own(nc.vector.scalar_tensor_tensor(x1[:, r, :].rearrange("p t d -> p (t d)"),
                                                           x3[:, r, :].rearrange("p t d -> p (t d)"), tanhs[:, 1:2],
                                                           x1[:, r, :].rearrange("p t d -> p (t d)"),
                                                           ALU.mult, ALU.add))
                    nc.vector.engine_nop().then_inc(o_ready, 1)




def _parts(value):
    out, rest = [], np.float32(value)
    for _ in range(3):
        bits = np.array([rest], np.float32).view(np.uint32)
        high = ((bits + 0x8000) & np.uint32(0xFFFF0000)).view(np.float32)[0]
        out.append(high)
        rest = np.float32(rest - high)
    assert rest == 0
    return out


def _constants():
    c = np.zeros((P, C_END), np.float32)
    rows = np.arange(P)
    c[:, C_ID:C_ID + P] = np.eye(P)
    c[:, C_SUM:C_SUM + P] = (rows[:, None] % DH == rows[None, :] % DH) * float(DH) ** -0.5
    c[:, C_BAND:C_BAND + P] = np.where(rows[None, :] >= rows[:, None] + P - WIN, 0, NEG)
    c[:, C_BAND + P:C_BAND + 2 * P] = np.where(rows[None, :] <= rows[:, None], 0, NEG)
    c[:, C_IOTA:C_IOTA + 64] = np.arange(64)
    c[:, C_TRI:C_TRI + 64] = rows[:, None] < np.arange(64)[None, :]
    c[:, C_ONES:C_ONES + 128] = 1.0
    c[:, C_START] = KC * rows
    c[:, C_EXTS] = c[:, C_EXTT] = 0.0
    for n, m in enumerate(_parts(MASKED)):
        for half in range(2):
            r = ROWS * half + ROW_MASK + n
            c[r, C_EXTS], c[r, C_EXTT] = m, -m
            c[r + 3, C_EXTT] = 1.0
    c[1:3, C_BA], c[2, C_BB], c[4, C_ROW4] = -1.0, -1.0, 1.0
    for half in range(2):
        for n, part in enumerate(K_PARTS):
            c[ROWS * half + DK * n:ROWS * half + DK * n + DK, C_KA] = -float(part > 0)
            c[ROWS * half + DK * n:ROWS * half + DK * n + DK, C_KB] = -float(part > 1)
    c[:, C_EIOTA:C_EIOTA + NE] = np.arange(NE)
    pos = np.arange(S, dtype=np.float32) / np.float32(32.0)
    inv = (1.0 / np.float32(150000.0) ** (np.arange(0, DH, 2, dtype=np.float32) / np.float32(DH))).astype(np.float32)
    freq = (pos[:, None] * inv[None, :]).astype(np.float32)
    sin, cos = np.sin(freq).T, np.cos(freq).T
    cs = np.zeros((P, S), np.float32)
    cs[0:DH:2], cs[1:DH:2] = cos, cos
    cs[DH::2], cs[DH + 1::2] = -sin, sin
    valid = (np.arange(NC * KC) < SK).astype(np.float32)[:, None]
    return c, cs, valid


_OUT = ("out_0_dram", (1, S, D), "float32")


def kernel(x, ctx_1024, mask_Bx1xS2_ik0, g_xattn, g_ffn, L0_xattn_Wq, L0_xattn_bq, L0_xattn_Wk, L0_xattn_bk,
           L0_xattn_Wv, L0_xattn_bv, L0_xattn_Wo, L0_xattn_bo, L0_ffn_attn_norm_w, L0_ffn_ffn_norm_w, L0_ffn_qkv_w,
           L0_ffn_qkv_b, L0_ffn_proj_w, L0_ffn_proj_b, L0_ffn_attn_sink, L0_ffn_gate_w, L0_ffn_gate_b, L0_ffn_W_up,
           L0_ffn_W_down):
    import concourse.bacc as bacc
    from concourse.bass_utils import run_bass_kernel_spmd

    consts, cs, valid = _constants()
    rows = np.array([(NP * half + pair) * DK + d for half in range(2) for d in range(DK) for pair in range(NP)])
    cols = np.array([[DH * f + c for c in range(DH)] + [DH * f + (c ^ 1) for c in range(DH)] for f in range(HF + KV)])
    qkv_w, qkv_b = np.asarray(L0_ffn_qkv_w), np.asarray(L0_ffn_qkv_b)
    proj_w = np.asarray(L0_ffn_proj_w).reshape(KV, 2, 2, DH, D).transpose(1, 3, 0, 2, 4).reshape(P, HF // 2, D)
    ctx_t = np.zeros((D, NC * KC), np.float32)
    ctx_t[:, :SK] = np.asarray(ctx_1024)[0].T
    mask = np.zeros((NC * KC,), np.int32)
    mask[:SK] = np.asarray(mask_Bx1xS2_ik0)[0, 0]
    wk, bk = np.asarray(L0_xattn_Wk), np.asarray(L0_xattn_bk)
    wk_rows, bk_rows = np.zeros((D, NP, P), np.float32), np.zeros((5, NP, P), np.float32)
    for half in range(2):
        for n in range(len(K_PARTS)):
            for pair in range(NP):
                r, h = ROWS * half + DK * n, (NP * half + pair) * DK
                wk_rows[:, pair, r:r + DK] = wk[h:h + DK].T
                bk_rows[0:3, pair, r:r + DK] = bk[h:h + DK]
        r = slice(ROWS * half + ROW_MASK, ROWS * half + ROWS)
        bk_rows[3, :, r], bk_rows[4, :, r] = consts[r, C_EXTS], consts[r, C_EXTT]
    arrays = {
        "x": x, "ctxT": ctx_t, "mask": mask, "valid": valid, "consts": consts, "cs": cs,
        "g_xattn": g_xattn, "g_ffn": g_ffn,
        "WqT": np.asarray(L0_xattn_Wq)[rows].T, "bq": np.asarray(L0_xattn_bq)[rows][:, None],
        "wk": wk_rows, "bkx": bk_rows,
        "WvT": np.asarray(L0_xattn_Wv).T, "bv": L0_xattn_bv, "WoT": np.asarray(L0_xattn_Wo).T, "bo": L0_xattn_bo,
        "attn_norm_w": L0_ffn_attn_norm_w, "ffn_norm_w": L0_ffn_ffn_norm_w,
        "wqk": qkv_w[:, cols], "bqk": qkv_b[cols].T, "wvv": qkv_w[:, (HF + KV) * DH:], "bvv": qkv_b[(HF + KV) * DH:],
        "proj_w": proj_w, "proj_b": L0_ffn_proj_b, "sink": L0_ffn_attn_sink,
        "gate_w": L0_ffn_gate_w, "gate_b": L0_ffn_gate_b, "W_up": L0_ffn_W_up, "W_down": L0_ffn_W_down,
    }
    arrays = {f"in_{n}": np.ascontiguousarray(v) for n, v in arrays.items()}
    nc = bacc.Bacc("TRN2", target_bir_lowering=False, num_devices=1)
    args = {n[3:]: nc.dram_tensor(n, v.shape, mybir.dt.from_np(v.dtype), kind="ExternalInput").ap()
            for n, v in arrays.items()}
    name, shape, dtype = _OUT
    out = nc.dram_tensor(name, shape, mybir.dt.from_np(np.dtype(dtype)), kind="ExternalOutput").ap()
    build(nc, args, out)
    r = run_bass_kernel_spmd(nc, [arrays], core_ids=[0])
    return r.results[0][name]
```
